# Optimizing a Trainium2 kernel written in Bass

```python
import numpy as np
import jax
import jax.numpy as jnp

def _softmax(x, axis=-1):
    return jax.nn.softmax(x, axis=axis)

def _gelu(x):
    return jax.nn.gelu(x, approximate=True)

def _silu(x):
    return jax.nn.silu(x)

def _sigmoid(x):
    return jax.nn.sigmoid(x)

def _layernorm(x, axis=-1, eps=1e-05):
    m = jnp.mean(x, axis=axis, keepdims=True)
    v = jnp.var(x, axis=axis, keepdims=True)
    return (x - m) / jnp.sqrt(v + eps)

def _scatter_add(tgt, idx, src, axis=0):
    return tgt.at[idx].add(src)

def _segment_sum(src, seg, n):
    return jax.ops.segment_sum(src, seg, n)
kernel_name = 'mk_xattn_ffn_d2_seqx_r4_b32a1e'

def setup_inputs(seed: int=0):
    np.random.seed(seed)
    _w = jnp.asarray

    def _rec_inputs():
        import jax
        import jax.numpy as jnp
        _rk = jax.random.key(seed)
        x = -0.0002928 + 1 * jax.random.normal(jax.random.fold_in(_rk, 1), (32, 128, 256), jnp.float32)
        _lenS = 128 - jax.random.randint(jax.random.fold_in(_rk, 7), (32,), 0, max(1, 128 // 4) + 1, jnp.int32)
        _lenS2 = 128 - jax.random.randint(jax.random.fold_in(_rk, 8), (32,), 0, max(1, 128 // 4) + 1, jnp.int32)
        _ctx_1024P = jax.random.normal(jax.random.fold_in(_rk, 11), (32, 16, 256), jnp.float32)
        _ctx_1024c = jax.random.dirichlet(jax.random.fold_in(_rk, 511), 0.3 * jnp.ones((16,), jnp.float32), (32, 128))
        _ctx_1024t = jnp.einsum('bsk,bkd->bsd', _ctx_1024c, _ctx_1024P)
        _ctx_1024t = _ctx_1024t * jax.lax.rsqrt(jnp.mean(jnp.square(_ctx_1024t)) + 1e-12) * 0.953939
        ctx_1024 = -1.39393e-06 + 0.999914 * (_ctx_1024t + 0.3 * jax.random.normal(jax.random.fold_in(_rk, 611), (32, 128, 256), jnp.float32))
        _validS = jnp.arange(128)[None, :] < _lenS[:, None]
        _validS2 = jnp.arange(128)[None, :] < _lenS2[:, None]
        _causal = jnp.tril(jnp.ones((128, 128), dtype=bool))
        mask_BxSxS2_ik1 = jnp.where(jnp.broadcast_to(_validS2[:, None, :], (32, 128, 128)), 1, 0).astype(jnp.int32)
        return (x, ctx_1024, mask_BxSxS2_ik1)
    x, ctx_1024, mask_BxSxS2_ik1 = _rec_inputs()

    def _L0_xattn_setup():
        import jax, jax.numpy as jnp
        import numpy as np
        N_HEADS = 16
        NEG_INF = -10000.0

        def _mha(q, k, v, mask):
            B, S, D = q.shape
            H = N_HEADS
            hd = D // H
            qh = q.reshape(B, S, H, hd).transpose(0, 2, 1, 3)
            kh = k.reshape(B, S, H, hd).transpose(0, 2, 1, 3)
            vh = v.reshape(B, S, H, hd).transpose(0, 2, 1, 3)
            scores = jnp.einsum('bhqd,bhkd->bhqk', qh, kh) / jnp.sqrt(jnp.float32(hd))
            scores = scores + mask[:, None, :, :].astype(scores.dtype) * NEG_INF
            probs = jax.nn.softmax(scores, axis=-1)
            out = jnp.einsum('bhqk,bhkd->bhqd', probs, vh)
            return out.transpose(0, 2, 1, 3).reshape(B, S, D)
        key = jax.random.key(seed)
        k1, k2, k3, k4 = jax.random.split(key, 4)
        B, S, D = (2, 512, 256)
        q = jax.random.normal(k1, (B, S, D), dtype=jnp.float32)
        k = jax.random.normal(k2, (B, S, D), dtype=jnp.float32)
        v = jax.random.normal(k3, (B, S, D), dtype=jnp.float32)
        mask = jax.random.randint(k4, (B, S, S), 0, 2, dtype=jnp.int32)
        return {'q': q, 'k': k, 'v': v, 'mask': mask}
    _L0_xattn_all = _L0_xattn_setup()
    _L0_xattn_in = {k: v for k, v in _L0_xattn_all.items() if k in ()}
    del _L0_xattn_all

    def _L0_ffn_setup():
        import jax, jax.numpy as jnp
        import numpy as np
        BLOCK = 32
        W_BITS = 4
        ACT_BITS = 16

        def act_qdq(x):
            qmax = 2.0 ** (ACT_BITS - 1) - 1.0
            scale = jnp.maximum(jnp.max(jnp.abs(x)) / qmax, 1e-12)
            return jnp.clip(jnp.round(x / scale), -qmax - 1.0, qmax) * scale

        def fixed_qdq_u16(x):
            scale = 1.0 / 65536.0
            return jnp.clip(jnp.round(x / scale), 0.0, 65535.0) * scale

        def lpbq_dequant(w):
            O, I = w.shape
            qmax = 2.0 ** (W_BITS - 1) - 1.0
            wb = w.reshape(O, I // BLOCK, BLOCK)
            s = jnp.maximum(jnp.max(jnp.abs(wb), axis=-1, keepdims=True) / qmax, 1e-12)
            wq = jnp.clip(jnp.round(wb / s), -qmax - 1.0, qmax) * s
            return wq.reshape(O, I)
        key = jax.random.key(seed)
        k1, k2, k3, k4 = jax.random.split(key, 4)
        B, S, H, I = (2, 1024, 256, 768)
        x = jax.random.normal(k1, (B, S, H), jnp.float32)
        w_gate = jax.random.normal(k2, (I, H), jnp.float32) * 0.02
        w_up = jax.random.normal(k3, (I, H), jnp.float32) * 0.02
        w_down = jax.random.normal(k4, (H, I), jnp.float32) * 0.02
        return {'x': x, 'w_gate': w_gate, 'w_up': w_up, 'w_down': w_down}
    _L0_ffn_all = _L0_ffn_setup()
    _L0_ffn_in = {k: v for k, v in _L0_ffn_all.items() if k in ('w_gate', 'w_up', 'w_down')}
    del _L0_ffn_all

    def _L1_xattn_setup():
        import jax, jax.numpy as jnp
        import numpy as np
        N_HEAD, MODEL_DIM, KEY_DIM, VALUE_DIM = (16, 256, 64, 64)
        B, S = (4, 512)
        EPS = 1e-05
        TEMP = float(np.sqrt(KEY_DIM))
        key = jax.random.key(seed)
        ks = jax.random.split(key, 12)
        d = {'query': jax.random.normal(ks[0], (B, S, MODEL_DIM), jnp.float32), 'key': jax.random.normal(ks[1], (B, S, MODEL_DIM), jnp.float32), 'value': jax.random.normal(ks[2], (B, S, MODEL_DIM), jnp.float32), 'Wq': jax.random.normal(ks[3], (MODEL_DIM, N_HEAD * KEY_DIM), jnp.float32) * np.sqrt(2.0 / (MODEL_DIM + KEY_DIM)), 'bq': jnp.zeros((N_HEAD * KEY_DIM,), jnp.float32), 'Wk': jax.random.normal(ks[4], (MODEL_DIM, N_HEAD * KEY_DIM), jnp.float32) * np.sqrt(2.0 / (MODEL_DIM + KEY_DIM)), 'bk': jnp.zeros((N_HEAD * KEY_DIM,), jnp.float32), 'Wv': jax.random.normal(ks[5], (MODEL_DIM, N_HEAD * VALUE_DIM), jnp.float32) * np.sqrt(2.0 / (MODEL_DIM + VALUE_DIM)), 'bv': jnp.zeros((N_HEAD * VALUE_DIM,), jnp.float32), 'Wo': jax.random.normal(ks[6], (N_HEAD * VALUE_DIM, MODEL_DIM), jnp.float32) * np.sqrt(2.0 / (N_HEAD * VALUE_DIM + MODEL_DIM)), 'bo': jnp.zeros((MODEL_DIM,), jnp.float32), 'ln_gamma': jnp.ones((MODEL_DIM,), jnp.float32), 'ln_beta': jnp.zeros((MODEL_DIM,), jnp.float32)}
        return d
    _L1_xattn_all = _L1_xattn_setup()
    _L1_xattn_in = {k: v for k, v in _L1_xattn_all.items() if k in ('Wq', 'bq', 'Wk', 'bk', 'Wv', 'bv', 'Wo', 'bo', 'ln_gamma', 'ln_beta')}
    del _L1_xattn_all

    def _L1_ffn_setup():
        import jax, jax.numpy as jnp
        import numpy as np
        E, D, H = (8, 256, 1024)
        B, S = (4, 1024)
        TEMPERATURE = 1.0
        key = jax.random.key(seed)
        ks = jax.random.split(key, 7)
        sc = 0.02
        return {'x': jax.random.normal(ks[0], (B, S, D), dtype=jnp.float32), 'W1': jax.random.normal(ks[1], (E, D, H), dtype=jnp.float32) * sc, 'b1': jax.random.normal(ks[2], (E, H), dtype=jnp.float32) * sc, 'W2': jax.random.normal(ks[3], (E, H, D), dtype=jnp.float32) * sc, 'b2': jax.random.normal(ks[4], (E, D), dtype=jnp.float32) * sc, 'Wr': jax.random.normal(ks[5], (D, E), dtype=jnp.float32) * sc, 'br': jax.random.normal(ks[6], (E,), dtype=jnp.float32) * sc}
    _L1_ffn_all = _L1_ffn_setup()
    _L1_ffn_in = {k: v for k, v in _L1_ffn_all.items() if k in ('W1', 'b1', 'W2', 'b2', 'Wr', 'br')}
    del _L1_ffn_all
    return {'x': x, 'ctx_1024': ctx_1024, 'mask_BxSxS2_ik1': mask_BxSxS2_ik1, 'L0_ffn_w_gate': _L0_ffn_in['w_gate'], 'L0_ffn_w_up': _L0_ffn_in['w_up'], 'L0_ffn_w_down': _L0_ffn_in['w_down'], 'L1_xattn_Wq': _L1_xattn_in['Wq'], 'L1_xattn_bq': _L1_xattn_in['bq'], 'L1_xattn_Wk': _L1_xattn_in['Wk'], 'L1_xattn_bk': _L1_xattn_in['bk'], 'L1_xattn_Wv': _L1_xattn_in['Wv'], 'L1_xattn_bv': _L1_xattn_in['bv'], 'L1_xattn_Wo': _L1_xattn_in['Wo'], 'L1_xattn_bo': _L1_xattn_in['bo'], 'L1_xattn_ln_gamma': _L1_xattn_in['ln_gamma'], 'L1_xattn_ln_beta': _L1_xattn_in['ln_beta'], 'L1_ffn_W1': _L1_ffn_in['W1'], 'L1_ffn_b1': _L1_ffn_in['b1'], 'L1_ffn_W2': _L1_ffn_in['W2'], 'L1_ffn_b2': _L1_ffn_in['b2'], 'L1_ffn_Wr': _L1_ffn_in['Wr'], 'L1_ffn_br': _L1_ffn_in['br']}

def reference(x, ctx_1024, mask_BxSxS2_ik1, L0_ffn_w_gate, L0_ffn_w_up, L0_ffn_w_down, L1_xattn_Wq, L1_xattn_bq, L1_xattn_Wk, L1_xattn_bk, L1_xattn_Wv, L1_xattn_bv, L1_xattn_Wo, L1_xattn_bo, L1_xattn_ln_gamma, L1_xattn_ln_beta, L1_ffn_W1, L1_ffn_b1, L1_ffn_W2, L1_ffn_b2, L1_ffn_Wr, L1_ffn_br):
    import jax
    import jax.numpy as jnp

    def _L0_xattn_ref(q, k, v, mask):
        import jax, jax.numpy as jnp
        import numpy as np
        N_HEADS = 16
        NEG_INF = -10000.0

        def _mha(q, k, v, mask):
            B, S, D = q.shape
            H = N_HEADS
            hd = D // H
            qh = q.reshape(B, S, H, hd).transpose(0, 2, 1, 3)
            kh = k.reshape(B, S, H, hd).transpose(0, 2, 1, 3)
            vh = v.reshape(B, S, H, hd).transpose(0, 2, 1, 3)
            scores = jnp.einsum('bhqd,bhkd->bhqk', qh, kh) / jnp.sqrt(jnp.float32(hd))
            scores = scores + mask[:, None, :, :].astype(scores.dtype) * NEG_INF
            probs = jax.nn.softmax(scores, axis=-1)
            out = jnp.einsum('bhqk,bhkd->bhqd', probs, vh)
            return out.transpose(0, 2, 1, 3).reshape(B, S, D)
        return _mha(q, k, v, mask)

    def _L0_ffn_ref(x, w_gate, w_up, w_down):
        import jax, jax.numpy as jnp
        import numpy as np
        BLOCK = 32
        W_BITS = 4
        ACT_BITS = 16

        def act_qdq(x):
            qmax = 2.0 ** (ACT_BITS - 1) - 1.0
            scale = jnp.maximum(jnp.max(jnp.abs(x)) / qmax, 1e-12)
            return jnp.clip(jnp.round(x / scale), -qmax - 1.0, qmax) * scale

        def fixed_qdq_u16(x):
            scale = 1.0 / 65536.0
            return jnp.clip(jnp.round(x / scale), 0.0, 65535.0) * scale

        def lpbq_dequant(w):
            O, I = w.shape
            qmax = 2.0 ** (W_BITS - 1) - 1.0
            wb = w.reshape(O, I // BLOCK, BLOCK)
            s = jnp.maximum(jnp.max(jnp.abs(wb), axis=-1, keepdims=True) / qmax, 1e-12)
            wq = jnp.clip(jnp.round(wb / s), -qmax - 1.0, qmax) * s
            return wq.reshape(O, I)
        x = act_qdq(x)
        up = act_qdq(x @ lpbq_dequant(w_up).T)
        gate = act_qdq(x @ lpbq_dequant(w_gate).T)
        sig = fixed_qdq_u16(jax.nn.sigmoid(gate))
        gate = act_qdq(gate * sig)
        o = act_qdq(gate * up)
        return o @ lpbq_dequant(w_down).T

    def _L1_xattn_ref(query, key, value, Wq, bq, Wk, bk, Wv, bv, Wo, bo, ln_gamma, ln_beta):
        import jax, jax.numpy as jnp
        import numpy as np
        N_HEAD, MODEL_DIM, KEY_DIM, VALUE_DIM = (16, 256, 64, 64)
        B, S = (4, 512)
        EPS = 1e-05
        TEMP = float(np.sqrt(KEY_DIM))
        b, sq, _ = query.shape
        residual = query
        q = (query @ Wq + bq).reshape(b, sq, N_HEAD, KEY_DIM)
        k = (key @ Wk + bk).reshape(b, key.shape[1], N_HEAD, KEY_DIM)
        v = (value @ Wv + bv).reshape(b, value.shape[1], N_HEAD, VALUE_DIM)
        scores = jnp.einsum('bqhd,bkhd->bhqk', q, k) / TEMP
        attn = jax.nn.softmax(scores, axis=-1)
        out = jnp.einsum('bhqk,bkhd->bqhd', attn, v).reshape(b, sq, N_HEAD * VALUE_DIM)
        out = out @ Wo + bo + residual
        mu = jnp.mean(out, axis=-1, keepdims=True)
        var = jnp.var(out, axis=-1, keepdims=True)
        return (out - mu) * jax.lax.rsqrt(var + EPS) * ln_gamma + ln_beta

    def _L1_ffn_ref(x, W1, b1, W2, b2, Wr, br):
        import jax, jax.numpy as jnp
        import numpy as np
        E, D, H = (8, 256, 1024)
        B, S = (4, 1024)
        TEMPERATURE = 1.0
        routing_logits = (x @ Wr + br) / TEMPERATURE
        routing_probs = jax.nn.softmax(routing_logits, axis=-1)
        indices = jnp.argmax(routing_probs, axis=-1)
        out = jnp.zeros_like(x)
        num_experts = W1.shape[0]
        for i in range(num_experts):
            mask = (indices == i).astype(x.dtype)[..., None]
            xi = x * mask
            h = jax.nn.relu(xi @ W1[i] + b1[i])
            out = out + (h @ W2[i] + b2[i])
        return out
    x = x + _L0_xattn_ref(_layernorm(x, axis=-1), ctx_1024, ctx_1024, mask_BxSxS2_ik1)
    x = x + _L0_ffn_ref(_layernorm(x, axis=-1), L0_ffn_w_gate, L0_ffn_w_up, L0_ffn_w_down)
    x = x + _L1_xattn_ref(_layernorm(x, axis=-1), ctx_1024, ctx_1024, L1_xattn_Wq, L1_xattn_bq, L1_xattn_Wk, L1_xattn_bk, L1_xattn_Wv, L1_xattn_bv, L1_xattn_Wo, L1_xattn_bo, L1_xattn_ln_gamma, L1_xattn_ln_beta)
    x = x + _L1_ffn_ref(_layernorm(x, axis=-1), L1_ffn_W1, L1_ffn_b1, L1_ffn_W2, L1_ffn_b2, L1_ffn_Wr, L1_ffn_br)
    return x

_drawn_inputs = setup_inputs


def setup_inputs(seed=0):
    import zlib

    import numpy as np

    out = dict(_drawn_inputs(seed))
    spreads = {'L1_xattn_bq': (0.0, 0.389),
     'L1_xattn_bk': (0.0, 0.8),
     'L1_xattn_bv': (0.0, 0.1),
     'L1_xattn_bo': (0.0, 0.1),
     'L1_xattn_ln_gamma': (1.0, 0.2),
     'L1_xattn_ln_beta': (0.0, 0.1)}
    factors = {'L1_ffn_b1': 5.432, 'L1_ffn_br': 3.082}
    for name, (base, spread) in spreads.items():
        noise = np.random.default_rng([zlib.crc32(name.encode()), seed]).standard_normal(out[name].shape)
        drawn = base * np.exp(spread * noise) if base else spread * noise
        out[name] = jnp.asarray(drawn.astype(out[name].dtype))
    for name, factor in factors.items():
        out[name] = (out[name] * factor).astype(out[name].dtype)
    return out
```

```python
from contextlib import ExitStack

import concourse.bass as bass
from concourse import mybir

ALU = mybir.AluOpType
ACT = mybir.ActivationFunctionType
AX_X = mybir.AxisListType.X
F32 = mybir.dt.float32
F16 = mybir.dt.float16
I32 = mybir.dt.int32
I16 = mybir.dt.int16
U16 = mybir.dt.uint16
U32 = mybir.dt.uint32

P = 128
NB = 32
D = 256
ND = D // P
NH = 16
HD0 = D // NH
HB = 4
BANK = 512
EPS = 1e-5
NEG = -10000.0
UN = 4


def inside(b, first, last):
    return not isinstance(b, int) or first <= b <= last


FF = 768
NF = FF // P
BLOCK = 32
W_MAX = 7.0
A_MAX = 32767.0
TINY = 1e-12
MAGIC = 12582912.0


def dequantise_weights(nc, ident, weights):
    COLS = FF * D // P
    NBLK = COLS // BLOCK
    used = []
    with ExitStack() as stack:
        def sb(name, shape, dt=F32):
            return stack.enter_context(nc.sbuf_tensor("w_" + name, shape, dt))

        def sem(name):
            used.append(stack.enter_context(nc.semaphore("w_" + name)))
            return used[-1]

        raw = sb("raw", [P, len(weights), NBLK, BLOCK])
        scale = sb("scale", [P, 2, NBLK])
        inv = sb("inv", [P, 2, NBLK])
        steps = sb("steps", [P, 2, NBLK, BLOCK])
        rounded = sb("rounded", [P, 2, NBLK, BLOCK], I16)
        deq = sb("deq", [P, 2, NBLK, BLOCK])
        ps = stack.enter_context(nc.psum_tensor("w_ps", [P, 4, BANK], F32))

        loaded = [sem(f"loaded{n}") for n in range(len(weights))]
        chain = sem("chain")
        deq_ready = sem("deq_ready")
        turned = sem("turned")
        copied = sem("copied")
        PER = 4
        GROUPS = COLS // P // PER

        with nc.Block() as block:

            @block.sync
            def _(sp):
                for n, (w, _) in enumerate(weights):
                    dst = raw[:, n].rearrange("p n k -> p (n k)").rearrange("p (o i) -> p o i", i=w.shape[1])
                    sp.dma_start(dst, w.rearrange("(o p) i -> p o i", p=P)).then_inc(loaded[n], 16)

            @block.vector
            def _(dve):
                done = [0]

                def then(instruction):
                    done[0] += 1
                    instruction.then_inc(chain, 1)
                    dve.wait_ge(chain, done[0])

                for n in range(len(weights)):
                    s = n % 2
                    dve.wait_ge(loaded[n], 16)

                    def wide(t):
                        return t[:, s, :].unsqueeze(2).to_broadcast([P, NBLK, BLOCK])

                    then(dve.tensor_reduce(scale[:, s], raw[:, n], AX_X, ALU.max, apply_absolute_value=True))
                    then(dve.tensor_scalar(scale[:, s], scale[:, s], 1.0 / W_MAX, TINY, ALU.mult, ALU.max))
                    then(dve.reciprocal(inv[:, s], scale[:, s]))
                    then(dve.tensor_tensor(steps[:, s], raw[:, n], wide(inv), ALU.mult))
                    then(dve.tensor_scalar(rounded[:, s], steps[:, s], W_MAX, -W_MAX - 1.0, ALU.min, ALU.max))
                    if n >= 2:
                        dve.wait_ge(turned, GROUPS * (n - 1))
                    dve.tensor_tensor(deq[:, s], rounded[:, s], wide(scale), ALU.mult).then_inc(deq_ready, 1)

            @block.tensor
            def _(pe):
                for n, (w, _) in enumerate(weights):
                    pe.wait_ge(deq_ready, n + 1)
                    flat = deq[:, n % 2].rearrange("p n k -> p (n k)")
                    for g in range(GROUPS):
                        m = GROUPS * n + g
                        if m >= 4:
                            pe.wait_ge(copied, m - 3)
                        for q in range(PER):
                            c = (PER * g + q) * P
                            last = pe.transpose(ps[:, m % 4, q * P:(q + 1) * P], flat[:, c:c + P], ident[:])
                        last.then_inc(turned, 1)

            @block.scalar
            def _(act):
                for n, (w, wT) in enumerate(weights):
                    ni = w.shape[1] // P
                    for g in range(GROUPS):
                        m = GROUPS * n + g
                        act.wait_ge(turned, m + 1)
                        for q in range(PER):
                            o, k = divmod(PER * g + q, ni)
                            last = act.activation(wT[:, k, o * P:(o + 1) * P], ps[:, m % 4, q * P:(q + 1) * P], ACT.Copy)
                        last.then_inc(copied, 1)
    return used


def attention0(nc, ident, yT, ymax, x, ctx, ctx_blocks, mask_t, x1_dram):
    HALF = NH // 2
    VW = HD0 + 1
    used = []
    with ExitStack() as ctx_stack:
        def sb(name, shape, dt=F32):
            return ctx_stack.enter_context(nc.sbuf_tensor("a_" + name, shape, dt))

        def psum(name, shape, dt=F32):
            return ctx_stack.enter_context(nc.psum_tensor("a_" + name, shape, dt))

        def sem(name):
            used.append(ctx_stack.enter_context(nc.semaphore("a_" + name)))
            return used[-1]

        x_sb = sb("x", [P, NB, D])
        v_raw = sb("v_raw", [P, NB, D])
        v_ones = sb("v_ones", [P, 2, NH, VW])
        keys = sb("keys", [P, 2, ND, HALF, 2, P])
        mask_int = sb("mask_int", [P, 8, P], I32)
        mask16 = sb("mask16", [P, NB, P], F16)
        neg_eye = sb("neg_eye", [P, HB, P], F16)
        stats0 = sb("stats0", [P, NB, 6])
        mv0 = sb("mv0", [P, NB, 2])
        var0 = sb("var0", [P, NB])
        power = sb("power", [P, NB])
        rstd0 = sb("rstd0", [P, NB])
        q_in = sb("q_in", [P, 2, D])
        qT = sb("qT", [P, 2, ND, P])
        row_max = sb("row_max", [P, 2, HALF])
        prob = sb("prob", [P, 2, 2, HALF, P])
        probT = sb("probT", [P, 4, HB, P])
        inv_sum = sb("inv_sum", [P, 2, NH])
        attn = sb("attn", [P, 2, NH, HD0])
        stats1 = sb("stats1", [P, 2, 6])
        mv1 = sb("mv1", [P, 2, 2])
        eps = sb("eps", [P, 1])
        var1 = sb("var1", [P, 2, 1])
        rstd1 = sb("rstd1", [P, 2, 1])
        y = sb("y", [P, 2, D])

        ps_score = psum("ps_score", [P, 2, HALF, P])
        ps_probT = psum("ps_probT", [P, 2, HB, P])
        ps_qy = psum("ps_qy", [P, 2, ND, P])
        ps_out = psum("ps_out", [P, BANK])
        out_heads = ps_out[:, 0:NH * VW].rearrange("p (h w) -> p h w", w=VW)

        x_loaded = [sem(f"x_loaded{c}") for c in range(4)]
        v_loaded = sem("v_loaded")
        mask_loaded = sem("mask_loaded")
        keys_loaded = [sem(f"keys_loaded{s}") for s in range(2)]
        x1_stored = sem("x1_stored")
        keys_zero = sem("keys_zero")
        consts = sem("consts")
        mask_ready = sem("mask_ready")
        v_ready = sem("v_ready")
        stats0_done = sem("stats0_done")
        mv0_done = sem("mv0_done")
        var0_done = sem("var0_done")
        rstd0_done = sem("rstd0_done")
        q_in_ready = sem("q_in_ready")
        qy_done = sem("qy_done")
        qT_ready = sem("qT_ready")
        yT_ready = sem("yT_ready")
        scores_done = sem("scores_done")
        max_done = sem("max_done")
        shifted = sem("shifted")
        exp_done = sem("exp_done")
        probT_done = sem("probT_done")
        probT_ready = sem("probT_ready")
        out_done = sem("out_done")
        inv_done = sem("inv_done")
        out_read = sem("out_read")
        x1_ready = sem("x1_ready")
        stats1_done = sem("stats1_done")
        mv1_done = sem("mv1_done")
        var1_done = sem("var1_done")
        rstd1_done = sem("rstd1_done")
        y_ready = sem("y_ready")
        y_max_done = sem("y_max_done")

        PAIR_DMAS = HALF
        NQ = NH // HB

        with nc.Block() as block:

            @block.sync
            def _(sp):
                def load_keys(pair, slot):
                    for j in range(HALF):
                        rows = slice(HD0 * j, HD0 * (j + 1))
                        for_j = keys[rows, slot, :, j, :, :]
                        sp.dma_start(for_j, ctx_blocks[pair, j]).then_inc(keys_loaded[slot], 16)

                for c in range(4):
                    part = slice(8 * c, 8 * (c + 1))
                    sp.dma_start(x_sb[:, part, :], x[part].rearrange("b t d -> t b d")).then_inc(x_loaded[c], 16)
                    if c == 0:
                        sp.dma_start(mask_int[:], mask_t[:, 0:8, :]).then_inc(mask_loaded, 16)
                        sp.wait_ge(keys_zero, 1)
                        load_keys(0, 0)
                        load_keys(1, 1)
                        sp.dma_start(v_raw[:], ctx.rearrange("b t d -> t b d")).then_inc(v_loaded, 16)
                for c in range(1, 4):
                    sp.wait_ge(mask_ready, c)
                    sp.dma_start(mask_int[:], mask_t[:, 8 * c:8 * (c + 1), :]).then_inc(mask_loaded, 16)

                def step(b, u, pair):
                    if u % 2 == 1 and inside(b, 0, NB - 5):
                        sp.wait_ge(scores_done, 2 * b + 2)
                        load_keys(pair + 2, u // 2)
                    sp.wait_ge(x1_ready, b + 1)
                    sp.dma_start(x1_dram[b], x_sb[:, b, :]).then_inc(x1_stored, 16)

                with sp.Fori(0, NB // UN - 1) as i:
                    for u in range(UN):
                        step(UN * i + u, u, 2 * i + u // 2)
                for b in range(NB - UN, NB):
                    step(b, b % UN, b // 2)
                sp.wait_ge(x1_stored, 16 * NB)

            @block.gpsimd
            def _(pool):
                def values(b, s):
                    if inside(b, 2, NB - 1):
                        pool.wait_ge(out_done, NQ * (b - 1))
                    src = v_raw[:, b, :].rearrange("p (h w) -> p h w", w=HD0)
                    pool.tensor_copy(v_ones[:, s, :, 0:HD0], src).then_inc(v_ready, 1)

                pool.memset(keys[:], 0.0).then_inc(keys_zero, 1)
                pool.memset(power[:], -0.5).then_inc(consts, 1)
                pool.memset(eps[:], EPS).then_inc(consts, 1)
                pool.memset(v_ones[:], 1.0).then_inc(consts, 1)
                pool.memset(neg_eye[:], 0.0).then_inc(consts, 1)
                pool.wait_ge(consts, 4)
                pool.affine_select(out=neg_eye[:], in_=neg_eye[:], compare_op=ALU.not_equal, fill=NEG, base=0,
                                   pattern=[[0, HB], [-1, P]], channel_multiplier=1).then_inc(consts, 1)
                for c in range(4):
                    part = slice(8 * c, 8 * (c + 1))
                    pool.wait_ge(mv0_done, 8 * (c + 1))
                    pool.tensor_scalar(var0[:, part], mv0[:, part, 1], EPS, None, ALU.add).then_inc(var0_done, 1)
                    pool.wait_ge(var0_done, c + 1)
                    pool.tensor_tensor(rstd0[:, part], var0[:, part], power[:, part], ALU.pow).then_inc(rstd0_done, 1)
                    pool.wait_ge(mask_loaded, 16 * (c + 1))
                    pool.tensor_copy(mask16[:, part, :], mask_int[:]).then_inc(mask_ready, 1)
                    if c == 0:
                        pool.wait_ge(v_loaded, 16)
                        for b in range(2):
                            values(b, b)

                def step(b, s):
                    if inside(b, 0, NB - 3):
                        values(b + 2, s)
                    pool.wait_ge(mv1_done, b + 1)
                    pool.tensor_tensor(var1[:, s], mv1[:, s, 1:2], eps[:], ALU.add).then_inc(var1_done, 1)
                    pool.wait_ge(var1_done, b + 1)
                    pool.tensor_tensor(rstd1[:, s], var1[:, s], power[:, 0:1], ALU.pow).then_inc(rstd1_done, 1)

                with pool.Fori(0, NB // UN - 1) as i:
                    for u in range(UN):
                        step(UN * i + u, u % 2)
                for b in range(NB - UN, NB):
                    step(b, b % 2)

            @block.tensor
            def _(pe):
                def scores(b, u, half):
                    if half == 0:
                        pe.wait_ge(qT_ready, b + 1)
                        if u % 2 == 0:
                            turn = 1 + b // UN if isinstance(b, int) else turns[0] + 1
                            pe.wait_ge(keys_loaded[u // 2], 16 * PAIR_DMAS * turn)
                    if inside(b, 1, NB):
                        pe.wait_ge(shifted, 2 * b + half - 1)
                    for q in range(2):
                        heads = slice(HB * q, HB * (q + 1))
                        out = ps_score[:, half, heads, :]
                        pe.matmul(out, qT[:, u % 2, half, :], keys[:, u // 2, half, heads, u % 2, :],
                                  start=True, stop=False)
                        last = pe.matmul(out, mask16[:, b, :], neg_eye[:], start=False, stop=True)
                    last.then_inc(scores_done, 1)

                def transposes(b, s, q):
                    n = NQ * b + q
                    if q % 2 == 0:
                        pe.wait_ge(exp_done, 2 * b + q // 2 + 1)
                    if inside(b, 1, NB) or q >= 2:
                        pe.wait_ge(probT_ready, n - 1)
                    for h in range(HB):
                        last = pe.transpose(ps_probT[:, q % 2, h, :], prob[:, s, q // 2, HB * (q % 2) + h, :], ident[:])
                    last.then_inc(probT_done, 1)

                def weighted(b, u, q):
                    pe.wait_ge(probT_ready, NQ * b + q + 1)
                    if q == 0:
                        pe.wait_ge(v_ready, b + 1)
                        if inside(b, 1, NB):
                            pe.wait_ge(out_read, b)
                    for h in range(HB):
                        head = HB * q + h
                        last = pe.matmul(out_heads[:, head, :], probT[:, q, h, :], v_ones[:, u % 2, head, :],
                                         start=True, stop=True)
                    last.then_inc(out_done, 1)

                def turn_qy(g, s):
                    if inside(g, 5, NB + 4):
                        pe.wait_ge(yT_ready, g - 4)
                    elif g >= 1:
                        pe.wait_ge(qT_ready, g)
                    if inside(g, 0, NB - 1):
                        pe.wait_ge(q_in_ready, g + 1)
                        for k in range(ND):
                            last = pe.transpose(ps_qy[:, 0, k, :], q_in[:, s, k * P:(k + 1) * P], ident[:])
                    if inside(g, 4, NB + 3):
                        pe.wait_ge(y_ready, g - 3)
                        for k in range(ND):
                            last = pe.transpose(ps_qy[:, 1, k, :], y[:, s, k * P:(k + 1) * P], ident[:])
                    last.then_inc(qy_done, 1)

                def step(b, u):
                    for half in range(2):
                        if inside(b, 0, NB - 1):
                            scores(b, u, half)
                        if inside(b, 1, NB):
                            p, pu = b - 1, (u - 1) % UN
                            if half == 0:
                                transposes(p, pu % 2, 0)
                                transposes(p, pu % 2, 1)
                            else:
                                weighted(p, pu, 0)
                                weighted(p, pu, 1)
                                transposes(p, pu % 2, 2)
                                transposes(p, pu % 2, 3)
                                turn_qy(b + 1, (u + 1) % 2)
                                weighted(p, pu, 2)
                                weighted(p, pu, 3)
                    if isinstance(b, int) and (b < 1 or b > NB):
                        turn_qy(b + 1, (u + 1) % 2)

                pe.wait_ge(mask_ready, 4)
                pe.wait_ge(consts, 4)
                turn_qy(0, 0)
                turns = [0]
                for b in range(UN):
                    step(b, b % UN)
                with pe.Fori(1, NB // UN - 1) as i:
                    turns[0] = i
                    for u in range(UN):
                        step(UN * i + u, u)
                for b in range(NB - UN, NB + 3):
                    step(b, b % UN)

            @block.vector
            def _(dve):
                def queries(b, s):
                    dve.wait_ge(rstd0_done, b // 8 + 1 if isinstance(b, int) else 4)
                    if inside(b, 2, NB - 1):
                        dve.wait_ge(qy_done, b - 1)
                    dve.tensor_scalar(q_in[:, s, :], x_sb[:, b, :], mv0[:, b, 0:1], rstd0[:, bass.ds(b, 1)],
                                      ALU.subtract, ALU.mult).then_inc(q_in_ready, 1)

                def softmax_shift(b, s, half):
                    n = 2 * b + half + 1
                    dve.wait_ge(scores_done, n)
                    dve.tensor_reduce(row_max[:, half, :], ps_score[:, half], AX_X, ALU.max).then_inc(max_done, 1)
                    dve.wait_ge(max_done, n)
                    if inside(b, 2, NB):
                        dve.wait_ge(probT_done, NQ * (b - 2) + 2 * half + 2)
                    dve.tensor_tensor(prob[:, s, half], ps_score[:, half],
                                      row_max[:, half, :].unsqueeze(2).to_broadcast([P, HALF, P]),
                                      ALU.subtract).then_inc(shifted, 1)

                def residual(b, s):
                    dve.wait_ge(out_done, NQ * b + NQ)
                    dve.reciprocal(inv_sum[:, s, :].unsqueeze(2), out_heads[:, :, HD0:VW]).then_inc(inv_done, 1)
                    dve.wait_ge(inv_done, b + 1)
                    dve.tensor_tensor(attn[:, s], out_heads[:, :, 0:HD0],
                                      inv_sum[:, s, :].unsqueeze(2).to_broadcast([P, NH, HD0]),
                                      ALU.mult).then_inc(out_read, 1)
                    dve.wait_ge(out_read, b + 1)
                    dve.tensor_tensor(x_sb[:, b, :], x_sb[:, b, :], attn[:, s].rearrange("p h w -> p (h w)"),
                                      ALU.add).then_inc(x1_ready, 1)
                    dve.wait_ge(stats0_done, NB)
                    dve.wait_ge(x1_ready, b + 1)
                    dve.bn_stats(stats1[:, s, :], x_sb[:, b, :]).then_inc(stats1_done, 1)
                    dve.wait_ge(stats0_done, NB)
                    dve.wait_ge(stats1_done, b + 1)
                    dve.bn_aggr(mv1[:, s, :], stats1[:, s, :]).then_inc(mv1_done, 1)

                def normalise(b, s):
                    dve.wait_ge(rstd1_done, b + 1)
                    if inside(b, 2, NB - 1):
                        dve.wait_ge(qy_done, b + 3)
                    dve.tensor_scalar(y[:, s, :], x_sb[:, b, :], mv1[:, s, 0:1], rstd1[:, s, :],
                                      ALU.subtract, ALU.mult).then_inc(y_ready, 1)
                    dve.wait_ge(y_ready, b + 1)
                    dve.tensor_reduce(ymax[:, bass.ds(b, 1)], y[:, s, :], AX_X, ALU.max, apply_absolute_value=True)\
                       .then_inc(y_max_done, 1)

                def step(b, s):
                    if inside(b, 0, NB - 2):
                        queries(b + 1, 1 - s)
                    if inside(b, 0, NB - 1):
                        softmax_shift(b, s, 0)
                        softmax_shift(b, s, 1)
                    if inside(b, 2, NB + 1):
                        normalise(b - 2, s)
                    if inside(b, 1, NB):
                        residual(b - 1, 1 - s)

                for b in range(NB):
                    dve.wait_ge(x_loaded[b // 8], 16)
                    dve.bn_stats(stats0[:, b, :], x_sb[:, b, :]).then_inc(stats0_done, 1)
                    if b >= 1:
                        dve.wait_ge(stats0_done, b)
                        dve.bn_aggr(mv0[:, b - 1, :], stats0[:, b - 1, :]).then_inc(mv0_done, 1)
                dve.wait_ge(stats0_done, NB)
                dve.bn_aggr(mv0[:, NB - 1, :], stats0[:, NB - 1, :]).then_inc(mv0_done, 1)
                queries(0, 0)
                for b in range(UN):
                    step(b, b % 2)
                with dve.Fori(1, NB // UN - 1) as i:
                    for u in range(UN):
                        step(UN * i + u, u % 2)
                for b in range(NB - UN, NB + 2):
                    step(b, b % 2)

            @block.scalar
            def _(act):
                def exponentials(b, s, half):
                    act.wait_ge(shifted, 2 * b + half + 1)
                    act.activation(prob[:, s, half], prob[:, s, half], ACT.Exp).then_inc(exp_done, 1)

                def copy_probT(b, q):
                    act.wait_ge(probT_done, NQ * b + q + 1)
                    if inside(b, 1, NB):
                        act.wait_ge(out_done, NQ * b + q - 3)
                    act.activation(probT[:, q], ps_probT[:, q % 2], ACT.Copy).then_inc(probT_ready, 1)

                def copy_qy(g, s):
                    act.wait_ge(qy_done, g + 1)
                    if inside(g, 0, NB - 1):
                        if inside(g, 2, NB - 1):
                            act.wait_ge(scores_done, 2 * g - 2)
                        last = act.activation(qT[:, s], ps_qy[:, 0], ACT.Copy, scale=float(HD0) ** -0.5)
                        last.then_inc(qT_ready, 1)
                    if inside(g, 4, NB + 3):
                        act.activation(yT[:, :, bass.ds((g - 4) * P, P)], ps_qy[:, 1], ACT.Copy).then_inc(yT_ready, 1)

                def step(b, u):
                    s = (u + 1) % 2
                    for half in range(2):
                        if inside(b, 1, NB):
                            copy_probT(b - 1, 2 * half)
                            copy_probT(b - 1, 2 * half + 1)
                        if inside(b, 0, NB - 1):
                            exponentials(b, 1 - s, half)
                    copy_qy(b + 1, s)

                copy_qy(0, 0)
                for b in range(UN):
                    step(b, b % UN)
                with act.Fori(1, NB // UN - 1) as i:
                    for u in range(UN):
                        step(UN * i + u, u)
                for b in range(NB - UN, NB + 3):
                    step(b, b % UN)
    return used


def feed_forward0(nc, yT, ymax, upT, gateT, downT, x1_dram, x2_dram, mv2, rstd2):
    T = NB * P
    CH = BANK
    NC = T // CH
    COLS = NF * T
    UNIT = 2048
    NU = COLS // UNIT
    with ExitStack() as stack:
        def sb(name, shape, dt=F32):
            return stack.enter_context(nc.sbuf_tensor("b_" + name, shape, dt))

        def sem(name):
            return stack.enter_context(nc.semaphore("b_" + name))

        act_sb = sb("act", [P, NF, T])
        up16 = sb("up16", [P, NF, T], I16)
        act_flat = act_sb[:].rearrange("p f t -> p (f t)")
        up_flat = up16[:].rearrange("p f t -> p (f t)")
        spare = yT[:].rearrange("p k t -> p (k t)")
        quant = spare[:, 0:UNIT].bitcast(I16).rearrange("p (s n) -> p s n", s=2)
        sig16 = spare[:, UNIT:2 * UNIT].bitcast(U16).rearrange("p (s n) -> p s n", s=2)
        sig = spare[:, 2 * UNIT:4 * UNIT].rearrange("p (s n) -> p s n", s=2)
        inner = spare[:, 0:2 * NF * CH].rearrange("p (s f t) -> p s f t", s=2, f=NF)

        pmax = sb("pmax", [P, NF * NC])
        one = sb("one", [P, 8, 1])
        factors = sb("factors", [P, 5, 2, 1])
        x1_sb = sb("x1", [P, 4, D])
        x2_sb = sb("x2", [P, 4, D])
        stats2 = sb("stats2", [P, NB, 6])
        var2 = sb("var2", [P, NB])
        power = sb("power", [P, NB])
        ps = stack.enter_context(nc.psum_tensor("b_ps", [P, 8, BANK], F32))

        consts = sem("consts")
        part_max = sem("part_max")
        all_max = sem("all_max")
        scalars = sem("scalars")
        scale_ready = sem("scale_ready")
        y_rounded = sem("y_rounded")
        y_ready = sem("y_ready")
        product_done = sem("product_done")
        copied = sem("copied")
        max_done = sem("max_done")
        up_ready = sem("up_ready")
        gate_quant = sem("gate_quant")
        sig_done = sem("sig_done")
        sig_quant = sem("sig_quant")
        silu_done = sem("silu_done")
        silu_quant = sem("silu_quant")
        inner_done = sem("inner_done")
        inner_rounded = sem("inner_rounded")
        inner_ready = sem("inner_ready")
        down_done = sem("down_done")
        x1_loaded = [sem(f"x1_loaded{s}") for s in range(4)]
        x2_ready = sem("x2_ready")
        x2_stored = [sem(f"x2_stored{s}") for s in range(4)]
        stats_done = sem("stats_done")
        mv_done = sem("mv_done")
        var_done = sem("var_done")
        rstd_done = sem("rstd_done")

        Y, UP, GATE, SILU, INNER = range(5)
        TILES = CH // P

        with nc.Block() as block:

            @block.sync
            def _(sp):
                def step(t, s):
                    if inside(t, 4, NB - 1):
                        sp.wait_ge(x2_ready, t - 3)
                    sp.dma_start(x1_sb[:, s, :], x1_dram[t]).then_inc(x1_loaded[s], 16)
                    if inside(t, 3, NB - 1):
                        store(t - 3, (s + 1) % 4)

                def store(t, s):
                    sp.wait_ge(x2_ready, t + 1)
                    sp.dma_start(x2_dram[t], x2_sb[:, s, :]).then_inc(x2_stored[s], 16)

                for t in range(4):
                    step(t, t)
                with sp.Fori(1, NB // 4) as i:
                    for s in range(4):
                        step(4 * i + s, s)
                for t in range(NB - 3, NB):
                    store(t, t % 4)
                for s in range(4):
                    sp.wait_ge(x2_stored[s], 16 * NB // 4)

            @block.gpsimd
            def _(pool):
                pool.memset(power[:], -0.5).then_inc(consts, 1)
                for n in range(5):
                    pool.wait_ge(part_max, n + 1)
                    pool.partition_all_reduce(one[:, 1, :], one[:, 0, :], P, bass.bass_isa.ReduceOp.max)\
                        .then_inc(all_max, 1)
                pool.wait_ge(consts, 1)
                pool.wait_ge(mv_done, NB)
                pool.tensor_scalar(var2[:], mv2[:, :, 1], EPS, None, ALU.add).then_inc(var_done, 1)
                pool.wait_ge(var_done, 1)
                pool.tensor_tensor(rstd2[:], var2[:], power[:], ALU.pow).then_inc(rstd_done, 1)

            @block.tensor
            def _(pe):
                for m, wT in enumerate((upT, gateT)):
                    def chunk(c):
                        if m == 0:
                            pe.wait_ge(y_ready, c + 1)
                        for f in range(NF):
                            n = NF * (c + NC * m) + f
                            if inside(n, NF, 2 * NC * NF):
                                pe.wait_ge(copied, n - NF + 1)
                            for k in range(ND):
                                last = pe.matmul(ps[:, f, :], wT[:, k, f * P:(f + 1) * P],
                                                 yT[:, k, bass.ds(c * CH, CH)], start=(k == 0), stop=(k == ND - 1))
                            last.then_inc(product_done, 1)

                    chunk(0)
                    with pe.Fori(1, NC) as c:
                        chunk(c)

                def down(c, s):
                    pe.wait_ge(inner_ready, c + 1)
                    for t in range(TILES):
                        n = TILES * c + t
                        if inside(n, 2, NB):
                            pe.wait_ge(x2_ready, n - 1)
                        for f in range(NF):
                            last = pe.matmul(ps[:, 6 + t % 2, 0:D], inner[:, s, f, t * P:(t + 1) * P], downT[:, f, :],
                                             start=(f == 0), stop=(f == NF - 1))
                        last.then_inc(down_done, 1)

                for c in range(2):
                    down(c, c)
                with pe.Fori(1, NC // 2) as i:
                    for s in range(2):
                        down(2 * i + s, s)

            @block.scalar
            def _(act):
                def whole_y(c):
                    act.wait_ge(y_rounded, c + 1)
                    part = yT[:, :, bass.ds(c * CH, CH)]
                    act.activation(part, part, ACT.Copy, bias=-MAGIC).then_inc(y_ready, 1)

                def copy_chunk(c, m):
                    if m == 1:
                        act.wait_ge(up_ready, c + 1)
                    for f in range(NF):
                        act.wait_ge(product_done, NF * (c + NC * m) + f + 1)
                        act.activation(act_sb[:, f, bass.ds(c * CH, CH)], ps[:, f, :], ACT.Copy).then_inc(copied, 1)

                whole_y(0)
                whole_y(1)
                with act.Fori(0, NC - 2) as c:
                    whole_y(c + 2)
                    copy_chunk(c, 0)
                for c in range(NC - 2, NC):
                    copy_chunk(c, 0)
                with act.Fori(0, NC) as c:
                    copy_chunk(c, 1)

                act.wait_ge(scale_ready, GATE + 1)
                with act.Fori(0, NU // 2) as i:
                    for s in range(2):
                        u = 2 * i + s
                        act.wait_ge(gate_quant, u + 1)
                        act.activation(sig[:, s, :], quant[:, s, :], ACT.Sigmoid, scale=factors[:, GATE, 0, :])\
                           .then_inc(sig_done, 1)

                def whole_inner(c, s):
                    act.wait_ge(inner_rounded, c + 1)
                    if inside(c, 2, NC):
                        act.wait_ge(down_done, TILES * (c - 1))
                    act.activation(inner[:, s], act_sb[:, :, bass.ds(c * CH, CH)], ACT.Copy, bias=-MAGIC)\
                       .then_inc(inner_ready, 1)

                for c in range(2):
                    whole_inner(c, c)
                with act.Fori(1, NC // 2) as i:
                    for s in range(2):
                        whole_inner(2 * i + s, s)

            @block.vector
            def _(dve):
                done = [0]

                def then(instruction):
                    done[0] += 1
                    instruction.then_inc(scalars, 1)
                    dve.wait_ge(scalars, done[0])

                def scale_of(n, maxima, unit):
                    dve.tensor_reduce(one[:, 0, :], maxima, AX_X, ALU.max).then_inc(part_max, 1)
                    dve.wait_ge(all_max, n + 1)
                    scale, factor = factors[:, n, 0, :], factors[:, n, 1, :]
                    if unit is None:
                        then(dve.tensor_scalar(scale, one[:, 1, :], 1.0 / A_MAX, TINY, ALU.mult, ALU.max))
                        dve.reciprocal(factor, scale).then_inc(scale_ready, 1)
                    else:
                        then(dve.tensor_scalar(one[:, 2, :], one[:, 1, :], unit, 1.0 / A_MAX, ALU.mult, ALU.mult))
                        then(dve.tensor_scalar(scale, one[:, 2, :], TINY, None, ALU.max))
                        then(dve.reciprocal(one[:, 3, :], scale))
                        dve.tensor_tensor(factor, one[:, 3, :], unit, ALU.mult).then_inc(scale_ready, 1)
                    dve.wait_ge(scale_ready, n + 1)

                def maxima_of_chunk(c, m):
                    for f in range(NF):
                        n = NF * c + f
                        dve.wait_ge(copied, n + NF * NC * m + 1)
                        dve.tensor_reduce(pmax[:, bass.ds(n, 1)], act_sb[:, f, bass.ds(c * CH, CH)], AX_X, ALU.max,
                                          apply_absolute_value=True).then_inc(max_done, 1)

                scale_of(Y, ymax[:], None)
                with dve.Fori(0, NC) as c:
                    part = yT[:, :, bass.ds(c * CH, CH)]
                    dve.tensor_scalar(part, part, factors[:, Y, 1, :], MAGIC, ALU.mult, ALU.add).then_inc(y_rounded, 1)
                with dve.Fori(0, NC) as c:
                    maxima_of_chunk(c, 0)
                dve.wait_ge(max_done, NF * NC)
                scale_of(UP, pmax[:], factors[:, Y, 0, :])
                with dve.Fori(0, NC) as c:
                    part = bass.ds(c * CH, CH)
                    dve.tensor_scalar(up16[:, :, part], act_sb[:, :, part], factors[:, UP, 1, :], None, ALU.mult)\
                       .then_inc(up_ready, 1)
                with dve.Fori(0, NC) as c:
                    maxima_of_chunk(c, 1)
                dve.wait_ge(max_done, 2 * NF * NC)
                scale_of(GATE, pmax[:], factors[:, Y, 0, :])

                def quantise_gate(u, s):
                    if inside(u, 2, NU):
                        dve.wait_ge(silu_done, u - 1)
                    dve.tensor_scalar(quant[:, s, :], act_flat[:, bass.ds(u * UNIT, UNIT)], factors[:, GATE, 1, :], None,
                                      ALU.mult).then_inc(gate_quant, 1)

                def silu(u, s):
                    cols = act_flat[:, bass.ds(u * UNIT, UNIT)]
                    dve.wait_ge(sig_done, u + 1)
                    dve.tensor_scalar(sig16[:, s, :], sig[:, s, :], 65536.0, 65535.0, ALU.mult, ALU.min)\
                       .then_inc(sig_quant, 1)
                    dve.wait_ge(sig_quant, u + 1)
                    dve.tensor_tensor(cols, quant[:, s, :], sig16[:, s, :], ALU.mult).then_inc(silu_done, 1)
                    dve.wait_ge(silu_done, u + 1)
                    dve.tensor_reduce(pmax[:, bass.ds(u, 1)], cols, AX_X, ALU.max, apply_absolute_value=True)\
                       .then_inc(max_done, 1)

                quantise_gate(0, 0)
                quantise_gate(1, 1)
                silu(0, 0)
                quantise_gate(2, 0)
                silu(1, 1)
                with dve.Fori(1, NU // 2 - 1) as i:
                    for s in range(2):
                        quantise_gate(2 * i + s + 1, 1 - s)
                        silu(2 * i + s, s)
                quantise_gate(NU - 1, 1)
                silu(NU - 2, 0)
                silu(NU - 1, 1)
                dve.wait_ge(max_done, 2 * NF * NC + NU)
                then(dve.tensor_scalar(one[:, 4, :], factors[:, GATE, 0, :], 1.0 / 65536.0, None, ALU.mult))
                scale_of(SILU, pmax[:, 0:NU], one[:, 4, :])

                def times_up(u, s):
                    cols = act_flat[:, bass.ds(u * UNIT, UNIT)]
                    dve.tensor_scalar(quant[:, s, :], cols, factors[:, SILU, 1, :], None, ALU.mult).then_inc(silu_quant, 1)
                    dve.wait_ge(silu_quant, u + 1)
                    dve.tensor_tensor(cols, quant[:, s, :], up_flat[:, bass.ds(u * UNIT, UNIT)], ALU.mult)\
                       .then_inc(inner_done, 1)
                    dve.wait_ge(inner_done, u + 1)
                    dve.tensor_reduce(pmax[:, bass.ds(u, 1)], cols, AX_X, ALU.max, apply_absolute_value=True)\
                       .then_inc(max_done, 1)

                with dve.Fori(0, NU // 2) as i:
                    for s in range(2):
                        times_up(2 * i + s, s)
                dve.wait_ge(max_done, 2 * NF * NC + 2 * NU)
                then(dve.tensor_tensor(one[:, 5, :], factors[:, SILU, 0, :], factors[:, UP, 0, :], ALU.mult))
                scale_of(INNER, pmax[:, 0:NU], one[:, 5, :])

                def round_inner(c):
                    part = act_sb[:, :, bass.ds(c * CH, CH)]
                    dve.tensor_scalar(part, part, factors[:, INNER, 1, :], MAGIC, ALU.mult, ALU.add).then_inc(inner_rounded, 1)

                def residual(t, s):
                    dve.wait_ge(down_done, t + 1)
                    dve.wait_ge(x1_loaded[s], 16 * (t // 4 + 1 if isinstance(t, int) else turn[0] + 1))
                    if inside(t, 4, NB - 1):
                        dve.wait_ge(x2_stored[s], 16 * (t // 4 if isinstance(t, int) else turn[0]))
                    dve.scalar_tensor_tensor(x2_sb[:, s, :], ps[:, 6 + s % 2, 0:D], factors[:, INNER, 0, :],
                                             x1_sb[:, s, :], ALU.mult, ALU.add).then_inc(x2_ready, 1)
                    dve.wait_ge(all_max, 1)
                    dve.wait_ge(x2_ready, t + 1)
                    dve.bn_stats(stats2[:, t, :], x2_sb[:, s, :]).then_inc(stats_done, 1)

                turn = [0]
                round_inner(0)
                round_inner(1)
                for t in range(TILES):
                    residual(t, t)
                with dve.Fori(1, NC - 1) as c:
                    turn[0] = c
                    round_inner(c + 1)
                    for s in range(TILES):
                        residual(TILES * c + s, s)
                for t in range(NB - TILES, NB):
                    residual(t, t % 4)
                dve.wait_ge(stats_done, NB)
                for t in range(NB):
                    dve.bn_aggr(mv2[:, t, :], stats2[:, t, :]).then_inc(mv_done, 1)


KD = 64
INNER_C = NH * KD
NE = 8


def attention1(nc, ident, mv2, rstd2, logits, w, ctx_t, x2_dram, x3_dram, z_dram):
    BLKS = INNER_C // P
    VW = KD + 1
    PT = 2 * P
    NU = NH // HB
    FIRST, LAST = -4, NB + 3
    with ExitStack() as stack:
        def sb(name, shape, dt=F32):
            return stack.enter_context(nc.sbuf_tensor("c_" + name, shape, dt))

        def psum(name, shape, dt=F32):
            return stack.enter_context(nc.psum_tensor("c_" + name, shape, dt))

        def sem(name):
            return stack.enter_context(nc.semaphore("c_" + name))

        wq = sb("wq", [P, ND, INNER_C])
        wk = sb("wk", [P, ND, INNER_C])
        wv = sb("wv", [P, ND, INNER_C])
        wo = sb("wo", [P, BLKS, D])
        wr = sb("wr", [P, ND, NE])
        bq = sb("bq", [P, BLKS])
        bk = sb("bk", [P, BLKS])
        bv = sb("bv", [P, INNER_C])
        bo = sb("bo", [P, D])
        gamma = sb("gamma", [P, D])
        beta = sb("beta", [P, D])
        br = sb("br", [P, NE])
        power = sb("power", [P, 1])
        ctxT = sb("ctxT", [P, 2, ND, PT])
        x2_early = sb("x2_early", [P, 4, D])
        x2_late = sb("x2_late", [P, 4, D])
        xn = sb("xn", [P, 2, D])
        xnT = sb("xnT", [P, 2, ND, PT])
        qT = sb("qT", [P, 2, BLKS, PT])
        kT = sb("kT", [P, 2, BLKS, PT])
        v_ones = sb("v_ones", [P, 2, 2, NH, VW])
        row_max = sb("row_max", [P, NU, HB])
        prob = sb("prob", [P, NU, HB, P])
        probT = sb("probT", [P, NU, HB, P])
        inv_sum = sb("inv_sum", [P, NU, HB])
        attn = sb("attn", [P, 2, 2, HB, 2, KD])
        attnT = sb("attnT", [P, 2, BLKS, P])
        eps = sb("eps", [P, 1])
        centred = sb("centred", [P, 2, D])
        xn_late = sb("xn_late", [P, 2, D])
        xn_bo = sb("xn_bo", [P, 2, D])
        x2_beta = sb("x2_beta", [P, 4, D])
        proj = sb("proj", [P, 2, D])
        stats_o = sb("stats_o", [P, 2, 6])
        mv_o = sb("mv_o", [P, 2, 2])
        var_o = sb("var_o", [P, 2, 1])
        rstd_o = sb("rstd_o", [P, 2, 1])
        normed = sb("normed", [P, 2, D])
        scaled = sb("scaled", [P, 2, D])
        x3 = sb("x3", [P, 4, D])
        stats_3 = sb("stats_3", [P, 2, 6])
        mv_3 = sb("mv_3", [P, 2, 2])
        var_3 = sb("var_3", [P, 2, 1])
        rstd_3 = sb("rstd_3", [P, 2, 1])
        z = sb("z", [P, 4, D])
        zT = sb("zT", [P, 2, ND, P])

        ps_score = psum("ps_score", [P, 2, HB, P])
        ps_probT = psum("ps_probT", [P, 2, HB, P])
        ps_out = psum("ps_out", [P, BANK])
        ps_proj = psum("ps_proj", [P, 2, BANK])
        ps_aux = psum("ps_aux", [P, BANK])
        out_heads = ps_out[:, 0:HB * VW].rearrange("p (h w) -> p h w", w=VW)

        w_loaded = sem("w_loaded")
        bias_loaded = sem("bias_loaded")
        ctx_loaded = [sem(f"ctx_loaded{s}") for s in range(2)]
        early_loaded = [sem(f"early_loaded{s}") for s in range(4)]
        late_loaded = [sem(f"late_loaded{s}") for s in range(4)]
        x3_stored = [sem(f"x3_stored{s}") for s in range(4)]
        z_stored = [sem(f"z_stored{s}") for s in range(4)]
        consts = sem("consts")
        xn_ready = sem("xn_ready")
        xnT_done = sem("xnT_done")
        xnT_ready = sem("xnT_ready")
        proj_done = sem("proj_done")
        qk_ready = sem("qk_ready")
        v_ready = sem("v_ready")
        scores_done = sem("scores_done")
        max_done = sem("max_done")
        shifted = sem("shifted")
        exp_done = sem("exp_done")
        probT_done = sem("probT_done")
        probT_ready = sem("probT_ready")
        out_done = sem("out_done")
        inv_done = sem("inv_done")
        attn_ready = sem("attn_ready")
        attnT_done = sem("attnT_done")
        attnT_ready = sem("attnT_ready")
        output_done = sem("output_done")
        proj_ready = sem("proj_ready")
        late_centred = sem("late_centred")
        late_norm = sem("late_norm")
        xn_bo_ready = sem("xn_bo_ready")
        x2_beta_ready = sem("x2_beta_ready")
        stats_o_done = sem("stats_o_done")
        mv_o_done = sem("mv_o_done")
        var_o_done = sem("var_o_done")
        rstd_o_done = sem("rstd_o_done")
        normed_done = sem("normed_done")
        scaled_done = sem("scaled_done")
        x3_ready = sem("x3_ready")
        stats_3_done = sem("stats_3_done")
        mv_3_done = sem("mv_3_done")
        var_3_done = sem("var_3_done")
        rstd_3_done = sem("rstd_3_done")
        z_ready = sem("z_ready")
        zT_done = sem("zT_done")
        zT_ready = sem("zT_ready")
        logits_done = sem("logits_done")
        logits_read = sem("logits_read")

        N_W, N_BIAS = 5, 7
        projects = (-2, NB - 3)

        def uses(t, turn):
            return t // 4 + 1 if isinstance(t, int) else turn

        def run_steps(engine, step, first=FIRST, last=LAST):
            for b in range(first, 4):
                step(b, b % 4, None)
            with engine.Fori(1, NB // 4 - 1) as i:
                for u in range(4):
                    step(4 * i + u, u, i)
            for b in range(NB - 4, last + 1):
                step(b, b % 4, None)

        with nc.Block() as block:

            @block.sync
            def _(sp):
                def early(t, s):
                    if inside(t, 4, NB - 1):
                        sp.wait_ge(xn_ready, t - 3)
                    sp.dma_start(x2_early[:, s, :], x2_dram[t]).then_inc(early_loaded[s], 16)

                def late(t, s):
                    if inside(t, 4, NB - 1):
                        sp.wait_ge(x2_beta_ready, t - 3)
                    sp.dma_start(x2_late[:, s, :], x2_dram[t]).then_inc(late_loaded[s], 16)

                def context(pair, s):
                    if inside(pair, 2, NB // 2 - 1):
                        sp.wait_ge(proj_done, 12 * (pair - 1))
                    sp.dma_start(ctxT[:, s], ctx_t[:, :, bass.ds(pair * PT, PT)]).then_inc(ctx_loaded[s], 16)

                def step(b, u, i):
                    if inside(b, FIRST, NB - 5):
                        early(b + 4, u)
                    if inside(b, -2, NB - 3):
                        late(b + 2, (u + 2) % 4)
                    if u % 2 == 0 and inside(b, 0, NB - 5):
                        context(b // 2 + 2 if isinstance(b, int) else 2 * i + u // 2 + 2, (u // 2) % 2)
                    if inside(b, 3, NB + 2):
                        sp.wait_ge(x3_ready, b - 2)
                        sp.dma_start(x3_dram[b - 3], x3[:, (u + 1) % 4, :]).then_inc(x3_stored[(u + 1) % 4], 16)
                    if inside(b, 4, NB + 3):
                        sp.wait_ge(z_ready, b - 3)
                        sp.dma_start(z_dram[b - 4], z[:, u, :]).then_inc(z_stored[u], 16)

                for b in range(FIRST, 0):
                    step(b, b % 4, None)
                for dst, src in ((wq, w["wq"]), (wk, w["wk"])):
                    sp.dma_start(dst[:], src).then_inc(w_loaded, 16)
                for dst, src in ((bq, w["bq"]), (bk, w["bk"])):
                    sp.dma_start(dst[:], src).then_inc(bias_loaded, 16)
                context(0, 0)
                sp.dma_start(wv[:], w["wv"]).then_inc(w_loaded, 16)
                for dst, src in ((bv, w["bv"]), (bo, w["bo"]), (gamma, w["gamma"]), (beta, w["beta"]), (br, w["br"])):
                    sp.dma_start(dst[:], src.partition_broadcast(P)).then_inc(bias_loaded, 16)
                context(1, 1)
                for dst, src in ((wo, w["wo"]), (wr, w["wr"])):
                    sp.dma_start(dst[:], src).then_inc(w_loaded, 16)
                run_steps(sp, step, 0)
                for s in range(4):
                    sp.wait_ge(x3_stored[s], 16 * NB // 4)
                    sp.wait_ge(z_stored[s], 16 * NB // 4)

            @block.gpsimd
            def _(pool):
                pool.memset(power[:], -0.5).then_inc(consts, 1)
                pool.memset(eps[:], EPS).then_inc(consts, 1)
                pool.memset(v_ones[:], 1.0).then_inc(consts, 1)
                pool.wait_ge(consts, 3)
                pool.wait_ge(bias_loaded, 16 * N_BIAS)

                def residuals(t, u, i):
                    s = u % 2
                    pool.wait_ge(late_loaded[u], 16 * uses(t, None if i is None else i + 1))
                    if inside(t, 2, NB - 1):
                        pool.wait_ge(xn_bo_ready, t - 1)
                    pool.tensor_tensor(centred[:, s, :], x2_late[:, u, :], mv2[:, t, 0:1].to_broadcast([P, D]),
                                       ALU.subtract).then_inc(late_centred, 1)
                    pool.wait_ge(consts, 3)
                    pool.wait_ge(late_centred, t + 1)
                    pool.tensor_tensor(xn_late[:, s, :], centred[:, s, :], rstd2[:, bass.ds(t, 1)].to_broadcast([P, D]),
                                       ALU.mult).then_inc(late_norm, 1)
                    pool.wait_ge(late_norm, t + 1)
                    if inside(t, 2, NB - 1):
                        pool.wait_ge(proj_ready, t - 1)
                    pool.tensor_tensor(xn_bo[:, s, :], xn_late[:, s, :], bo[:], ALU.add).then_inc(xn_bo_ready, 1)
                    if inside(t, 4, NB - 1):
                        pool.wait_ge(x3_ready, t - 3)
                    pool.tensor_tensor(x2_beta[:, u, :], x2_late[:, u, :], beta[:], ALU.add).then_inc(x2_beta_ready, 1)

                def inverse_deviation(t, s, var, mv, rstd, mv_done, var_done, rstd_done):
                    pool.wait_ge(mv_done, t + 1)
                    pool.tensor_tensor(var[:, s], mv[:, s, 1:2], eps[:], ALU.add).then_inc(var_done, 1)
                    pool.wait_ge(var_done, t + 1)
                    pool.tensor_tensor(rstd[:, s], var[:, s], power[:], ALU.pow).then_inc(rstd_done, 1)

                def step(b, u, i):
                    if inside(b, 0, NB - 1):
                        residuals(b, u, i)
                    if inside(b, 2, NB + 1):
                        inverse_deviation(b - 2, u % 2, var_3, mv_3, rstd_3, mv_3_done, var_3_done, rstd_3_done)
                    if inside(b, 1, NB):
                        inverse_deviation(b - 1, (u + 1) % 2, var_o, mv_o, rstd_o, mv_o_done, var_o_done, rstd_o_done)

                run_steps(pool, step, 0, NB + 1)

            @block.tensor
            def _(pe):
                def scores(b, u, n):
                    g, r = divmod(n, 2)
                    s, tok = u // 2, slice((u % 2) * P, (u % 2 + 1) * P)
                    rows = slice(r * KD, (r + 1) * KD)
                    if n == 0 and u % 2 == 0:
                        pe.wait_ge(qk_ready, BLKS * (b + 2))
                    if inside(b, 1, NB) or n >= 2:
                        pe.wait_ge(shifted, NU * b + n - 1)
                    for j in range(HB):
                        blk = HB * g + j
                        last = pe.matmul(ps_score[:, n % 2, j, :], qT[rows, s, blk, tok], kT[rows, s, blk, tok],
                                         start=True, stop=True)
                    last.then_inc(scores_done, 1)

                def transposes(b, n):
                    pe.wait_ge(exp_done, NU * b + n + 1)
                    if inside(b, 1, NB) or n >= 2:
                        pe.wait_ge(probT_ready, NU * b + n - 1)
                    for j in range(HB):
                        last = pe.transpose(ps_probT[:, n % 2, j, :], prob[:, n, j, :], ident[:])
                    last.then_inc(probT_done, 1)

                def weighted(b, u, n):
                    g, r = divmod(n, 2)
                    pe.wait_ge(probT_ready, NU * b + n + 1)
                    if n == 0:
                        pe.wait_ge(v_ready, 2 * (b + 1))
                    if inside(b, 1, NB) or n >= 1:
                        pe.wait_ge(attn_ready, NU * b + n)
                    for j in range(HB):
                        head = 2 * (HB * g + j) + r
                        last = pe.matmul(out_heads[:, j, :], probT[:, n, j, :], v_ones[:, u // 2, u % 2, head, :],
                                         start=True, stop=True)
                    last.then_inc(out_done, 1)

                def project(b, u, j, weights, src):
                    for h in range(2):
                        blk = HB * (u % 2) + 2 * j + h
                        for k in range(ND):
                            last = pe.matmul(ps_proj[:, j, h * PT:(h + 1) * PT], weights[:, k, blk * P:(blk + 1) * P],
                                             src[:, k, :], start=(k == 0), stop=(k == ND - 1))
                    last.then_inc(proj_done, 1)

                def queries(b, u, j):
                    if inside(b, *projects):
                        if j == 0 and u % 2 == 0:
                            pe.wait_ge(xnT_ready, b + 4)
                        if inside(b, -1, NB - 3):
                            pe.wait_ge(v_ready, 2 * b + 3 + j)
                        project(b, u, j, wq, xnT[:, 1 - u // 2])

                def keys(b, u, j, i):
                    if inside(b, *projects):
                        if j == 0 and u % 2 == 0:
                            pair_uses = (b // 2 + 1) // 2 + 1 if isinstance(b, int) else i + 1 + u // 2
                            pe.wait_ge(ctx_loaded[1 - u // 2], 16 * pair_uses)
                        pe.wait_ge(qk_ready, 8 * (b + 2) + 2 * (j + 1))
                        project(b, u, j, wk, ctxT[:, 1 - u // 2])

                def values(b, u, j):
                    if inside(b, *projects):
                        pe.wait_ge(qk_ready, 8 * (b + 2) + 4 + 2 * (j + 1))
                        tok = slice((u % 2) * P, (u % 2 + 1) * P)
                        for k in range(ND):
                            last = pe.matmul(ps_proj[:, j, :], ctxT[:, 1 - u // 2, k, tok], wv[:, k, j * BANK:(j + 1) * BANK],
                                             start=(k == 0), stop=(k == ND - 1))
                        last.then_inc(proj_done, 1)

                def bank_after_logits(b):
                    pe.wait_ge(logits_read, b - 3)

                def logits_of(t):
                    pe.wait_ge(zT_ready, t + 1)
                    for k in range(ND):
                        last = pe.matmul(ps_aux[:, 0:NE], zT[:, 0, k, :], wr[:, k, :], start=(k == 0), stop=(k == ND - 1))
                    last.then_inc(logits_done, 1)

                def turn_x(b, u):
                    if inside(b, 4, NB - 5):
                        bank_after_logits(b)
                    elif inside(b, 2, 3):
                        pe.wait_ge(proj_ready, b - 1)
                    elif inside(b, FIRST + 1, 1):
                        pe.wait_ge(xnT_ready, b + 4)
                    pe.wait_ge(xn_ready, b + 5)
                    for k in range(ND):
                        last = pe.transpose(ps_aux[:, k * P:(k + 1) * P], xn[:, u % 2, k * P:(k + 1) * P], ident[:])
                    last.then_inc(xnT_done, 1)

                def turn_attn(b, u, half):
                    t, s = b - 1, (u + 1) % 2
                    if half == 1:
                        pe.wait_ge(attnT_ready, 2 * t + 1)
                    elif inside(b, FIRST, NB - 5):
                        pe.wait_ge(xnT_ready, b + 5)
                    else:
                        bank_after_logits(b)
                    pe.wait_ge(attn_ready, NU * t + 2 * half + 2)
                    for j in range(HB):
                        last = pe.transpose(ps_aux[:, j * P:(j + 1) * P],
                                            attn[:, s, half, j].rearrange("p r w -> p (r w)"), ident[:])
                    last.then_inc(attnT_done, 1)

                def output(b, u):
                    t, s = b - 1, (u + 1) % 2
                    pe.wait_ge(attnT_ready, 2 * t + 2)
                    for blk in range(BLKS):
                        last = pe.matmul(ps_aux[:, 0:D], attnT[:, s, blk, :], wo[:, blk, :],
                                         start=(blk == 0), stop=(blk == BLKS - 1))
                    last.then_inc(output_done, 1)

                def turn_z(b, u):
                    if inside(b, FIRST, NB):
                        pe.wait_ge(proj_ready, b)
                    else:
                        bank_after_logits(b)
                    pe.wait_ge(z_ready, b - 2)
                    for k in range(ND):
                        last = pe.transpose(ps_aux[:, k * P:(k + 1) * P], z[:, (u + 1) % 4, k * P:(k + 1) * P], ident[:])
                    last.then_inc(zT_done, 1)

                def step(b, u, i):
                    for n in range(NU):
                        p, pu, pn = (b, u, n - 1) if n else (b - 1, (u - 1) % 4, NU - 1)
                        if inside(b, 0, NB - 1):
                            scores(b, u, n)
                        if n == 0:
                            queries(b, u, 0)
                        elif n == 1:
                            keys(b, u, 0, i)
                        elif n == 2:
                            values(b, u, 0)
                        else:
                            values(b, u, 1)
                        if inside(p, 0, NB - 1):
                            transposes(p, pn)
                        if n == 0:
                            if inside(b, 4, NB + 3):
                                logits_of(b - 4)
                            queries(b, u, 1)
                        elif n == 1:
                            keys(b, u, 1, i)
                        elif n == 2 and inside(b, 1, NB):
                            turn_attn(b, u, 1)
                        elif n == 3 and inside(b, 1, NB):
                            output(b, u)
                        if inside(p, 0, NB - 1):
                            weighted(p, pu, pn)
                        if n == 0 and inside(b, FIRST, NB - 5):
                            turn_x(b, u)
                        elif n == 1 and inside(b, 1, NB):
                            turn_attn(b, u, 0)
                        elif n == 3 and inside(b, 3, NB + 2):
                            turn_z(b, u)

                pe.wait_ge(w_loaded, 16 * N_W)
                run_steps(pe, step)

            @block.vector
            def _(dve):
                def normalise(t, u, i):
                    s = u % 2
                    dve.wait_ge(early_loaded[u], 16 * uses(t, None if i is None else i))
                    if inside(t, 2, NB - 1):
                        dve.wait_ge(xnT_done, t - 1)
                    dve.tensor_scalar(xn[:, s, :], x2_early[:, u, :], mv2[:, t, 0:1], rstd2[:, bass.ds(t, 1)],
                                      ALU.subtract, ALU.mult).then_inc(xn_ready, 1)

                def softmax_shift(b, n):
                    m = NU * b + n + 1
                    dve.wait_ge(scores_done, m)
                    dve.tensor_reduce(row_max[:, n, :], ps_score[:, n % 2], AX_X, ALU.max).then_inc(max_done, 1)
                    dve.wait_ge(max_done, m)
                    if inside(b, 1, NB):
                        dve.wait_ge(probT_done, m - NU)
                    dve.tensor_tensor(prob[:, n], ps_score[:, n % 2],
                                      row_max[:, n, :].unsqueeze(2).to_broadcast([P, HB, P]),
                                      ALU.subtract).then_inc(shifted, 1)

                def divide(b, u, n):
                    g, r = divmod(n, 2)
                    m = NU * b + n + 1
                    dve.wait_ge(out_done, m)
                    dve.reciprocal(inv_sum[:, n, :].unsqueeze(2), out_heads[:, :, KD:VW]).then_inc(inv_done, 1)
                    dve.wait_ge(inv_done, m)
                    if inside(b, 2, NB):
                        dve.wait_ge(attnT_done, 2 * (b - 1) - 1 + g)
                    dve.tensor_tensor(attn[:, u % 2, g, :, r, :], out_heads[:, :, 0:KD],
                                      inv_sum[:, n, :].unsqueeze(2).to_broadcast([P, HB, KD]),
                                      ALU.mult).then_inc(attn_ready, 1)

                def copy_values(b, u, j):
                    dve.wait_ge(proj_done, 6 * (b + 2) + 5 + j)
                    heads = slice(j * NH // 2, (j + 1) * NH // 2)
                    dve.tensor_tensor(v_ones[:, 1 - u // 2, u % 2, heads, 0:KD],
                                      ps_proj[:, j, :].rearrange("p (h w) -> p h w", w=KD),
                                      bv[:, j * BANK:(j + 1) * BANK].rearrange("p (h w) -> p h w", w=KD),
                                      ALU.add).then_inc(v_ready, 1)

                def route(t):
                    dve.wait_ge(logits_done, t + 1)
                    dve.tensor_tensor(logits[:, t, :], ps_aux[:, 0:NE], br[:], ALU.add).then_inc(logits_read, 1)

                def add_residual(t, s):
                    dve.wait_ge(output_done, t + 1)
                    dve.wait_ge(xn_bo_ready, t + 1)
                    dve.tensor_tensor(proj[:, s, :], ps_aux[:, 0:D], xn_bo[:, s, :], ALU.add).then_inc(proj_ready, 1)
                    dve.wait_ge(proj_ready, t + 1)
                    dve.bn_stats(stats_o[:, s, :], proj[:, s, :]).then_inc(stats_o_done, 1)
                    dve.wait_ge(consts, 3)
                    dve.wait_ge(stats_o_done, t + 1)
                    dve.bn_aggr(mv_o[:, s, :], stats_o[:, s, :]).then_inc(mv_o_done, 1)

                def normalise_output(t, u, i):
                    s = u % 2
                    dve.wait_ge(rstd_o_done, t + 1)
                    dve.tensor_scalar(normed[:, s, :], proj[:, s, :], mv_o[:, s, 0:1], rstd_o[:, s, :],
                                      ALU.subtract, ALU.mult).then_inc(normed_done, 1)
                    dve.wait_ge(normed_done, t + 1)
                    dve.tensor_tensor(scaled[:, s, :], normed[:, s, :], gamma[:], ALU.mult).then_inc(scaled_done, 1)
                    dve.wait_ge(scaled_done, t + 1)
                    dve.wait_ge(x2_beta_ready, t + 1)
                    if inside(t, 4, NB - 1):
                        dve.wait_ge(x3_stored[u], 16 * (uses(t, i) - 1))
                    dve.tensor_tensor(x3[:, u, :], scaled[:, s, :], x2_beta[:, u, :], ALU.add).then_inc(x3_ready, 1)
                    dve.wait_ge(x3_ready, t + 1)
                    dve.bn_stats(stats_3[:, s, :], x3[:, u, :]).then_inc(stats_3_done, 1)
                    dve.wait_ge(consts, 3)
                    dve.wait_ge(stats_3_done, t + 1)
                    dve.bn_aggr(mv_3[:, s, :], stats_3[:, s, :]).then_inc(mv_3_done, 1)

                def normalise_routed(t, u, i):
                    s = u % 2
                    dve.wait_ge(rstd_3_done, t + 1)
                    if inside(t, 4, NB - 1):
                        dve.wait_ge(z_stored[u], 16 * (uses(t, i) - 1))
                    dve.tensor_scalar(z[:, u, :], x3[:, u, :], mv_3[:, s, 0:1], rstd_3[:, s, :],
                                      ALU.subtract, ALU.mult).then_inc(z_ready, 1)

                def step(b, u, i):
                    turn = [None if i is None else (i + 1 if u >= k else i) for k in range(4)]
                    if inside(b, FIRST, NB - 5):
                        normalise(b + 4, u, None if i is None else i + 2)
                    for n in range(NU):
                        p, pu, pn = (b, u, n - 1) if n else (b - 1, (u - 1) % 4, NU - 1)
                        if inside(b, 0, NB - 1):
                            softmax_shift(b, n)
                        if n >= 2 and inside(b, *projects):
                            copy_values(b, u, n - 2)
                        if n == 0:
                            if inside(b, 4, NB + 3):
                                route(b - 4)
                            if inside(b, 2, NB + 1):
                                normalise_output(b - 2, (u + 2) % 4, turn[2])
                        if n == 1 and inside(b, 3, NB + 2):
                            normalise_routed(b - 3, (u + 1) % 4, turn[3])
                        if inside(p, 0, NB - 1):
                            divide(p, pu, pn)
                    if inside(b, 1, NB):
                        add_residual(b - 1, (u + 1) % 2)

                dve.wait_ge(consts, 3)
                dve.wait_ge(bias_loaded, 16 * N_BIAS)
                run_steps(dve, step)

            @block.scalar
            def _(act):
                def exponentials(b, n):
                    act.wait_ge(shifted, NU * b + n + 1)
                    act.activation(prob[:, n], prob[:, n], ACT.Exp, scale=float(KD) ** -0.5).then_inc(exp_done, 1)

                def copy_probT(b, n):
                    m = NU * b + n + 1
                    act.wait_ge(probT_done, m)
                    if inside(b, 1, NB):
                        act.wait_ge(out_done, m - NU)
                    act.activation(probT[:, n], ps_probT[:, n % 2], ACT.Copy).then_inc(probT_ready, 1)

                def copy_projection(b, u, j, dst, bias, n):
                    if inside(b, *projects):
                        act.wait_ge(proj_done, 6 * (b + 2) + n + j + 1)
                        for h in range(2):
                            blk = HB * (u % 2) + 2 * j + h
                            act.activation(dst[:, 1 - u // 2, blk, :], ps_proj[:, j, h * PT:(h + 1) * PT], ACT.Identity,
                                           bias=bias[:, blk:blk + 1]).then_inc(qk_ready, 1)

                def copy_x(b, u):
                    act.wait_ge(xnT_done, b + 5)
                    tok = slice((u % 2) * P, (u % 2 + 1) * P)
                    act.activation(xnT[:, u // 2, :, tok], ps_aux[:, 0:D].rearrange("p (k t) -> p k t", t=P),
                                   ACT.Copy).then_inc(xnT_ready, 1)

                def copy_attn(t, s, half):
                    act.wait_ge(attnT_done, 2 * t + half + 1)
                    act.activation(attnT[:, s, HB * half:HB * (half + 1), :],
                                   ps_aux[:].rearrange("p (k t) -> p k t", t=P), ACT.Copy).then_inc(attnT_ready, 1)

                def copy_z(t):
                    act.wait_ge(zT_done, t + 1)
                    act.activation(zT[:, 0], ps_aux[:, 0:D].rearrange("p (k t) -> p k t", t=P), ACT.Copy).then_inc(zT_ready, 1)

                def step(b, u, i):
                    for n in range(NU):
                        p, pn = (b, n - 1) if n else (b - 1, NU - 1)
                        if inside(b, 0, NB - 1):
                            exponentials(b, n)
                        if n < 2:
                            copy_projection(b, u, 0, (qT, kT)[n], (bq, bk)[n], 2 * n)
                        if inside(p, 0, NB - 1):
                            copy_probT(p, pn)
                        if n < 2:
                            copy_projection(b, u, 1, (qT, kT)[n], (bq, bk)[n], 2 * n)
                        if n == 0 and inside(b, FIRST, NB - 5):
                            copy_x(b, u)
                        elif n in (1, 2) and inside(b, 1, NB):
                            copy_attn(b - 1, (u + 1) % 2, n - 1)
                        elif n == 3 and inside(b, 3, NB + 2):
                            copy_z(b - 3)

                act.wait_ge(bias_loaded, 16 * N_BIAS)
                run_steps(act, step)


FE = 1024
NT = NB + NE - 1
NS = 3
assert NT % NS == 0


def experts(nc, ident, logits, w, z_dram, x3_dram, ids_dram, out):
    FB = FE // P
    TOKENS = NB * P
    with ExitStack() as stack:
        def sb(name, shape, dt=F32):
            return stack.enter_context(nc.sbuf_tensor("d_" + name, shape, dt))

        def psum(name, shape, dt=F32):
            return stack.enter_context(nc.psum_tensor("d_" + name, shape, dt))

        def sem(name):
            return stack.enter_context(nc.semaphore("d_" + name))

        w1 = sb("w1", [P, NE, ND, FE])
        w2 = sb("w2", [P, NE, FB, D])
        b1T = sb("b1T", [P, NE, FB])
        relu_b1 = sb("relu_b1", [P, NE, FB])
        b2 = sb("b2", [P, NE, D])
        idle = sb("idle", [P, NE, D])
        idle_b2 = sb("idle_b2", [P, NE, D])
        idle_sum = sb("idle_sum", [P, D])
        other = sb("other", [P, NE, D])
        before = sb("before", [P, P])
        ones = sb("ones", [P, P])
        reverse = sb("reverse", [P, NE])
        starts = sb("starts", [P, NB])
        tile_no = sb("tile_no", [P, NT])
        iota = sb("iota", [P, NT], I32)
        top = sb("top", [P, NB])
        is_top = sb("is_top", [P, NB, NE])
        first_top = sb("first_top", [P, NB, NE])
        choice = sb("choice", [P, NB])
        onehot = sb("onehot", [P, NB, NE])
        counts = sb("counts", [P, NE, NB])
        running = sb("running", [P, NE, NB])
        fills = sb("fills", [P, NE, NB])
        tiles = sb("tiles", [P, NE])
        tile_end = sb("tile_end", [P, NE])
        base = sb("base", [P, NE])
        offset = sb("offset", [P, NE, NB])
        place = sb("place", [P, NB, NE])
        slot_f = sb("slot_f", [P, NB])
        slot = sb("slot", [P, NB], I32)
        slot_tile = sb("slot_tile", [P, NB], I32)
        slot_row = sb("slot_row", [P, NB], I32)
        slot_at = sb("slot_at", [P, NB], I32)
        token_id = sb("token_id", [P, NB], I32)
        ends_before = sb("ends_before", [P, NT, NE])
        tile_expert_f = sb("tile_expert_f", [P, NT])
        tile_expert = sb("tile_expert", [P, NT], I32)
        ids = sb("ids", [P, NT], I32)
        from_ids = sb("from_ids", [P, NS], I32)
        to_ids = sb("to_ids", [P, NS], I32)
        z = sb("z", [P, NS, D])
        x3 = sb("x3", [P, NS, D])
        zT = sb("zT", [P, NS, ND, P])
        h = sb("h", [P, FE])
        hT = sb("hT", [P, NS, FB, P])
        y = sb("y", [P, NS, D])
        res = sb("res", [P, NS, D])

        ps_h = psum("ps_h", [P, FE])
        ps_hT = psum("ps_hT", [P, FB, P])
        ps_y = psum("ps_y", [P, BANK])
        ps_zT = psum("ps_zT", [P, BANK])
        ps_idle = psum("ps_idle", [P, 2, BANK])

        w2_loaded = sem("w2_loaded")
        w1_loaded = sem("w1_loaded")
        bias_loaded = sem("bias_loaded")
        consts = sem("consts")
        chain = sem("chain")
        onehot_ready = sem("onehot_ready")
        counted = sem("counted")
        ids_blank = sem("ids_blank")
        slots_ready = sem("slots_ready")
        ids_scattered = sem("ids_scattered")
        ids_loaded = sem("ids_loaded")
        tile_expert_ready = sem("tile_expert_ready")
        relu_b1_ready = sem("relu_b1_ready")
        idle_done = sem("idle_done")
        idle_copied = sem("idle_copied")
        z_gathered = [sem(f"z_gathered{s}") for s in range(NS)]
        x3_gathered = [sem(f"x3_gathered{s}") for s in range(NS)]
        z_turned = sem("z_turned")
        from_ready = sem("from_ready")
        to_ready = sem("to_ready")
        zT_ready = sem("zT_ready")
        h_done = sem("h_done")
        h_ready = sem("h_ready")
        h_turned = sem("h_turned")
        hT_ready = sem("hT_ready")
        y_done = sem("y_done")
        y_read = sem("y_read")
        res_ready = sem("res_ready")
        out_stored = [sem(f"out_stored{s}") for s in range(NS)]

        def run_tiles(engine, step, last=NT - 1):
            for j in range(NS):
                step(j, j, 0)
            with engine.Fori(1, NT // NS - 1) as i:
                for s in range(NS):
                    step(NS * i + s, s, i)
            for j in range(NT - NS, last + 1):
                step(j, j % NS, j // NS)

        def expert_of(engine, j):
            return engine.value_load(tile_expert[0:1, bass.ds(j, 1)], min_val=0, max_val=NE - 1)

        with nc.Block() as block:

            @block.sync
            def _(sp):
                for dst, src in ((b1T, w["b1T"]), (b2, w["b2"].partition_broadcast(P))):
                    sp.dma_start(dst[:], src).then_inc(bias_loaded, 16)
                sp.wait_ge(consts, 1)
                sp.dma_start(ids_dram.rearrange("(p j) a -> p (j a)", p=P), ids[:]).then_inc(ids_blank, 16)
                for e in range(NE):
                    sp.dma_start(w2[:, e], w["w2"][e]).then_inc(w2_loaded, 16)
                for e in range(NE):
                    sp.dma_start(w1[:, e], w["w1"][e]).then_inc(w1_loaded, 16)
                sp.wait_ge(ids_scattered, 16 * NB)
                sp.dma_start(ids[:], ids_dram.rearrange("(p j) a -> p (j a)", p=P)).then_inc(ids_loaded, 16)

            @block.gpsimd
            def _(pool):
                pool.memset(ids[:], TOKENS).then_inc(consts, 1)
                pool.memset(ones[:], 1.0).then_inc(consts, 1)
                pool.memset(before[:], 1.0).then_inc(consts, 1)
                pool.memset(z[:], 0.0).then_inc(consts, 1)
                pool.memset(x3[:], 0.0).then_inc(consts, 1)
                pool.iota(token_id[:], pattern=[[P, NB]], base=0, channel_multiplier=1).then_inc(consts, 1)
                pool.iota(iota[:], pattern=[[1, NT]], base=0, channel_multiplier=0).then_inc(consts, 1)
                pool.wait_ge(consts, 7)
                pool.affine_select(out=before[:], in_=before[:], compare_op=ALU.is_gt, fill=0.0, base=0,
                                   pattern=[[1, P]], channel_multiplier=-1).then_inc(consts, 1)
                pool.tensor_copy(tile_no[:], iota[:]).then_inc(consts, 1)
                pool.wait_ge(consts, 9)
                pool.tensor_scalar(starts[:], tile_no[:, 0:NB], float(P), None, ALU.mult).then_inc(consts, 1)
                pool.tensor_scalar(reverse[:], tile_no[:, 0:NE], -1.0, float(NE), ALU.mult, ALU.add).then_inc(consts, 1)

                pool.wait_ge(ids_blank, 16)
                pool.wait_ge(slots_ready, 1)
                for t in range(NB):
                    pool.indirect_dma_start(ids_dram, bass.IndirectOffsetOnAxis(slot_at[:, t:t + 1].bitcast(U32), 0),
                                            token_id[:, t:t + 1], None).then_inc(ids_scattered, 16)
                pool.wait_ge(ids_loaded, 16)
                last_token = pool.to_reg(TOKENS - 1)

                def gather(j, s, i):
                    pool.wait_ge(ids_loaded, 16)
                    if inside(j, NS, NT - 1):
                        pool.wait_ge(z_turned, j - NS + 1)
                        pool.wait_ge(res_ready, j - NS + 1)
                        pool.wait_ge(x3_gathered[s], 16 * i)
                    pool.tensor_copy(from_ids[:, s:s + 1], ids[:, bass.ds(j, 1)]).then_inc(from_ready, 1)
                    turn = j + 1 if isinstance(j, int) else pool.to_reg(j + 1)
                    pool.wait_ge(ids_loaded, 16)
                    pool.wait_ge(from_ready, turn)
                    index = bass.IndirectOffsetOnAxis(from_ids[:, s:s + 1].bitcast(U32), 0)
                    pool.indirect_dma_start(z[:, s, :], None, z_dram, index, bounds_check=last_token, oob_is_err=False)\
                        .then_inc(z_gathered[s], 16)
                    pool.indirect_dma_start(x3[:, s, :], None, x3_dram, index, bounds_check=last_token, oob_is_err=False)\
                        .then_inc(x3_gathered[s], 16)

                def scatter(j, s, i):
                    pool.wait_ge(ids_loaded, 16)
                    if inside(j, NS, NT - 1):
                        pool.wait_ge(out_stored[s], 16 * i)
                    pool.tensor_copy(to_ids[:, s:s + 1], ids[:, bass.ds(j, 1)]).then_inc(to_ready, 1)
                    turn = j + 1 if isinstance(j, int) else pool.to_reg(j + 1)
                    pool.wait_ge(ids_loaded, 16)
                    pool.wait_ge(to_ready, turn)
                    pool.wait_ge(res_ready, turn)
                    index = bass.IndirectOffsetOnAxis(to_ids[:, s:s + 1].bitcast(U32), 0)
                    pool.indirect_dma_start(out, index, res[:, s, :], None, bounds_check=last_token, oob_is_err=False)\
                        .then_inc(out_stored[s], 16)

                for j in range(NS - 1):
                    gather(j, j, 0)

                def step(j, s, i):
                    if inside(j, 0, NT - NS):
                        gather(j + NS - 1, (s + NS - 1) % NS, i if s == 0 else i + 1)
                    scatter(j, s, i)

                run_tiles(pool, step)
                for s in range(NS):
                    pool.wait_ge(out_stored[s], 16 * (NT // NS))

            @block.tensor
            def _(pe):
                pe.wait_ge(consts, 8)
                pe.wait_ge(onehot_ready, 1)
                flat = onehot[:].rearrange("p t e -> p (t e)")
                pe.matmul(ps_h[:, 0:NB * NE], before[:], flat, start=True, stop=True)
                pe.matmul(ps_h[:, BANK:BANK + NB * NE], ones[:], flat, start=True, stop=True).then_inc(counted, 1)
                pe.wait_ge(relu_b1_ready, 1)
                for e in range(NE):
                    pe.wait_ge(w2_loaded, 16 * NE)
                    if e >= 2:
                        pe.wait_ge(idle_copied, e - 1)
                    for f in range(FB):
                        last = pe.matmul(ps_idle[:, e % 2, 0:D], relu_b1[:, e, f:f + 1].to_broadcast([P, P]), w2[:, e, f, :],
                                         start=(f == 0), stop=(f == FB - 1))
                    last.then_inc(idle_done, 1)
                pe.wait_ge(w1_loaded, 16 * NE)
                pe.wait_ge(tile_expert_ready, 1)

                def turn_z(j, s, i):
                    pe.wait_ge(z_gathered[s], 16 * (i + 1))
                    if inside(j, 1, NT - 1):
                        pe.wait_ge(zT_ready, j)
                    for k in range(ND):
                        last = pe.transpose(ps_zT[:, k * P:(k + 1) * P], z[:, s, k * P:(k + 1) * P], ident[:])
                    last.then_inc(z_turned, 1)

                def first_layer(j, s, e):
                    pe.wait_ge(zT_ready, j + 1)
                    if inside(j, 1, NT - 1):
                        pe.wait_ge(h_ready, 2 * j)
                    for c in range(FE // BANK):
                        for k in range(ND):
                            last = pe.matmul(ps_h[:, c * BANK:(c + 1) * BANK], zT[:, s, k, :],
                                             w1[:, e, k, c * BANK:(c + 1) * BANK], start=(k == 0), stop=(k == ND - 1))
                        last.then_inc(h_done, 1)

                def turn_h(j):
                    for c in range(2):
                        pe.wait_ge(h_ready, 2 * j + c + 1)
                        if inside(j, 1, NT - 1):
                            pe.wait_ge(hT_ready, FB * j - FB // 2 * (1 - c))
                        for f in range(c * FB // 2, (c + 1) * FB // 2):
                            last = pe.transpose(ps_hT[:, f, :], h[:, f * P:(f + 1) * P], ident[:])
                        last.then_inc(h_turned, 1)

                def second_layer(j, s, e):
                    pe.wait_ge(hT_ready, FB * (j + 1))
                    if inside(j, 1, NT - 1):
                        pe.wait_ge(y_read, j)
                    for f in range(FB):
                        last = pe.matmul(ps_y[:, 0:D], hT[:, s, f, :], w2[:, e, f, :], start=(f == 0), stop=(f == FB - 1))
                    last.then_inc(y_done, 1)

                def step(j, s, i):
                    if inside(j, 0, NT - 1):
                        first_layer(j, s, expert_of(pe, j))
                    if inside(j, 0, NT - 2):
                        turn_z(j + 1, (s + 1) % NS, i + (s == NS - 1))
                    if inside(j, 1, NT):
                        second_layer(j - 1, (s + NS - 1) % NS, expert_of(pe, j - 1))
                    if inside(j, 0, NT - 1):
                        turn_h(j)

                turn_z(0, 0, 0)
                run_tiles(pe, step, NT)

            @block.vector
            def _(dve):
                done = [0]

                def then(instruction):
                    done[0] += 1
                    instruction.then_inc(chain, 1)
                    dve.wait_ge(chain, done[0])

                def by_tile(t, n=NE):
                    return t.unsqueeze(2).to_broadcast([P, t.shape[1], n])

                def every_tile(t, n):
                    return t.unsqueeze(1).to_broadcast([P, n, t.shape[1]])

                dve.wait_ge(consts, 11)
                then(dve.tensor_reduce(top[:], logits[:], AX_X, ALU.max))
                then(dve.tensor_tensor(is_top[:], logits[:], by_tile(top[:]), ALU.is_equal))
                then(dve.tensor_tensor(first_top[:], is_top[:], every_tile(reverse[:], NB), ALU.mult))
                then(dve.tensor_reduce(choice[:], first_top[:], AX_X, ALU.max))
                dve.tensor_tensor(onehot[:], every_tile(reverse[:], NB), by_tile(choice[:]), ALU.is_equal)\
                   .then_inc(onehot_ready, 1)
                dve.wait_ge(counted, 1)
                then(dve.tensor_copy(counts[:], ps_h[:, BANK:BANK + NB * NE].rearrange("p (t e) -> p e t", e=NE)))
                src, dst = counts, running
                for reach in (1, 2, 4, 8, 16):
                    dve.tensor_copy(dst[:, :, 0:reach], src[:, :, 0:reach]).then_inc(chain, 1)
                    done[0] += 1
                    then(dve.tensor_tensor(dst[:, :, reach:NB], src[:, :, reach:NB], src[:, :, 0:NB - reach], ALU.add))
                    src, dst = dst, offset if dst is running else running
                totals = running[:, :, NB - 1]
                then(dve.tensor_tensor(fills[:], by_tile(totals, NB), every_tile(starts[:], NE), ALU.is_gt))
                then(dve.tensor_reduce(tiles[:], fills[:], AX_X, ALU.add))
                src, dst = tiles, tile_end
                for reach in (1, 2, 4):
                    dve.tensor_copy(dst[:, 0:reach], src[:, 0:reach]).then_inc(chain, 1)
                    done[0] += 1
                    then(dve.tensor_tensor(dst[:, reach:NE], src[:, reach:NE], src[:, 0:NE - reach], ALU.add))
                    src, dst = dst, base if dst is tile_end else tile_end
                then(dve.tensor_tensor(base[:], tile_end[:], tiles[:], ALU.subtract))
                then(dve.tensor_scalar(base[:], base[:], float(P), None, ALU.mult))
                then(dve.tensor_tensor(offset[:], running[:], counts[:], ALU.subtract))
                then(dve.tensor_tensor(offset[:], offset[:], by_tile(base[:], NB), ALU.add))
                then(dve.tensor_tensor(place[:], ps_h[:, 0:NB * NE].rearrange("p (t e) -> p t e", e=NE),
                                       offset[:].rearrange("p e t -> p t e"), ALU.add))
                then(dve.tensor_tensor(place[:], place[:], onehot[:], ALU.mult))
                then(dve.tensor_reduce(slot_f[:], place[:], AX_X, ALU.add))
                then(dve.tensor_copy(slot[:], slot_f[:]))
                then(dve.tensor_scalar(slot_tile[:], slot[:], P.bit_length() - 1, None, ALU.logical_shift_right))
                then(dve.tensor_scalar(slot_row[:], slot[:], P - 1, None, ALU.bitwise_and))
                then(dve.tensor_scalar(slot_at[:], slot_row[:], NT, None, ALU.mult))
                dve.tensor_tensor(slot_at[:], slot_at[:], slot_tile[:], ALU.add).then_inc(slots_ready, 1)
                then(dve.tensor_tensor(ends_before[:], every_tile(tile_end[:], NT), by_tile(tile_no[:]), ALU.is_le))
                then(dve.tensor_reduce(tile_expert_f[:], ends_before[:], AX_X, ALU.add))
                then(dve.tensor_scalar(tile_expert_f[:], tile_expert_f[:], float(NE - 1), None, ALU.min))
                dve.tensor_copy(tile_expert[:], tile_expert_f[:]).then_inc(tile_expert_ready, 1)

                dve.wait_ge(bias_loaded, 32)
                dve.tensor_scalar(relu_b1[:], b1T[:], 0.0, None, ALU.max).then_inc(relu_b1_ready, 1)
                for e in range(NE):
                    dve.wait_ge(idle_done, e + 1)
                    dve.tensor_copy(idle[:, e, :], ps_idle[:, e % 2, 0:D]).then_inc(idle_copied, 1)
                dve.wait_ge(idle_copied, NE)
                then(dve.tensor_tensor(idle_b2[:], idle[:], b2[:], ALU.add))
                then(dve.tensor_reduce(idle_sum[:], idle_b2[:].rearrange("p e d -> p d e"), AX_X, ALU.add))
                then(dve.tensor_tensor(other[:], every_tile(idle_sum[:], NE), idle[:], ALU.subtract))

                def copy_h(j):
                    for c in range(2):
                        dve.wait_ge(h_done, 2 * j + c + 1)
                        if inside(j, 1, NT - 1):
                            dve.wait_ge(h_turned, 2 * j + c - 1)
                        cols = slice(c * BANK, (c + 1) * BANK)
                        dve.tensor_copy(h[:, cols], ps_h[:, cols]).then_inc(h_ready, 1)

                def finish(j, s, i):
                    dve.wait_ge(y_done, j + 1)
                    e = expert_of(dve, j)
                    dve.tensor_tensor(y[:, s, :], ps_y[:, 0:D], other[:, e, :], ALU.add).then_inc(y_read, 1)
                    dve.wait_ge(y_read, j + 1)
                    dve.wait_ge(x3_gathered[s], 16 * (i + 1))
                    if inside(j, NS, NT - 1):
                        dve.wait_ge(out_stored[s], 16 * i)
                    dve.tensor_tensor(res[:, s, :], y[:, s, :], x3[:, s, :], ALU.add).then_inc(res_ready, 1)

                def step(j, s, i):
                    if inside(j, 0, NT - 1):
                        copy_h(j)
                    if inside(j, 1, NT):
                        finish(j - 1, (s + NS - 1) % NS, i if s else i - 1)

                dve.wait_ge(tile_expert_ready, 1)
                run_tiles(dve, step, NT)

            @block.scalar
            def _(act):
                def copy_z(j, s):
                    act.wait_ge(z_turned, j + 1)
                    if inside(j, NS, NT - 1):
                        act.wait_ge(h_done, 2 * (j - NS + 1))
                    act.activation(zT[:, s], ps_zT[:, 0:D].rearrange("p (k t) -> p k t", t=P), ACT.Copy).then_inc(zT_ready, 1)

                def rectify(j, s):
                    e = expert_of(act, j)
                    if inside(j, NS, NT - 1):
                        act.wait_ge(y_done, j - NS + 1)
                    for f in range(FB):
                        if f % (FB // 2) == 0:
                            act.wait_ge(h_turned, 2 * j + f // (FB // 2) + 1)
                        act.activation(hT[:, s, f, :], ps_hT[:, f, :], ACT.Relu, bias=b1T[:, e, f:f + 1]).then_inc(hT_ready, 1)

                def step(j, s, i):
                    if inside(j, 0, NT - 2):
                        copy_z(j + 1, (s + 1) % NS)
                    rectify(j, s)

                act.wait_ge(bias_loaded, 32)
                act.wait_ge(tile_expert_ready, 1)
                copy_z(0, 0)
                run_tiles(act, step)


def cross_attention_network(nc, eye, x, ctx, ctx_blocks, ctx_t, mask_t, w_up, w_gate, w_down, w, experts_w, out):
    x1, x2, x3, z = (nc.dram_tensor(f"{name}_scratch", [NB, P, D], F32).ap() for name in ("x1", "x2", "x3", "z"))
    ids = nc.dram_tensor("ids_scratch", [P * NT, 1], I32).ap()
    with ExitStack() as persistent:
        def sb(stack, name, shape):
            return stack.enter_context(nc.sbuf_tensor(name, shape, F32))

        ident = sb(persistent, "ident", [P, P])
        mv2 = sb(persistent, "mv2", [P, NB, 2])
        rstd2 = sb(persistent, "rstd2", [P, NB])
        logits = sb(persistent, "logits", [P, NB, NE])
        ident_loaded = persistent.enter_context(nc.semaphore("ident_loaded"))
        with nc.Block() as block:
            @block.sync
            def _(sp):
                sp.dma_start(ident[:], eye).then_inc(ident_loaded, 16)
                sp.wait_ge(ident_loaded, 16)

        with ExitStack() as first:
            yT = sb(first, "yT", [P, ND, NB * P])
            ymax = sb(first, "ymax", [P, NB])
            upT = sb(first, "upT", [P, ND, FF])
            gateT = sb(first, "gateT", [P, ND, FF])
            downT = sb(first, "downT", [P, NF, D])
            used = dequantise_weights(nc, ident, [(w_up, upT), (w_gate, gateT), (w_down, downT)])
            used += attention0(nc, ident, yT, ymax, x, ctx, ctx_blocks, mask_t, x1)
            feed_forward0(nc, yT, ymax, upT, gateT, downT, x1, x2, mv2, rstd2)
        with nc.Block() as block:
            @block.gpsimd
            def _(pool):
                for semaphore in used:
                    pool.sem_clear(semaphore)
        attention1(nc, ident, mv2, rstd2, logits, w, ctx_t, x2, x3, z)
        experts(nc, ident, logits, experts_w, z.rearrange("b p d -> (b p) d"), x3.rearrange("b p d -> (b p) d"), ids, out)


def kernel(**inputs):
    import numpy as np
    from concourse import bacc
    from concourse.bass_utils import run_bass_kernel_spmd

    a = {name: np.asarray(value) for name, value in inputs.items()}
    x, ctx, mask = a["x"], a["ctx_1024"], a["mask_BxSxS2_ik1"]

    def attn(name):
        return a["L1_xattn_" + name]

    def expert(name):
        return a["L1_ffn_" + name]

    def by_rows(weights):
        return weights.reshape(-1, P, weights.shape[-1]).transpose(1, 0, 2)

    arrays = {
        "eye": np.eye(P, dtype=np.float32),
        "x": x,
        "ctx": ctx,
        "ctx_blocks": ctx.reshape(NB // 2, 2, P, 2, NH // 2, HD0).transpose(0, 4, 5, 3, 1, 2),
        "ctx_t": ctx.reshape(NB * P, ND, P).transpose(2, 1, 0),
        "mask_t": mask.transpose(2, 0, 1),
        "w_up": a["L0_ffn_w_up"],
        "w_gate": a["L0_ffn_w_gate"],
        "w_down": a["L0_ffn_w_down"],
        "wq": by_rows(attn("Wq")),
        "wk": by_rows(attn("Wk")),
        "wv": by_rows(attn("Wv")),
        "wo": by_rows(attn("Wo")),
        "wr": by_rows(expert("Wr")),
        "bq": attn("bq").reshape(-1, P).T,
        "bk": attn("bk").reshape(-1, P).T,
        "bv": attn("bv"),
        "bo": attn("bo"),
        "gamma": attn("ln_gamma"),
        "beta": attn("ln_beta"),
        "br": expert("br"),
        "w1": expert("W1").reshape(NE, ND, P, FE).transpose(0, 2, 1, 3),
        "w2": expert("W2").reshape(NE, FE // P, P, D).transpose(0, 2, 1, 3),
        "b1T": expert("b1").reshape(NE, FE // P, P).transpose(2, 0, 1),
        "b2": expert("b2"),
    }
    arrays = {f"{name}_in": np.ascontiguousarray(array) for name, array in arrays.items()}

    nc = bacc.Bacc("TRN2", target_bir_lowering=False, num_devices=1)
    d = {name[:-3]: nc.dram_tensor(name, array.shape, mybir.dt.from_np(array.dtype), kind="ExternalInput").ap()
         for name, array in arrays.items()}
    out = nc.dram_tensor("out", [NB * P, D], F32, kind="ExternalOutput").ap()
    attention_w = {name: d[name] for name in ("wq", "wk", "wv", "wo", "wr", "bq", "bk", "bv", "bo", "gamma", "beta", "br")}
    experts_w = {"w1": [d["w1"][e] for e in range(NE)], "w2": [d["w2"][e] for e in range(NE)], "b1T": d["b1T"], "b2": d["b2"]}
    cross_attention_network(nc, d["eye"], d["x"], d["ctx"], d["ctx_blocks"], d["ctx_t"], d["mask_t"],
                            d["w_up"], d["w_gate"], d["w_down"], attention_w, experts_w, out)
    result = run_bass_kernel_spmd(nc, [arrays], core_ids=[0])
    return result.results[0]["out"].reshape(NB, P, D)
```

```python
from contextlib import ExitStack
from itertools import product

import concourse.bass as bass
from concourse import mybir

ALU = mybir.AluOpType
ACT = mybir.ActivationFunctionType
AX_X = mybir.AxisListType.X
F32 = mybir.dt.float32
F32R = mybir.dt.float32r
F16 = mybir.dt.float16
I32 = mybir.dt.int32
I16 = mybir.dt.int16
U16 = mybir.dt.uint16
U32 = mybir.dt.uint32

P = 128
NB = 32
D = 256
ND = D // P
NH = 16
HD0 = D // NH
HB = 4
BANK = 512
EPS = 1e-5
NEG = -10000.0
PARTS = ((0, 0), (0, 1), (1, 0))
UN = 4


def inside(b, first, last):
    return not isinstance(b, int) or first <= b <= last


FF = 768
NF = FF // P
BLOCK = 32
W_MAX = 7.0
A_MAX = 32767.0
TINY = 1e-12
MAGIC = 12582912.0


def weight_quantiser(sem, ident, weights, raw, steps, rounded, deq, scale, inv, ps):
    PER = 4
    GROUPS = FF * D // P // P // PER
    loaded = [sem(f"w_loaded{n}") for n in range(len(weights))]
    chain = sem("w_chain")
    deq_ready = sem("w_deq_ready")
    turned = sem("w_turned")
    copied = sem("w_copied")

    def load(sp, n):
        w = weights[n][0]
        dst = raw[:, n].rearrange("p n k -> p (n k)").rearrange("p (o i) -> p o i", i=w.shape[1])
        sp.dma_start(dst, w.rearrange("(o p) i -> p o i", p=P)).then_inc(loaded[n], 16)

    def quantise(dve):
        done = [0]

        def then(instruction):
            done[0] += 1
            instruction.then_inc(chain, 1)
            dve.wait_ge(chain, done[0])

        for n in range(len(weights)):
            s = n % 2

            def wide(t):
                return t[:, s, :].unsqueeze(2).to_broadcast(list(raw[:, n].shape))

            dve.wait_ge(loaded[n], 16)
            then(dve.tensor_reduce(scale[:, s], raw[:, n], AX_X, ALU.max, apply_absolute_value=True))
            then(dve.tensor_scalar(scale[:, s], scale[:, s], 1.0 / W_MAX, TINY, ALU.mult, ALU.max))
            then(dve.reciprocal(inv[:, s], scale[:, s]))
            then(dve.tensor_tensor(steps[:, s], raw[:, n], wide(inv), ALU.mult))
            then(dve.tensor_scalar(rounded[:, s], steps[:, s], W_MAX, -W_MAX - 1.0, ALU.min, ALU.max))
            if n >= 2:
                dve.wait_ge(turned, GROUPS * (n - 1))
            dve.tensor_tensor(deq[:, s], rounded[:, s], wide(scale), ALU.mult).then_inc(deq_ready, 1)

    def turn(pe):
        for n in range(len(weights)):
            pe.wait_ge(deq_ready, n + 1)
            flat = deq[:, n % 2].rearrange("p n k -> p (n k)")
            for g in range(GROUPS):
                m = GROUPS * n + g
                if m >= 4:
                    pe.wait_ge(copied, m - 3)
                for q in range(PER):
                    c = (PER * g + q) * P
                    last = pe.transpose(ps[:, m % 4, q * P:(q + 1) * P], flat[:, c:c + P], ident[:])
                last.then_inc(turned, 1)
        return lambda: pe.wait_ge(copied, GROUPS * len(weights))

    def copy(act):
        for n, (w, wT) in enumerate(weights):
            ni = w.shape[1] // P
            for g in range(GROUPS):
                m = GROUPS * n + g
                act.wait_ge(turned, m + 1)
                for q in range(PER):
                    o, k = divmod(PER * g + q, ni)
                    last = act.activation(wT[:, k, o * P:(o + 1) * P], ps[:, m % 4, q * P:(q + 1) * P], ACT.Copy)
                last.then_inc(copied, 1)

    return load, quantise, turn, copy


def attention0(nc, ident, weights, yT, ymax, x, ctx, ctx_blocks, mask_t, x1_dram):
    HALF = NH // 2
    VW = 2 * HD0
    used = []
    with ExitStack() as ctx_stack:
        def sb(name, shape, dt=F32):
            return ctx_stack.enter_context(nc.sbuf_tensor("a_" + name, shape, dt))

        def psum(name, shape, dt=F32):
            return ctx_stack.enter_context(nc.psum_tensor("a_" + name, shape, dt))

        def sem(name):
            used.append(ctx_stack.enter_context(nc.semaphore("a_" + name)))
            return used[-1]

        x_sb = sb("x", [P, NB, D])
        v_raw = sb("v_raw", [P, NB, D])
        v_ones = sb("v_ones", [P, 2, NH, VW])
        keys = sb("keys", [P, 2, ND, HALF, 2, P])
        mask_int = sb("mask_int", [P, 8, P], I32)
        mask16 = sb("mask16", [P, NB, P], F16)
        neg_eye = sb("neg_eye", [P, HB, P], F16)
        stats0 = sb("stats0", [P, NB, 6])
        mv0 = sb("mv0", [P, NB, 2])
        var0 = sb("var0", [P, NB])
        power = sb("power", [P, NB])
        rstd0 = sb("rstd0", [P, NB])
        q_in = sb("q_in", [P, 2, D])
        qT = sb("qT", [P, 2, ND, P])
        row_max = sb("row_max", [P, 2, HALF])
        prob = sb("prob", [P, 2, 2, HALF, P])
        probT = sb("probT", [P, 4, HB, P])
        outT = sb("outT", [P, NH // HB, P])
        inv_sum = sb("inv_sum", [P, 2, NH])
        attn = sb("attn", [P, 2, NH, HD0])
        stats1 = sb("stats1", [P, 2, 6])
        mv1 = sb("mv1", [P, 2, 2])
        eps = sb("eps", [P, 1])
        var1 = sb("var1", [P, 2, 1])
        rstd1 = sb("rstd1", [P, 2, 1])
        y = sb("y", [P, 2, D])

        ps_score = psum("ps_score", [P, 2, HALF, P])
        ps_probT = psum("ps_probT", [P, 2, HB, P])
        ps_qy = psum("ps_qy", [P, 2, ND, P])
        ps_out = psum("ps_out", [P, BANK])
        out_heads = ps_out[:].rearrange("p (h w) -> p h w", w=VW)

        x_loaded = [sem(f"x_loaded{c}") for c in range(4)]
        v_loaded = [sem(f"v_loaded{c}") for c in range(4)]
        mask_loaded = sem("mask_loaded")
        keys_loaded = [sem(f"keys_loaded{s}") for s in range(2)]
        x1_stored = sem("x1_stored")
        keys_zero = sem("keys_zero")
        consts = sem("consts")
        mask_ready = sem("mask_ready")
        v_ready = sem("v_ready")
        outT_ready = sem("outT_ready")
        out_turned = sem("out_turned")
        stats0_done = sem("stats0_done")
        mv0_done = sem("mv0_done")
        var0_done = sem("var0_done")
        rstd0_done = sem("rstd0_done")
        q_in_ready = sem("q_in_ready")
        qy_done = sem("qy_done")
        qT_ready = sem("qT_ready")
        yT_ready = sem("yT_ready")
        scores_done = sem("scores_done")
        max_done = sem("max_done")
        shifted = sem("shifted")
        exp_done = sem("exp_done")
        probT_done = sem("probT_done")
        probT_ready = sem("probT_ready")
        out_done = sem("out_done")
        inv_done = sem("inv_done")
        out_read = sem("out_read")
        x1_ready = sem("x1_ready")
        stats1_done = sem("stats1_done")
        mv1_done = sem("mv1_done")
        var1_done = sem("var1_done")
        rstd1_done = sem("rstd1_done")
        y_ready = sem("y_ready")
        y_max_done = sem("y_max_done")

        PAIR_DMAS = HALF
        NQ = NH // HB

        COLS = FF * D // P
        MATS = len(weights)
        spare = yT[:].rearrange("p k t -> p (k t)")
        w_scale = sb("w_scale", [P, 2, COLS // BLOCK])
        w_inv = sb("w_inv", [P, 2, COLS // BLOCK])

        def blocks(flat, n):
            return flat[:, 0:n * COLS].rearrange("p (m n k) -> p m n k", m=n, k=BLOCK)

        load_weights, quantise_weights, turn_weights, copy_weights = weight_quantiser(
            sem, ident, weights,
            raw=blocks(spare, MATS), deq=blocks(spare[:, MATS * COLS:], 2),
            steps=blocks(prob[:].rearrange("p a b h k -> p (a b h k)"), 2),
            rounded=blocks(probT[:].rearrange("p q h k -> p (q h k)").bitcast(I16), 2),
            scale=w_scale, inv=w_inv, ps=ps_score[:].rearrange("p a (b h) k -> p (a b) (h k)", h=HB))

        with nc.Block() as block:

            @block.sync
            def _(sp):
                def load_keys(pair, slot):
                    for j in range(HALF):
                        rows = slice(HD0 * j, HD0 * (j + 1))
                        for_j = keys[rows, slot, :, j, :, :]
                        sp.dma_start(for_j, ctx_blocks[pair, j]).then_inc(keys_loaded[slot], 16)

                def load_x(c):
                    part = slice(8 * c, 8 * (c + 1))
                    sp.dma_start(x_sb[:, part, :], x[part].rearrange("b t d -> t b d")).then_inc(x_loaded[c], 16)

                def load_v(c):
                    part = slice(8 * c, 8 * (c + 1))
                    sp.dma_start(v_raw[:, part, :], ctx[part].rearrange("b t d -> t b d")).then_inc(v_loaded[c], 16)

                def load_mask(c):
                    if c >= 1:
                        sp.wait_ge(mask_ready, c)
                    sp.dma_start(mask_int[:], mask_t[:, 8 * c:8 * (c + 1), :]).then_inc(mask_loaded, 16)

                load_weights(sp, 0)
                load_weights(sp, 1)
                load_x(0)
                load_weights(sp, 2)
                load_mask(0)
                sp.wait_ge(keys_zero, 1)
                load_keys(0, 0)
                load_keys(1, 1)
                load_v(0)
                for c in range(1, 4):
                    load_x(c)
                    load_mask(c)
                for c in range(1, 4):
                    load_v(c)

                def step(b, u, pair):
                    if u % 2 == 1 and inside(b, 0, NB - 5):
                        sp.wait_ge(scores_done, 2 * b + 2)
                        load_keys(pair + 2, u // 2)
                    sp.wait_ge(x1_ready, b + 1)
                    sp.dma_start(x1_dram[b], x_sb[:, b, :]).then_inc(x1_stored, 16)

                with sp.Fori(0, NB // UN - 1) as i:
                    for u in range(UN):
                        step(UN * i + u, u, 2 * i + u // 2)
                for b in range(NB - UN, NB):
                    step(b, b % UN, b // 2)
                sp.wait_ge(x1_stored, 16 * NB)

            @block.gpsimd
            def _(pool):
                def values(b, s):
                    if inside(b, 2, NB - 1):
                        pool.wait_ge(out_done, NQ * (b - 1))
                    src = v_raw[:, b, :].rearrange("p (h w) -> p h w", w=HD0)
                    pool.tensor_copy(v_ones[:, s, :, 0:HD0], src).then_inc(v_ready, 1)

                pool.memset(keys[:], 0.0).then_inc(keys_zero, 1)
                pool.memset(power[:], -0.5).then_inc(consts, 1)
                pool.memset(eps[:], EPS).then_inc(consts, 1)
                pool.memset(v_ones[:], 1.0).then_inc(consts, 1)
                pool.memset(neg_eye[:], 0.0).then_inc(consts, 1)
                pool.wait_ge(consts, 4)
                pool.affine_select(out=neg_eye[:], in_=neg_eye[:], compare_op=ALU.not_equal, fill=NEG, base=0,
                                   pattern=[[0, HB], [-1, P]], channel_multiplier=1).then_inc(consts, 1)
                def eight_sequences(c):
                    part = slice(8 * c, 8 * (c + 1))
                    pool.wait_ge(mv0_done, 8 * (c + 1))
                    pool.tensor_scalar(var0[:, part], mv0[:, part, 1], EPS, None, ALU.add).then_inc(var0_done, 1)
                    pool.wait_ge(var0_done, c + 1)
                    pool.tensor_tensor(rstd0[:, part], var0[:, part], power[:, part], ALU.pow).then_inc(rstd0_done, 1)
                    pool.wait_ge(mask_loaded, 16 * (c + 1))
                    pool.tensor_copy(mask16[:, part, :], mask_int[:]).then_inc(mask_ready, 1)

                def step(b, s):
                    if inside(b, 0, NB - 3):
                        values(b + 2, s)
                    pool.wait_ge(mv1_done, b + 1)
                    pool.tensor_tensor(var1[:, s], mv1[:, s, 1:2], eps[:], ALU.add).then_inc(var1_done, 1)
                    pool.wait_ge(var1_done, b + 1)
                    pool.tensor_tensor(rstd1[:, s], var1[:, s], power[:, 0:1], ALU.pow).then_inc(rstd1_done, 1)

                eight_sequences(0)
                pool.wait_ge(v_loaded[0], 16)
                for b in range(2):
                    values(b, b)
                for b in range(2 * UN):
                    if b < 3:
                        eight_sequences(b + 1)
                    elif b > UN:
                        pool.wait_ge(v_loaded[b - UN], 16)
                    step(b, b % 2)
                with pool.Fori(2, NB // UN - 1) as i:
                    for u in range(UN):
                        step(UN * i + u, u % 2)
                for b in range(NB - UN, NB):
                    step(b, b % 2)

            @block.tensor
            def _(pe):
                def scores(b, u, half):
                    if half == 0:
                        pe.wait_ge(qT_ready, b + 1)
                        if u % 2 == 0:
                            if not isinstance(b, int):
                                pe.wait_ge(mask_ready, 4)
                            turn = 1 + b // UN if isinstance(b, int) else turns[0] + 1
                            pe.wait_ge(keys_loaded[u // 2], 16 * PAIR_DMAS * turn)
                    if inside(b, 1, NB):
                        pe.wait_ge(shifted, 2 * b + half - 1)
                    for q in range(2):
                        heads = slice(HB * q, HB * (q + 1))
                        out = ps_score[:, half, heads, :]
                        pe.matmul(out, qT[:, u % 2, half, :], keys[:, u // 2, half, heads, u % 2, :],
                                  start=True, stop=False)
                        last = pe.matmul(out, mask16[:, b, :], neg_eye[:], start=False, stop=True)
                    last.then_inc(scores_done, 1)

                def transposes(b, s, q):
                    n = NQ * b + q
                    if q % 2 == 0:
                        pe.wait_ge(exp_done, 2 * b + q // 2 + 1)
                    if inside(b, 1, NB) or q >= 2:
                        pe.wait_ge(probT_ready, n - 1)
                    for h in range(HB):
                        last = pe.transpose(ps_probT[:, q % 2, h, :], prob[:, s, q // 2, HB * (q % 2) + h, :], ident[:])
                    last.then_inc(probT_done, 1)

                def weighted(b, u, q):
                    pe.wait_ge(probT_ready, NQ * b + q + 1)
                    if q == 0:
                        pe.wait_ge(v_ready, b + 1)
                        if inside(b, 1, NB):
                            pe.wait_ge(out_read, b)
                    for h in range(HB):
                        last = pe.matmul(ps_out[h * VW:(h + 1) * VW, q * P:(q + 1) * P], v_ones[:, u % 2, HB * q + h, :],
                                         probT[:, q, h, :], start=True, stop=True)
                    last.then_inc(out_done, 1)

                def turn_out(b):
                    pe.wait_ge(outT_ready, b + 1)
                    for q in range(NQ):
                        last = pe.transpose(ps_out[:, q * P:(q + 1) * P], outT[:, q, :], ident[:])
                    last.then_inc(out_turned, 1)

                def turn_qy(g, s):
                    if inside(g, 5, NB + 4):
                        pe.wait_ge(yT_ready, g - 4)
                    elif g >= 1:
                        pe.wait_ge(qT_ready, g)
                    if inside(g, 0, NB - 1):
                        pe.wait_ge(q_in_ready, g + 1)
                        for k in range(ND):
                            last = pe.transpose(ps_qy[:, 0, k, :], q_in[:, s, k * P:(k + 1) * P], ident[:])
                    if inside(g, 4, NB + 3):
                        pe.wait_ge(y_ready, g - 3)
                        for k in range(ND):
                            last = pe.transpose(ps_qy[:, 1, k, :], y[:, s, k * P:(k + 1) * P], ident[:])
                    last.then_inc(qy_done, 1)

                def step(b, u):
                    for half in range(2):
                        if inside(b, 0, NB - 1):
                            scores(b, u, half)
                        if half == 0 and inside(b, 2, NB + 1):
                            turn_out(b - 2)
                        if inside(b, 1, NB):
                            p, pu = b - 1, (u - 1) % UN
                            if half == 0:
                                transposes(p, pu % 2, 0)
                                transposes(p, pu % 2, 1)
                            else:
                                weighted(p, pu, 0)
                                weighted(p, pu, 1)
                                transposes(p, pu % 2, 2)
                                transposes(p, pu % 2, 3)
                                turn_qy(b + 1, (u + 1) % 2)
                                weighted(p, pu, 2)
                                weighted(p, pu, 3)
                    if isinstance(b, int) and (b < 1 or b > NB):
                        turn_qy(b + 1, (u + 1) % 2)

                weights_copied = turn_weights(pe)
                pe.wait_ge(consts, 5)
                turn_qy(0, 0)
                weights_copied()
                pe.wait_ge(mask_ready, 1)
                turns = [0]
                for b in range(UN):
                    step(b, b % UN)
                with pe.Fori(1, NB // UN - 1) as i:
                    turns[0] = i
                    for u in range(UN):
                        step(UN * i + u, u)
                for b in range(NB - UN, NB + 3):
                    step(b, b % UN)

            @block.vector
            def _(dve):
                def queries(b, s):
                    dve.wait_ge(rstd0_done, b // 8 + 1 if isinstance(b, int) else 4)
                    if inside(b, 2, NB - 1):
                        dve.wait_ge(qy_done, b - 1)
                    dve.tensor_scalar(q_in[:, s, :], x_sb[:, b, :], mv0[:, b, 0:1], rstd0[:, bass.ds(b, 1)],
                                      ALU.subtract, ALU.mult).then_inc(q_in_ready, 1)

                def softmax_shift(b, s, half):
                    n = 2 * b + half + 1
                    dve.wait_ge(scores_done, n)
                    dve.tensor_reduce(row_max[:, half, :], ps_score[:, half], AX_X, ALU.max).then_inc(max_done, 1)
                    dve.wait_ge(max_done, n)
                    if inside(b, 2, NB):
                        dve.wait_ge(probT_done, NQ * (b - 2) + 2 * half + 2)
                    dve.tensor_tensor(prob[:, s, half], ps_score[:, half],
                                      row_max[:, half, :].unsqueeze(2).to_broadcast([P, HALF, P]),
                                      ALU.subtract).then_inc(shifted, 1)

                def divide(b, s):
                    dve.wait_ge(out_turned, b + 1)
                    dve.reciprocal(inv_sum[:, s, :].unsqueeze(2), out_heads[:, :, HD0:HD0 + 1]).then_inc(inv_done, 1)
                    dve.wait_ge(inv_done, b + 1)
                    dve.tensor_tensor(attn[:, s], out_heads[:, :, 0:HD0],
                                      inv_sum[:, s, :].unsqueeze(2).to_broadcast([P, NH, HD0]),
                                      ALU.mult).then_inc(out_read, 1)

                def residual(b, s):
                    dve.wait_ge(out_read, b + 1)
                    dve.tensor_tensor(x_sb[:, b, :], x_sb[:, b, :], attn[:, s].rearrange("p h w -> p (h w)"),
                                      ALU.add).then_inc(x1_ready, 1)
                    dve.wait_ge(stats0_done, 8)
                    dve.wait_ge(x1_ready, b + 1)
                    dve.bn_stats(stats1[:, s, :], x_sb[:, b, :]).then_inc(stats1_done, 1)
                    dve.wait_ge(stats0_done, 8)
                    dve.wait_ge(stats1_done, b + 1)
                    dve.bn_aggr(mv1[:, s, :], stats1[:, s, :]).then_inc(mv1_done, 1)

                def normalise(b, s):
                    dve.wait_ge(rstd1_done, b + 1)
                    if inside(b, 2, NB - 1):
                        dve.wait_ge(qy_done, b + 3)
                    dve.tensor_scalar(y[:, s, :], x_sb[:, b, :], mv1[:, s, 0:1], rstd1[:, s, :],
                                      ALU.subtract, ALU.mult).then_inc(y_ready, 1)
                    dve.wait_ge(y_ready, b + 1)
                    dve.tensor_reduce(ymax[:, bass.ds(b, 1)], y[:, s, :], AX_X, ALU.max, apply_absolute_value=True)\
                       .then_inc(y_max_done, 1)

                def step(b, s):
                    if inside(b, 0, NB - 2):
                        queries(b + 1, 1 - s)
                    if inside(b, 2, NB + 1):
                        divide(b - 2, s)
                    if inside(b, 0, NB - 1):
                        softmax_shift(b, s, 0)
                    if inside(b, 2, NB + 1):
                        residual(b - 2, s)
                    if inside(b, 0, NB - 1):
                        softmax_shift(b, s, 1)
                    if inside(b, 2, NB + 1):
                        normalise(b - 2, s)

                def statistics(c):
                    dve.wait_ge(x_loaded[c], 16)
                    for b in range(8 * c, 8 * (c + 1)):
                        dve.bn_stats(stats0[:, b, :], x_sb[:, b, :]).then_inc(stats0_done, 1)
                    dve.wait_ge(stats0_done, 8 * (c + 1))
                    for b in range(8 * c, 8 * (c + 1)):
                        dve.bn_aggr(mv0[:, b, :], stats0[:, b, :]).then_inc(mv0_done, 1)

                quantise_weights(dve)
                statistics(0)
                queries(0, 0)
                for b in range(UN):
                    step(b, b % 2)
                    if b < 3:
                        statistics(b + 1)
                with dve.Fori(1, NB // UN - 1) as i:
                    for u in range(UN):
                        step(UN * i + u, u % 2)
                for b in range(NB - UN, NB + 2):
                    step(b, b % 2)

            @block.scalar
            def _(act):
                def exponentials(b, s, half):
                    act.wait_ge(shifted, 2 * b + half + 1)
                    act.activation(prob[:, s, half], prob[:, s, half], ACT.Exp).then_inc(exp_done, 1)

                def copy_probT(b, q):
                    act.wait_ge(probT_done, NQ * b + q + 1)
                    if inside(b, 1, NB):
                        act.wait_ge(out_done, NQ * b + q - 3)
                    act.activation(probT[:, q], ps_probT[:, q % 2], ACT.Copy).then_inc(probT_ready, 1)

                def copy_qy(g, s):
                    act.wait_ge(qy_done, g + 1)
                    if inside(g, 0, NB - 1):
                        if inside(g, 2, NB - 1):
                            act.wait_ge(scores_done, 2 * g - 2)
                        last = act.activation(qT[:, s], ps_qy[:, 0], ACT.Copy, scale=float(HD0) ** -0.5)
                        last.then_inc(qT_ready, 1)
                    if inside(g, 4, NB + 3):
                        act.activation(yT[:, :, bass.ds((g - 4) * P, P)], ps_qy[:, 1], ACT.Copy).then_inc(yT_ready, 1)

                def copy_out(b):
                    act.wait_ge(out_done, NQ * (b + 1))
                    if inside(b, 1, NB - 1):
                        act.wait_ge(out_turned, b)
                    act.activation(outT[:], ps_out[:].rearrange("p (q k) -> p q k", k=P), ACT.Copy).then_inc(outT_ready, 1)

                def step(b, u):
                    if inside(b, 1, NB):
                        copy_probT(b - 1, 0)
                        copy_probT(b - 1, 1)
                    if inside(b, 0, NB - 1):
                        exponentials(b, u % 2, 0)
                    if inside(b, 1, NB):
                        copy_probT(b - 1, 2)
                        copy_probT(b - 1, 3)
                    copy_qy(b + 1, (u + 1) % 2)
                    if inside(b, 1, NB):
                        copy_out(b - 1)
                    if inside(b, 0, NB - 1):
                        exponentials(b, u % 2, 1)

                copy_weights(act)
                copy_qy(0, 0)
                for b in range(UN):
                    step(b, b % UN)
                with act.Fori(1, NB // UN - 1) as i:
                    for u in range(UN):
                        step(UN * i + u, u)
                for b in range(NB - UN, NB + 3):
                    step(b, b % UN)
    return used


def feed_forward0(nc, yT, ymax, upT, gateT, downT, x1_dram, x2_dram, mv2, rstd2):
    T = NB * P
    CH = BANK
    NC = T // CH
    COLS = NF * T
    UNIT = 2048
    NU = COLS // UNIT
    with ExitStack() as stack:
        def sb(name, shape, dt=F32):
            return stack.enter_context(nc.sbuf_tensor("b_" + name, shape, dt))

        def sem(name):
            return stack.enter_context(nc.semaphore("b_" + name))

        act_sb = sb("act", [P, NF, T])
        up16 = sb("up16", [P, NF, T], I16)
        act_flat = act_sb[:].rearrange("p f t -> p (f t)")
        up_flat = up16[:].rearrange("p f t -> p (f t)")
        spare = yT[:].rearrange("p k t -> p (k t)")
        quant = spare[:, 0:UNIT].bitcast(I16).rearrange("p (s n) -> p s n", s=2)
        sig16 = spare[:, UNIT:2 * UNIT].bitcast(U16).rearrange("p (s n) -> p s n", s=2)
        sig = spare[:, 2 * UNIT:4 * UNIT].rearrange("p (s n) -> p s n", s=2)
        inner = spare[:, 0:2 * NF * CH].rearrange("p (s f t) -> p s f t", s=2, f=NF)

        pmax = sb("pmax", [P, NF * NC])
        one = sb("one", [P, 8, 1])
        factors = sb("factors", [P, 5, 2, 1])
        x1_sb = sb("x1", [P, 4, D])
        x2_sb = sb("x2", [P, 4, D])
        stats2 = sb("stats2", [P, NB, 6])
        var2 = sb("var2", [P, NB])
        power = sb("power", [P, NB])
        ps = stack.enter_context(nc.psum_tensor("b_ps", [P, 8, BANK], F32))

        consts = sem("consts")
        part_max = sem("part_max")
        all_max = sem("all_max")
        scalars = sem("scalars")
        scale_ready = sem("scale_ready")
        y_rounded = sem("y_rounded")
        y_ready = sem("y_ready")
        product_done = sem("product_done")
        copied = sem("copied")
        max_done = sem("max_done")
        up_ready = sem("up_ready")
        gate_quant = sem("gate_quant")
        sig_done = sem("sig_done")
        sig_quant = sem("sig_quant")
        silu_done = sem("silu_done")
        silu_quant = sem("silu_quant")
        inner_done = sem("inner_done")
        inner_rounded = sem("inner_rounded")
        inner_ready = sem("inner_ready")
        down_done = sem("down_done")
        x1_loaded = [sem(f"x1_loaded{s}") for s in range(4)]
        x2_ready = sem("x2_ready")
        x2_stored = [sem(f"x2_stored{s}") for s in range(4)]
        stats_done = sem("stats_done")
        mv_done = sem("mv_done")
        var_done = sem("var_done")
        rstd_done = sem("rstd_done")

        Y, UP, GATE, SILU, INNER = range(5)
        TILES = CH // P

        with nc.Block() as block:

            @block.sync
            def _(sp):
                def step(t, s):
                    if inside(t, 4, NB - 1):
                        sp.wait_ge(x2_ready, t - 3)
                    sp.dma_start(x1_sb[:, s, :], x1_dram[t]).then_inc(x1_loaded[s], 16)
                    if inside(t, 3, NB - 1):
                        store(t - 3, (s + 1) % 4)

                def store(t, s):
                    sp.wait_ge(x2_ready, t + 1)
                    sp.dma_start(x2_dram[t], x2_sb[:, s, :]).then_inc(x2_stored[s], 16)

                for t in range(4):
                    step(t, t)
                with sp.Fori(1, NB // 4) as i:
                    for s in range(4):
                        step(4 * i + s, s)
                for t in range(NB - 3, NB):
                    store(t, t % 4)
                for s in range(4):
                    sp.wait_ge(x2_stored[s], 16 * NB // 4)

            @block.gpsimd
            def _(pool):
                pool.memset(power[:], -0.5).then_inc(consts, 1)
                for n in range(5):
                    pool.wait_ge(part_max, n + 1)
                    pool.partition_all_reduce(one[:, 1, :], one[:, 0, :], P, bass.bass_isa.ReduceOp.max)\
                        .then_inc(all_max, 1)
                pool.wait_ge(consts, 1)
                pool.wait_ge(mv_done, NB)
                pool.tensor_scalar(var2[:], mv2[:, :, 1], EPS, None, ALU.add).then_inc(var_done, 1)
                pool.wait_ge(var_done, 1)
                pool.tensor_tensor(rstd2[:], var2[:], power[:], ALU.pow).then_inc(rstd_done, 1)

            @block.tensor
            def _(pe):
                for m, wT in enumerate((upT, gateT)):
                    def chunk(c):
                        if m == 0:
                            pe.wait_ge(y_ready, c + 1)
                        for f in range(NF):
                            n = NF * (c + NC * m) + f
                            if inside(n, NF, 2 * NC * NF):
                                pe.wait_ge(copied, n - NF + 1)
                            for k in range(ND):
                                last = pe.matmul(ps[:, f, :], wT[:, k, f * P:(f + 1) * P],
                                                 yT[:, k, bass.ds(c * CH, CH)], start=(k == 0), stop=(k == ND - 1))
                            last.then_inc(product_done, 1)

                    chunk(0)
                    with pe.Fori(1, NC) as c:
                        chunk(c)

                def down(c, s):
                    pe.wait_ge(inner_ready, c + 1)
                    for t in range(TILES):
                        n = TILES * c + t
                        if inside(n, 2, NB):
                            pe.wait_ge(x2_ready, n - 1)
                        for f in range(NF):
                            last = pe.matmul(ps[:, 6 + t % 2, 0:D], inner[:, s, f, t * P:(t + 1) * P], downT[:, f, :],
                                             start=(f == 0), stop=(f == NF - 1))
                        last.then_inc(down_done, 1)

                for c in range(2):
                    down(c, c)
                with pe.Fori(1, NC // 2) as i:
                    for s in range(2):
                        down(2 * i + s, s)

            @block.scalar
            def _(act):
                def whole_y(c):
                    act.wait_ge(y_rounded, c + 1)
                    part = yT[:, :, bass.ds(c * CH, CH)]
                    act.activation(part, part, ACT.Copy, bias=-MAGIC).then_inc(y_ready, 1)

                def copy_chunk(c, m):
                    if m == 1:
                        act.wait_ge(up_ready, c + 1)
                    for f in range(NF):
                        act.wait_ge(product_done, NF * (c + NC * m) + f + 1)
                        act.activation(act_sb[:, f, bass.ds(c * CH, CH)], ps[:, f, :], ACT.Copy).then_inc(copied, 1)

                whole_y(0)
                whole_y(1)
                with act.Fori(0, NC - 2) as c:
                    whole_y(c + 2)
                    copy_chunk(c, 0)
                for c in range(NC - 2, NC):
                    copy_chunk(c, 0)
                with act.Fori(0, NC) as c:
                    copy_chunk(c, 1)

                act.wait_ge(scale_ready, GATE + 1)
                with act.Fori(0, NU // 2) as i:
                    for s in range(2):
                        u = 2 * i + s
                        act.wait_ge(gate_quant, u + 1)
                        act.activation(sig[:, s, :], quant[:, s, :], ACT.Sigmoid, scale=factors[:, GATE, 0, :])\
                           .then_inc(sig_done, 1)

                def whole_inner(c, s):
                    act.wait_ge(inner_rounded, c + 1)
                    if inside(c, 2, NC):
                        act.wait_ge(down_done, TILES * (c - 1))
                    act.activation(inner[:, s], act_sb[:, :, bass.ds(c * CH, CH)], ACT.Copy, bias=-MAGIC)\
                       .then_inc(inner_ready, 1)

                for c in range(2):
                    whole_inner(c, c)
                with act.Fori(1, NC // 2) as i:
                    for s in range(2):
                        whole_inner(2 * i + s, s)

            @block.vector
            def _(dve):
                done = [0]

                def then(instruction):
                    done[0] += 1
                    instruction.then_inc(scalars, 1)
                    dve.wait_ge(scalars, done[0])

                def scale_of(n, maxima, unit):
                    dve.tensor_reduce(one[:, 0, :], maxima, AX_X, ALU.max).then_inc(part_max, 1)
                    dve.wait_ge(all_max, n + 1)
                    scale, factor = factors[:, n, 0, :], factors[:, n, 1, :]
                    if unit is None:
                        then(dve.tensor_scalar(scale, one[:, 1, :], 1.0 / A_MAX, TINY, ALU.mult, ALU.max))
                        dve.reciprocal(factor, scale).then_inc(scale_ready, 1)
                    else:
                        then(dve.tensor_scalar(one[:, 2, :], one[:, 1, :], unit, 1.0 / A_MAX, ALU.mult, ALU.mult))
                        then(dve.tensor_scalar(scale, one[:, 2, :], TINY, None, ALU.max))
                        then(dve.reciprocal(one[:, 3, :], scale))
                        dve.tensor_tensor(factor, one[:, 3, :], unit, ALU.mult).then_inc(scale_ready, 1)
                    dve.wait_ge(scale_ready, n + 1)

                def maxima_of_chunk(c, m):
                    for f in range(NF):
                        n = NF * c + f
                        dve.wait_ge(copied, n + NF * NC * m + 1)
                        dve.tensor_reduce(pmax[:, bass.ds(n, 1)], act_sb[:, f, bass.ds(c * CH, CH)], AX_X, ALU.max,
                                          apply_absolute_value=True).then_inc(max_done, 1)

                scale_of(Y, ymax[:], None)
                with dve.Fori(0, NC) as c:
                    part = yT[:, :, bass.ds(c * CH, CH)]
                    dve.tensor_scalar(part, part, factors[:, Y, 1, :], MAGIC, ALU.mult, ALU.add).then_inc(y_rounded, 1)
                with dve.Fori(0, NC) as c:
                    maxima_of_chunk(c, 0)
                dve.wait_ge(max_done, NF * NC)
                scale_of(UP, pmax[:], factors[:, Y, 0, :])
                with dve.Fori(0, NC) as c:
                    part = bass.ds(c * CH, CH)
                    dve.tensor_scalar(up16[:, :, part], act_sb[:, :, part], factors[:, UP, 1, :], None, ALU.mult)\
                       .then_inc(up_ready, 1)
                with dve.Fori(0, NC) as c:
                    maxima_of_chunk(c, 1)
                dve.wait_ge(max_done, 2 * NF * NC)
                scale_of(GATE, pmax[:], factors[:, Y, 0, :])

                def quantise_gate(u, s):
                    if inside(u, 2, NU):
                        dve.wait_ge(silu_done, u - 1)
                    dve.tensor_scalar(quant[:, s, :], act_flat[:, bass.ds(u * UNIT, UNIT)], factors[:, GATE, 1, :], None,
                                      ALU.mult).then_inc(gate_quant, 1)

                def silu(u, s):
                    cols = act_flat[:, bass.ds(u * UNIT, UNIT)]
                    dve.wait_ge(sig_done, u + 1)
                    dve.tensor_scalar(sig16[:, s, :], sig[:, s, :], 65536.0, 65535.0, ALU.mult, ALU.min)\
                       .then_inc(sig_quant, 1)
                    dve.wait_ge(sig_quant, u + 1)
                    dve.tensor_tensor(cols, quant[:, s, :], sig16[:, s, :], ALU.mult).then_inc(silu_done, 1)
                    dve.wait_ge(silu_done, u + 1)
                    dve.tensor_reduce(pmax[:, bass.ds(u, 1)], cols, AX_X, ALU.max, apply_absolute_value=True)\
                       .then_inc(max_done, 1)

                quantise_gate(0, 0)
                quantise_gate(1, 1)
                silu(0, 0)
                quantise_gate(2, 0)
                silu(1, 1)
                with dve.Fori(1, NU // 2 - 1) as i:
                    for s in range(2):
                        quantise_gate(2 * i + s + 1, 1 - s)
                        silu(2 * i + s, s)
                quantise_gate(NU - 1, 1)
                silu(NU - 2, 0)
                silu(NU - 1, 1)
                dve.wait_ge(max_done, 2 * NF * NC + NU)
                then(dve.tensor_scalar(one[:, 4, :], factors[:, GATE, 0, :], 1.0 / 65536.0, None, ALU.mult))
                scale_of(SILU, pmax[:, 0:NU], one[:, 4, :])

                def times_up(u, s):
                    cols = act_flat[:, bass.ds(u * UNIT, UNIT)]
                    dve.tensor_scalar(quant[:, s, :], cols, factors[:, SILU, 1, :], None, ALU.mult).then_inc(silu_quant, 1)
                    dve.wait_ge(silu_quant, u + 1)
                    dve.tensor_tensor(cols, quant[:, s, :], up_flat[:, bass.ds(u * UNIT, UNIT)], ALU.mult)\
                       .then_inc(inner_done, 1)
                    dve.wait_ge(inner_done, u + 1)
                    dve.tensor_reduce(pmax[:, bass.ds(u, 1)], cols, AX_X, ALU.max, apply_absolute_value=True)\
                       .then_inc(max_done, 1)

                with dve.Fori(0, NU // 2) as i:
                    for s in range(2):
                        times_up(2 * i + s, s)
                dve.wait_ge(max_done, 2 * NF * NC + 2 * NU)
                then(dve.tensor_tensor(one[:, 5, :], factors[:, SILU, 0, :], factors[:, UP, 0, :], ALU.mult))
                scale_of(INNER, pmax[:, 0:NU], one[:, 5, :])

                def round_inner(c):
                    part = act_sb[:, :, bass.ds(c * CH, CH)]
                    dve.tensor_scalar(part, part, factors[:, INNER, 1, :], MAGIC, ALU.mult, ALU.add).then_inc(inner_rounded, 1)

                def residual(t, s):
                    dve.wait_ge(down_done, t + 1)
                    dve.wait_ge(x1_loaded[s], 16 * (t // 4 + 1 if isinstance(t, int) else turn[0] + 1))
                    if inside(t, 4, NB - 1):
                        dve.wait_ge(x2_stored[s], 16 * (t // 4 if isinstance(t, int) else turn[0]))
                    dve.scalar_tensor_tensor(x2_sb[:, s, :], ps[:, 6 + s % 2, 0:D], factors[:, INNER, 0, :],
                                             x1_sb[:, s, :], ALU.mult, ALU.add).then_inc(x2_ready, 1)
                    dve.wait_ge(all_max, 1)
                    dve.wait_ge(x2_ready, t + 1)
                    dve.bn_stats(stats2[:, t, :], x2_sb[:, s, :]).then_inc(stats_done, 1)

                turn = [0]
                round_inner(0)
                round_inner(1)
                for t in range(TILES):
                    residual(t, t)
                with dve.Fori(1, NC - 1) as c:
                    turn[0] = c
                    round_inner(c + 1)
                    for s in range(TILES):
                        residual(TILES * c + s, s)
                for t in range(NB - TILES, NB):
                    residual(t, t % 4)
                dve.wait_ge(stats_done, NB)
                for t in range(NB):
                    dve.bn_aggr(mv2[:, t, :], stats2[:, t, :]).then_inc(mv_done, 1)


KD = 64
INNER_C = NH * KD
NE = 8


def attention1(nc, ident, mv2, rstd2, logits, w, ctx_t, x2_dram, x3_dram, z_dram):
    BLKS = INNER_C // P
    PT = 2 * P
    NU = NH // HB
    FIRST, LAST = -4, NB + 3
    with ExitStack() as stack:
        def sb(name, shape, dt=F32):
            return stack.enter_context(nc.sbuf_tensor("c_" + name, shape, dt))

        def psum(name, shape, dt=F32):
            return stack.enter_context(nc.psum_tensor("c_" + name, shape, dt))

        def sem(name):
            return stack.enter_context(nc.semaphore("c_" + name))

        wq = sb("wq", [P, 2, ND, INNER_C], F32R)
        wk = sb("wk", [P, 2, ND, INNER_C], F32R)
        wv = sb("wv", [P, 2, ND, INNER_C], F32R)
        wo = sb("wo", [P, 2, BLKS, D], F32R)
        w_raw = sb("w_raw", [P, 2, ND * INNER_C])
        prob, probT = (w_raw[:, n].rearrange("p (n h k) -> p n h k", n=NU, h=HB) for n in range(2))
        wr = sb("wr", [P, ND, NE])
        bq = sb("bq", [P, BLKS])
        bk = sb("bk", [P, BLKS])
        bv = sb("bv", [P, INNER_C])
        bo = sb("bo", [P, D])
        gamma = sb("gamma", [P, D])
        beta = sb("beta", [P, D])
        br = sb("br", [P, NE])
        power = sb("power", [P, 1])
        ctx_raw = sb("ctx_raw", [P, 2, ND, PT])
        ctxT = sb("ctxT", [P, 2, 2, ND, PT], F32R)
        x2_early = sb("x2_early", [P, 4, D])
        x2_late = sb("x2_late", [P, 4, D])
        xn = sb("xn", [P, 2, D])
        xnT = sb("xnT", [P, 2, 2, ND, PT], F32R)
        qT = sb("qT", [P, 2, BLKS, PT])
        kT = sb("kT", [P, 2, BLKS, PT])
        v = sb("v", [P, 2, 2, NH, KD])
        row_max = sb("row_max", [P, NU, HB])
        shift = sb("shift", [P, NU, HB])
        row_sum = sb("row_sum", [P, NU, HB])
        inv_sum = sb("inv_sum", [P, NU, HB])
        attnT = sb("attnT", [P, 2, 2, BLKS, P], F32R)
        eps = sb("eps", [P, 1])
        xn_bo = sb("xn_bo", [P, 2, D])
        proj = sb("proj", [P, 2, D])
        stats_o = sb("stats_o", [P, 2, 6])
        mv_o = sb("mv_o", [P, 2, 2])
        var_o = sb("var_o", [P, 2, 1])
        rstd_o = sb("rstd_o", [P, 2, 1])
        x3 = sb("x3", [P, 4, D])
        stats_3 = sb("stats_3", [P, 2, 6])
        mv_3 = sb("mv_3", [P, 2, 2])
        var_3 = sb("var_3", [P, 2, 1])
        rstd_3 = sb("rstd_3", [P, 2, 1])
        z = sb("z", [P, 4, D])
        zT = sb("zT", [P, 2, ND, P])

        ps_score = psum("ps_score", [P, 2, HB, P])
        ps_probT = psum("ps_probT", [P, 2, HB, P])
        ps_out = psum("ps_out", [P, HB, P])
        ps_proj = psum("ps_proj", [P, 2, BANK])
        ps_aux = psum("ps_aux", [P, BANK])

        w_loaded = [sem(f"w_loaded{s}") for s in range(2)]
        wr_loaded = sem("wr_loaded")
        w_rounded = sem("w_rounded")
        w_split = sem("w_split")
        ctx_rounded = sem("ctx_rounded")
        ctx_split = sem("ctx_split")
        xnT_rounded = sem("xnT_rounded")
        attnT_rounded = sem("attnT_rounded")
        bias_loaded = sem("bias_loaded")
        ctx_loaded = [sem(f"ctx_loaded{s}") for s in range(2)]
        early_loaded = [sem(f"early_loaded{s}") for s in range(4)]
        late_loaded = [sem(f"late_loaded{s}") for s in range(4)]
        x3_stored = [sem(f"x3_stored{s}") for s in range(4)]
        z_stored = [sem(f"z_stored{s}") for s in range(4)]
        consts = sem("consts")
        xn_ready = sem("xn_ready")
        xnT_done = sem("xnT_done")
        xnT_ready = sem("xnT_ready")
        proj_done = sem("proj_done")
        qk_ready = sem("qk_ready")
        v_ready = sem("v_ready")
        scores_done = sem("scores_done")
        max_done = sem("max_done")
        shift_ready = sem("shift_ready")
        prob_ready = sem("prob_ready")
        exp_done = sem("exp_done")
        probT_done = sem("probT_done")
        probT_ready = sem("probT_ready")
        out_done = sem("out_done")
        inv_done = sem("inv_done")
        attnT_ready = sem("attnT_ready")
        output_done = sem("output_done")
        proj_ready = sem("proj_ready")
        late_centred = sem("late_centred")
        late_norm = sem("late_norm")
        xn_bo_ready = sem("xn_bo_ready")
        x2_beta_ready = sem("x2_beta_ready")
        stats_o_done = sem("stats_o_done")
        mv_o_done = sem("mv_o_done")
        var_o_done = sem("var_o_done")
        rstd_o_done = sem("rstd_o_done")
        normed_done = sem("normed_done")
        scaled_done = sem("scaled_done")
        x3_ready = sem("x3_ready")
        stats_3_done = sem("stats_3_done")
        mv_3_done = sem("mv_3_done")
        var_3_done = sem("var_3_done")
        rstd_3_done = sem("rstd_3_done")
        z_ready = sem("z_ready")
        zT_done = sem("zT_done")
        zT_ready = sem("zT_ready")
        logits_done = sem("logits_done")
        logits_read = sem("logits_read")

        N_BIAS = 7
        projects = (-2, NB - 3)

        def uses(t, turn):
            return t // 4 + 1 if isinstance(t, int) else turn

        def run_steps(engine, step, first=FIRST, last=LAST):
            for b in range(first, 8):
                step(b, b % 4, None)
            with engine.Fori(2, NB // 4 - 1) as i:
                for u in range(4):
                    step(4 * i + u, u, i)
            for b in range(NB - 4, last + 1):
                step(b, b % 4, None)

        with nc.Block() as block:

            @block.sync
            def _(sp):
                def early(t, s):
                    if inside(t, 4, NB - 1):
                        sp.wait_ge(xn_ready, t - 3)
                    sp.dma_start(x2_early[:, s, :], x2_dram[t]).then_inc(early_loaded[s], 16)

                def late(t, s):
                    if inside(t, 4, NB - 1):
                        sp.wait_ge(x3_ready, t - 3)
                    sp.dma_start(x2_late[:, s, :], x2_dram[t]).then_inc(late_loaded[s], 16)

                def context(pair, s):
                    if inside(pair, 2, NB // 2 - 1):
                        sp.wait_ge(ctx_split, pair - 1)
                    sp.dma_start(ctx_raw[:, s], ctx_t[:, :, bass.ds(pair * PT, PT)]).then_inc(ctx_loaded[s], 16)

                def step(b, u, i):
                    if inside(b, FIRST, NB - 5):
                        early(b + 4, u)
                    if inside(b, -2, NB - 3):
                        late(b + 2, (u + 2) % 4)
                    if u % 2 == 0 and inside(b, 0, NB - 5):
                        context(b // 2 + 2 if isinstance(b, int) else 2 * i + u // 2 + 2, (u // 2) % 2)
                    if inside(b, 3, NB + 2):
                        sp.wait_ge(x3_ready, b - 2)
                        sp.dma_start(x3_dram[b - 3], x3[:, (u + 1) % 4, :]).then_inc(x3_stored[(u + 1) % 4], 16)
                    if inside(b, 4, NB + 3):
                        sp.wait_ge(z_ready, b - 3)
                        sp.dma_start(z_dram[b - 4], z[:, u, :]).then_inc(z_stored[u], 16)

                for b in range(FIRST, 0):
                    step(b, b % 4, None)
                def weights(m, name):
                    if m >= 2:
                        sp.wait_ge(w_split, m - 1)
                    sp.dma_start(w_raw[:, m % 2], w[name].rearrange("p k n -> p (k n)")).then_inc(w_loaded[m % 2], 16)

                weights(0, "wq")
                weights(1, "wk")
                for dst, src in ((bq, w["bq"]), (bk, w["bk"])):
                    sp.dma_start(dst[:], src).then_inc(bias_loaded, 16)
                context(0, 0)
                weights(2, "wv")
                for dst, src in ((bv, w["bv"]), (bo, w["bo"]), (gamma, w["gamma"]), (beta, w["beta"]), (br, w["br"])):
                    sp.dma_start(dst[:], src.partition_broadcast(P)).then_inc(bias_loaded, 16)
                context(1, 1)
                sp.dma_start(wr[:], w["wr"]).then_inc(wr_loaded, 16)
                weights(3, "wo")
                run_steps(sp, step, 0)
                for s in range(4):
                    sp.wait_ge(x3_stored[s], 16 * NB // 4)
                    sp.wait_ge(z_stored[s], 16 * NB // 4)

            @block.gpsimd
            def _(pool):
                pool.memset(power[:], -0.5).then_inc(consts, 1)
                pool.memset(eps[:], EPS).then_inc(consts, 1)
                pool.wait_ge(consts, 2)
                pool.wait_ge(bias_loaded, 16 * N_BIAS)

                def residuals(t, u, i):
                    s = u % 2
                    pool.wait_ge(late_loaded[u], 16 * uses(t, None if i is None else i + 1))
                    if inside(t, 2, NB - 1):
                        pool.wait_ge(proj_ready, t - 1)
                    pool.tensor_tensor(xn_bo[:, s, :], x2_late[:, u, :], mv2[:, t, 0:1].to_broadcast([P, D]),
                                       ALU.subtract).then_inc(late_centred, 1)
                    pool.wait_ge(late_centred, t + 1)
                    pool.wait_ge(consts, 2)
                    pool.tensor_tensor(xn_bo[:, s, :], xn_bo[:, s, :], rstd2[:, bass.ds(t, 1)].to_broadcast([P, D]),
                                       ALU.mult).then_inc(late_norm, 1)
                    pool.wait_ge(late_norm, t + 1)
                    pool.tensor_tensor(xn_bo[:, s, :], xn_bo[:, s, :], bo[:], ALU.add).then_inc(xn_bo_ready, 1)
                    pool.tensor_tensor(x2_late[:, u, :], x2_late[:, u, :], beta[:], ALU.add).then_inc(x2_beta_ready, 1)

                def inverse_deviation(t, s, var, mv, rstd, mv_done, var_done, rstd_done):
                    pool.wait_ge(mv_done, t + 1)
                    pool.tensor_tensor(var[:, s], mv[:, s, 1:2], eps[:], ALU.add).then_inc(var_done, 1)
                    pool.wait_ge(var_done, t + 1)
                    pool.tensor_tensor(rstd[:, s], var[:, s], power[:], ALU.pow).then_inc(rstd_done, 1)

                def step(b, u, i):
                    if inside(b, 0, NB - 1):
                        residuals(b, u, i)
                    if inside(b, 2, NB + 1):
                        inverse_deviation(b - 2, u % 2, var_3, mv_3, rstd_3, mv_3_done, var_3_done, rstd_3_done)
                    if inside(b, 1, NB):
                        inverse_deviation(b - 1, (u + 1) % 2, var_o, mv_o, rstd_o, mv_o_done, var_o_done, rstd_o_done)

                run_steps(pool, step, 0, NB + 1)

            @block.tensor
            def _(pe):
                def scores(b, u, n):
                    g, r = divmod(n, 2)
                    s, tok = u // 2, slice((u % 2) * P, (u % 2 + 1) * P)
                    rows = slice(r * KD, (r + 1) * KD)
                    if n == 0 and u % 2 == 0:
                        pe.wait_ge(qk_ready, BLKS * (b + 2))
                    if inside(b, 1, NB) or n >= 2:
                        pe.wait_ge(exp_done, NU * b + n - 1)
                    for j in range(HB):
                        blk = HB * g + j
                        last = pe.matmul(ps_score[:, n % 2, j, :], qT[rows, s, blk, tok], kT[rows, s, blk, tok],
                                         start=True, stop=True)
                    last.then_inc(scores_done, 1)

                def transposes(b, n):
                    pe.wait_ge(prob_ready, NU * b + n + 1)
                    if inside(b, 1, NB) or n >= 2:
                        pe.wait_ge(probT_ready, NU * b + n - 1)
                    for j in range(HB):
                        last = pe.transpose(ps_probT[:, n % 2, j, :], prob[:, n, j, :], ident[:])
                    last.then_inc(probT_done, 1)

                def weighted(b, u, g):
                    pe.wait_ge(probT_ready, NU * b + 2 * g + 2)
                    if g == 0:
                        pe.wait_ge(v_ready, 2 * (b + 1))
                    if inside(b, 1, NB) or g >= 1:
                        pe.wait_ge(attnT_ready, 2 * b + g)
                    for j, r in product(range(HB), range(2)):
                        last = pe.matmul(ps_out[r * KD:(r + 1) * KD, j, :], v[:, u // 2, u % 2, 2 * (HB * g + j) + r, :],
                                         probT[:, 2 * g + r, j, :], start=True, stop=True)
                    last.then_inc(out_done, 1)

                def project(b, u, j, weights, src):
                    for h in range(2):
                        blk = HB * (u % 2) + 2 * j + h
                        for n, (k, (a, c)) in enumerate(product(range(ND), PARTS)):
                            last = pe.matmul(ps_proj[:, j, h * PT:(h + 1) * PT], weights[:, a, k, blk * P:(blk + 1) * P],
                                             src[:, c, k, :], start=(n == 0), stop=(n == ND * len(PARTS) - 1))
                    last.then_inc(proj_done, 1)

                def queries(b, u, j):
                    if inside(b, *projects):
                        if isinstance(b, int) and b == projects[0]:
                            pe.wait_ge(w_split, 1)
                        if j == 0 and u % 2 == 0:
                            pe.wait_ge(xnT_ready, b + 4)
                        if inside(b, -1, NB - 3):
                            pe.wait_ge(v_ready, 2 * b + 3 + j)
                        project(b, u, j, wq, xnT[:, 1 - u // 2])

                def keys(b, u, j, i):
                    if inside(b, *projects):
                        if j == 0 and u % 2 == 0:
                            pe.wait_ge(ctx_split, b // 2 + 2 if isinstance(b, int) else 2 * i + u // 2 + 2)
                        if isinstance(b, int) and b == projects[0]:
                            pe.wait_ge(w_split, 2)
                        pe.wait_ge(qk_ready, 8 * (b + 2) + 2 * (j + 1))
                        project(b, u, j, wk, ctxT[:, 1 - u // 2])

                def values(b, u, j):
                    if inside(b, *projects):
                        pe.wait_ge(qk_ready, 8 * (b + 2) + 4 + 2 * (j + 1))
                        tok = slice((u % 2) * P, (u % 2 + 1) * P)
                        if isinstance(b, int) and b == projects[0]:
                            pe.wait_ge(w_split, 3)
                        for n, (k, (a, c)) in enumerate(product(range(ND), PARTS)):
                            last = pe.matmul(ps_proj[:, j, :], ctxT[:, 1 - u // 2, a, k, tok],
                                             wv[:, c, k, j * BANK:(j + 1) * BANK],
                                             start=(n == 0), stop=(n == ND * len(PARTS) - 1))
                        last.then_inc(proj_done, 1)

                def bank_after_logits(b):
                    pe.wait_ge(logits_read, b - 3)

                def logits_of(t):
                    pe.wait_ge(zT_ready, t + 1)
                    for k in range(ND):
                        last = pe.matmul(ps_aux[:, 0:NE], zT[:, 0, k, :], wr[:, k, :], start=(k == 0), stop=(k == ND - 1))
                    last.then_inc(logits_done, 1)

                def turn_x(b, u):
                    if inside(b, 4, NB - 5):
                        bank_after_logits(b)
                    elif inside(b, 2, 3):
                        pe.wait_ge(proj_ready, b - 1)
                    elif inside(b, FIRST + 1, 1):
                        pe.wait_ge(xnT_ready, b + 4)
                    pe.wait_ge(xn_ready, b + 5)
                    for k in range(ND):
                        last = pe.transpose(ps_aux[:, k * P:(k + 1) * P], xn[:, u % 2, k * P:(k + 1) * P], ident[:])
                    last.then_inc(xnT_done, 1)

                def output(b, u):
                    t, s = b - 1, (u + 1) % 2
                    if inside(b, FIRST, NB - 5):
                        pe.wait_ge(xnT_ready, b + 5)
                    else:
                        bank_after_logits(b)
                    pe.wait_ge(attnT_ready, 2 * t + 2)
                    if isinstance(b, int) and b == 1:
                        pe.wait_ge(w_split, 4)
                    for n, (blk, (a, c)) in enumerate(product(range(BLKS), PARTS)):
                        last = pe.matmul(ps_aux[:, 0:D], attnT[:, s, a, blk, :], wo[:, c, blk, :],
                                         start=(n == 0), stop=(n == BLKS * len(PARTS) - 1))
                    last.then_inc(output_done, 1)

                def turn_z(b, u):
                    pe.wait_ge(proj_ready, min(b - 1, NB) if isinstance(b, int) else b - 1)
                    if not inside(b, FIRST, NB + 1):
                        bank_after_logits(b - 1)
                    pe.wait_ge(z_ready, b - 3)
                    for k in range(ND):
                        last = pe.transpose(ps_aux[:, k * P:(k + 1) * P], z[:, u, k * P:(k + 1) * P], ident[:])
                    last.then_inc(zT_done, 1)

                def step(b, u, i):
                    for n in range(NU):
                        p, pu, pn = (b, u, n - 1) if n else (b - 1, (u - 1) % 4, NU - 1)
                        if inside(b, 0, NB - 1):
                            scores(b, u, n)
                        if n == 0:
                            queries(b, u, 0)
                            if inside(b, 4, NB + 3):
                                turn_z(b, u)
                        elif n == 1:
                            keys(b, u, 0, i)
                        elif n == 3:
                            values(b, u, 1)
                        if inside(p, 0, NB - 1):
                            transposes(p, pn)
                        if n == 0:
                            queries(b, u, 1)
                            if inside(b, 4, NB + 3):
                                logits_of(b - 4)
                        elif n == 1:
                            keys(b, u, 1, i)
                        elif n == 2:
                            values(b, u, 0)
                        elif inside(b, 1, NB):
                            output(b, u)
                        if n == 0 and inside(b, 1, NB):
                            weighted(b - 1, (u - 1) % 4, 1)
                        elif n == 2 and inside(b, 0, NB - 1):
                            weighted(b, u, 0)
                        if n == 0 and inside(b, FIRST, NB - 5):
                            turn_x(b, u)

                pe.wait_ge(wr_loaded, 16)
                run_steps(pe, step)

            @block.vector
            def _(dve):
                def normalise(t, u, i):
                    s = u % 2
                    dve.wait_ge(early_loaded[u], 16 * uses(t, None if i is None else i))
                    if inside(t, 2, NB - 1):
                        dve.wait_ge(xnT_done, t - 1)
                    dve.tensor_scalar(xn[:, s, :], x2_early[:, u, :], mv2[:, t, 0:1], rstd2[:, bass.ds(t, 1)],
                                      ALU.subtract, ALU.mult).then_inc(xn_ready, 1)

                def maxima(b, n):
                    m = NU * b + n + 1
                    dve.wait_ge(scores_done, m)
                    dve.tensor_reduce(row_max[:, n, :], ps_score[:, n % 2], AX_X, ALU.max).then_inc(max_done, 1)
                    dve.wait_ge(max_done, m)
                    dve.tensor_scalar(shift[:, n, :], row_max[:, n, :], -float(KD) ** -0.5, None, ALU.mult)\
                       .then_inc(shift_ready, 1)

                def divide(b, n):
                    m = NU * b + n + 1
                    dve.wait_ge(exp_done, m)
                    dve.reciprocal(inv_sum[:, n, :], row_sum[:, n, :]).then_inc(inv_done, 1)
                    dve.wait_ge(inv_done, m)
                    dve.tensor_tensor(prob[:, n], prob[:, n], inv_sum[:, n, :].unsqueeze(2).to_broadcast([P, HB, P]),
                                      ALU.mult).then_inc(prob_ready, 1)

                def copy_values(b, u, j):
                    dve.wait_ge(proj_done, 6 * (b + 2) + 5 + j)
                    heads = slice(j * NH // 2, (j + 1) * NH // 2)
                    dve.tensor_tensor(v[:, 1 - u // 2, u % 2, heads, :],
                                      ps_proj[:, j, :].rearrange("p (h w) -> p h w", w=KD),
                                      bv[:, j * BANK:(j + 1) * BANK].rearrange("p (h w) -> p h w", w=KD),
                                      ALU.add).then_inc(v_ready, 1)

                def split_x(b, u):
                    dve.wait_ge(xnT_rounded, b + 5)
                    tok = slice((u % 2) * P, (u % 2 + 1) * P)
                    dve.tensor_tensor(xnT[:, u // 2, 1, :, tok], ps_aux[:, 0:D].rearrange("p (k t) -> p k t", t=P),
                                      xnT[:, u // 2, 0, :, tok], ALU.subtract).then_inc(xnT_ready, 1)

                def split_context(b, u):
                    s = (b + 3) // 2 % 2 if isinstance(b, int) else u // 2
                    dve.wait_ge(ctx_rounded, (b + 3) // 2 + 1 if isinstance(b, int) else 2 * turn_of_loop[0] + u // 2 + 3)
                    dve.tensor_tensor(ctxT[:, s, 1], ctx_raw[:, s], ctxT[:, s, 0], ALU.subtract).then_inc(ctx_split, 1)

                def split_attn(t, s, half):
                    dve.wait_ge(attnT_rounded, 2 * t + half + 1)
                    blks = slice(HB * half, HB * (half + 1))
                    dve.tensor_tensor(attnT[:, s, 1, blks, :], ps_out[:],
                                      attnT[:, s, 0, blks, :], ALU.subtract).then_inc(attnT_ready, 1)

                turn_of_loop = [None]

                def route(t):
                    dve.wait_ge(logits_done, t + 1)
                    dve.tensor_tensor(logits[:, t, :], ps_aux[:, 0:NE], br[:], ALU.add).then_inc(logits_read, 1)

                def add_residual(t, s):
                    dve.wait_ge(output_done, t + 1)
                    dve.wait_ge(xn_bo_ready, t + 1)
                    dve.tensor_tensor(proj[:, s, :], ps_aux[:, 0:D], xn_bo[:, s, :], ALU.add).then_inc(proj_ready, 1)

                def output_statistics(t, s):
                    dve.wait_ge(proj_ready, t + 1)
                    dve.bn_stats(stats_o[:, s, :], proj[:, s, :]).then_inc(stats_o_done, 1)
                    dve.wait_ge(consts, 2)
                    dve.wait_ge(stats_o_done, t + 1)
                    dve.bn_aggr(mv_o[:, s, :], stats_o[:, s, :]).then_inc(mv_o_done, 1)

                def normalise_output(t, u, i):
                    s = u % 2
                    dve.wait_ge(rstd_o_done, t + 1)
                    dve.tensor_scalar(proj[:, s, :], proj[:, s, :], mv_o[:, s, 0:1], rstd_o[:, s, :],
                                      ALU.subtract, ALU.mult).then_inc(normed_done, 1)
                    dve.wait_ge(normed_done, t + 1)
                    dve.tensor_tensor(proj[:, s, :], proj[:, s, :], gamma[:], ALU.mult).then_inc(scaled_done, 1)
                    dve.wait_ge(scaled_done, t + 1)
                    dve.wait_ge(x2_beta_ready, t + 1)
                    if inside(t, 4, NB - 1):
                        dve.wait_ge(x3_stored[u], 16 * (uses(t, i) - 1))
                    dve.tensor_tensor(x3[:, u, :], proj[:, s, :], x2_late[:, u, :], ALU.add).then_inc(x3_ready, 1)
                    dve.wait_ge(x3_ready, t + 1)
                    dve.bn_stats(stats_3[:, s, :], x3[:, u, :]).then_inc(stats_3_done, 1)
                    dve.wait_ge(consts, 2)
                    dve.wait_ge(stats_3_done, t + 1)
                    dve.bn_aggr(mv_3[:, s, :], stats_3[:, s, :]).then_inc(mv_3_done, 1)

                def normalise_routed(t, u, i):
                    s = u % 2
                    dve.wait_ge(rstd_3_done, t + 1)
                    if inside(t, 4, NB - 1):
                        dve.wait_ge(z_stored[u], 16 * (uses(t, i) - 1))
                    dve.tensor_scalar(z[:, u, :], x3[:, u, :], mv_3[:, s, 0:1], rstd_3[:, s, :],
                                      ALU.subtract, ALU.mult).then_inc(z_ready, 1)

                def step(b, u, i):
                    turn = [None if i is None else (i + 1 if u >= k else i) for k in range(4)]
                    turn_of_loop[0] = i
                    if inside(b, FIRST, NB - 5):
                        normalise(b + 4, u, None if i is None else i + 2)
                    for n in range(NU):
                        if n == 1 and inside(b, FIRST, NB - 5):
                            split_x(b, u)
                        if inside(b, 0, NB - 1):
                            maxima(b, n)
                        if n == 0:
                            if inside(b, 2, NB + 1):
                                normalise_output(b - 2, (u + 2) % 4, turn[2])
                            if inside(b, 4, NB + 3):
                                route(b - 4)
                        elif n == 2:
                            if inside(b, *projects):
                                copy_values(b, u, 0)
                        elif n == 3:
                            if inside(b, 0, NB - 1):
                                split_attn(b, u % 2, 0)
                            if inside(b, *projects):
                                copy_values(b, u, 1)
                            if u % 2 == 1 and inside(b, -3, NB - 5):
                                split_context(b, u)
                        if inside(b, 0, NB - 1):
                            divide(b, n)
                        if n == 1 and inside(b, 1, NB):
                            split_attn(b - 1, (u + 1) % 2, 1)
                        if n == 1 and inside(b, 3, NB + 2):
                            normalise_routed(b - 3, (u + 1) % 4, turn[3])
                        elif n == 3 and inside(b, 1, NB):
                            add_residual(b - 1, (u + 1) % 2)
                    if inside(b, 1, NB):
                        output_statistics(b - 1, (u + 1) % 2)

                for m, dst in enumerate((wq, wk, wv, wo)):
                    dve.wait_ge(w_rounded, m + 1)
                    high, low = (dst[:, n].rearrange("p k n -> p (k n)") for n in range(2))
                    dve.tensor_tensor(low, w_raw[:, m % 2], high, ALU.subtract).then_inc(w_split, 1)
                dve.wait_ge(bias_loaded, 16 * N_BIAS)
                run_steps(dve, step)

            @block.scalar
            def _(act):
                def exponentials(b, n):
                    m = NU * b + n + 1
                    act.wait_ge(shift_ready, m)
                    if inside(b, 1, NB):
                        act.wait_ge(probT_done, m - NU)
                    for j in range(HB):
                        last = act.activation(prob[:, n, j, :], ps_score[:, n % 2, j, :], ACT.Exp, scale=float(KD) ** -0.5,
                                              bias=shift[:, n, j:j + 1], accum_out=row_sum[:, n, j:j + 1])
                    last.then_inc(exp_done, 1)

                def copy_probT(b, n):
                    m = NU * b + n + 1
                    act.wait_ge(probT_done, m)
                    if inside(b, 1, NB):
                        act.wait_ge(out_done, 2 * b + n // 2 - 1)
                    act.activation(probT[:, n], ps_probT[:, n % 2], ACT.Copy).then_inc(probT_ready, 1)

                def copy_projection(b, u, j, dst, bias, n):
                    if inside(b, *projects):
                        act.wait_ge(proj_done, 6 * (b + 2) + n + j + 1)
                        for h in range(2):
                            blk = HB * (u % 2) + 2 * j + h
                            act.activation(dst[:, 1 - u // 2, blk, :], ps_proj[:, j, h * PT:(h + 1) * PT], ACT.Identity,
                                           bias=bias[:, blk:blk + 1]).then_inc(qk_ready, 1)

                def copy_x(b, u):
                    act.wait_ge(xnT_done, b + 5)
                    tok = slice((u % 2) * P, (u % 2 + 1) * P)
                    if inside(b, 0, NB - 5):
                        act.wait_ge(proj_done, 6 * b)
                    act.activation(xnT[:, u // 2, 0, :, tok], ps_aux[:, 0:D].rearrange("p (k t) -> p k t", t=P),
                                   ACT.Copy).then_inc(xnT_rounded, 1)

                def round_context(b, u, i):
                    if isinstance(b, int):
                        s, uses = (b + 3) // 2 % 2, (b + 3) // 4 + 1
                    else:
                        s, uses = u // 2, i + 2
                    act.wait_ge(ctx_loaded[s], 16 * uses)
                    if inside(b, 1, NB - 5):
                        act.wait_ge(proj_done, 6 * (b + 1))
                    act.activation(ctxT[:, s, 0], ctx_raw[:, s], ACT.Copy).then_inc(ctx_rounded, 1)

                def copy_attn(t, s, half):
                    act.wait_ge(out_done, 2 * t + half + 1)
                    if inside(t, 2, NB - 1):
                        act.wait_ge(output_done, t - 1)
                    act.activation(attnT[:, s, 0, HB * half:HB * (half + 1), :],
                                   ps_out[:], ACT.Copy).then_inc(attnT_rounded, 1)

                def copy_z(t):
                    act.wait_ge(zT_done, t + 1)
                    act.activation(zT[:, 0], ps_aux[:, 0:D].rearrange("p (k t) -> p k t", t=P), ACT.Copy).then_inc(zT_ready, 1)

                def step(b, u, i):
                    for n in range(NU):
                        p, pn = (b, n - 1) if n else (b - 1, NU - 1)
                        if n == 0:
                            copy_projection(b, u, 0, qT, bq, 0)
                            if inside(b, 4, NB + 3):
                                copy_z(b - 4)
                        elif n == 3 and inside(b, 0, NB - 1):
                            copy_attn(b, u % 2, 0)
                        if n % 2 == 0 and inside(p, 0, NB - 1):
                            copy_probT(p, pn)
                        if inside(b, 0, NB - 1):
                            exponentials(b, n)
                        if n == 0:
                            copy_projection(b, u, 1, qT, bq, 0)
                            if inside(b, FIRST, NB - 5):
                                copy_x(b, u)
                        elif n == 1:
                            copy_projection(b, u, 0, kT, bk, 2)
                        if n % 2 == 1 and inside(p, 0, NB - 1):
                            copy_probT(p, pn)
                        if n == 1:
                            if inside(b, 1, NB):
                                copy_attn(b - 1, (u + 1) % 2, 1)
                            copy_projection(b, u, 1, kT, bk, 2)
                        if n == 2 and u % 2 == 1 and inside(b, -3, NB - 5):
                            round_context(b, u, i)

                for m, dst in enumerate((wq, wk, wv, wo)):
                    act.wait_ge(w_loaded[m % 2], 16 * (m // 2 + 1))
                    act.activation(dst[:, 0].rearrange("p k n -> p (k n)"), w_raw[:, m % 2], ACT.Copy).then_inc(w_rounded, 1)
                act.wait_ge(bias_loaded, 16 * N_BIAS)
                run_steps(act, step)


FE = 1024
NT = NB + NE - 1
NS = 3
assert NT % NS == 0


def experts(nc, ident, logits, w, z_dram, x3_dram, ids_dram, out):
    FB = FE // P
    TOKENS = NB * P
    with ExitStack() as stack:
        def sb(name, shape, dt=F32):
            return stack.enter_context(nc.sbuf_tensor("d_" + name, shape, dt))

        def psum(name, shape, dt=F32):
            return stack.enter_context(nc.psum_tensor("d_" + name, shape, dt))

        def sem(name):
            return stack.enter_context(nc.semaphore("d_" + name))

        w1 = sb("w1", [P, NE, ND, FE])
        w2 = sb("w2", [P, NE, FB, D])
        b1T = sb("b1T", [P, NE, FB])
        relu_b1 = sb("relu_b1", [P, NE, FB])
        b2 = sb("b2", [P, NE, D])
        idle = sb("idle", [P, NE, D])
        idle_b2 = sb("idle_b2", [P, NE, D])
        idle_sum = sb("idle_sum", [P, D])
        other = sb("other", [P, NE, D])
        before = sb("before", [P, P])
        ones = sb("ones", [P, P])
        reverse = sb("reverse", [P, NE])
        starts = sb("starts", [P, NB])
        tile_no = sb("tile_no", [P, NT])
        iota = sb("iota", [P, NT], I32)
        top = sb("top", [P, NB])
        is_top = sb("is_top", [P, NB, NE])
        first_top = sb("first_top", [P, NB, NE])
        choice = sb("choice", [P, NB])
        onehot = sb("onehot", [P, NB, NE])
        counts = sb("counts", [P, NE, NB])
        running = sb("running", [P, NE, NB])
        fills = sb("fills", [P, NE, NB])
        tiles = sb("tiles", [P, NE])
        tile_end = sb("tile_end", [P, NE])
        base = sb("base", [P, NE])
        offset = sb("offset", [P, NE, NB])
        place = sb("place", [P, NB, NE])
        slot_f = sb("slot_f", [P, NB])
        slot = sb("slot", [P, NB], I32)
        slot_tile = sb("slot_tile", [P, NB], I32)
        slot_row = sb("slot_row", [P, NB], I32)
        slot_at = sb("slot_at", [P, NB], I32)
        token_id = sb("token_id", [P, NB], I32)
        ends_before = sb("ends_before", [P, NT, NE])
        tile_expert_f = sb("tile_expert_f", [P, NT])
        tile_expert = sb("tile_expert", [P, NT], I32)
        ids = sb("ids", [P, NT], I32)
        z_ids = sb("z_ids", [P, NS], I32)
        x3_ids = sb("x3_ids", [P, NS], I32)
        out_ids = sb("out_ids", [P, NS], I32)
        z = sb("z", [P, NS, D])
        x3 = sb("x3", [P, NS, D])
        zT = sb("zT", [P, NS, ND, P])
        h = sb("h", [P, FE])
        hT = sb("hT", [P, NS, FB, P])
        y = sb("y", [P, NS, D])
        res = sb("res", [P, NS, D])

        ps_h = psum("ps_h", [P, FE])
        ps_hT = psum("ps_hT", [P, FB, P])
        ps_y = psum("ps_y", [P, BANK])
        ps_zT = psum("ps_zT", [P, BANK])
        ps_idle = psum("ps_idle", [P, 2, BANK])

        w2_loaded = sem("w2_loaded")
        w1_loaded = sem("w1_loaded")
        bias_loaded = sem("bias_loaded")
        consts = sem("consts")
        chain = sem("chain")
        onehot_ready = sem("onehot_ready")
        counted = sem("counted")
        ids_blank = sem("ids_blank")
        slots_ready = sem("slots_ready")
        ids_scattered = sem("ids_scattered")
        ids_loaded = sem("ids_loaded")
        tile_expert_ready = sem("tile_expert_ready")
        relu_b1_ready = sem("relu_b1_ready")
        idle_done = sem("idle_done")
        idle_copied = sem("idle_copied")
        z_gathered = [sem(f"z_gathered{s}") for s in range(NS)]
        x3_gathered = [sem(f"x3_gathered{s}") for s in range(NS)]
        z_turned = sem("z_turned")
        z_ids_ready = sem("z_ids_ready")
        x3_ids_ready = sem("x3_ids_ready")
        out_ids_ready = sem("out_ids_ready")
        zT_ready = sem("zT_ready")
        h_done = sem("h_done")
        h_ready = sem("h_ready")
        h_turned = sem("h_turned")
        hT_ready = sem("hT_ready")
        y_done = sem("y_done")
        y_read = sem("y_read")
        res_ready = sem("res_ready")
        out_stored = [sem(f"out_stored{s}") for s in range(NS)]

        def run_tiles(engine, step, last=NT - 1):
            for j in range(2 * NS):
                step(j, j % NS, j // NS)
            with engine.Fori(2, NT // NS - 1) as i:
                for s in range(NS):
                    step(NS * i + s, s, i)
            for j in range(NT - NS, last + 1):
                step(j, j % NS, j // NS)

        def expert_of(engine, j):
            return engine.value_load(tile_expert[0:1, bass.ds(j, 1)], min_val=0, max_val=NE - 1)

        with nc.Block() as block:

            @block.sync
            def _(sp):
                for dst, src in ((b1T, w["b1T"]), (b2, w["b2"].partition_broadcast(P))):
                    sp.dma_start(dst[:], src).then_inc(bias_loaded, 16)
                sp.wait_ge(consts, 1)
                sp.dma_start(ids_dram.rearrange("(p j) a -> p (j a)", p=P), ids[:]).then_inc(ids_blank, 16)
                for e in range(NE):
                    sp.dma_start(w2[:, e], w["w2"][e]).then_inc(w2_loaded, 16)
                for e in range(NE):
                    sp.dma_start(w1[:, e], w["w1"][e]).then_inc(w1_loaded, 16)
                sp.wait_ge(ids_scattered, 16 * NB)
                sp.dma_start(ids[:], ids_dram.rearrange("(p j) a -> p (j a)", p=P)).then_inc(ids_loaded, 16)

            @block.gpsimd
            def _(pool):
                pool.memset(ids[:], TOKENS).then_inc(consts, 1)
                pool.memset(ones[:], 1.0).then_inc(consts, 1)
                pool.memset(before[:], 1.0).then_inc(consts, 1)
                pool.memset(z[:], 0.0).then_inc(consts, 1)
                pool.memset(x3[:], 0.0).then_inc(consts, 1)
                pool.iota(token_id[:], pattern=[[P, NB]], base=0, channel_multiplier=1).then_inc(consts, 1)
                pool.iota(iota[:], pattern=[[1, NT]], base=0, channel_multiplier=0).then_inc(consts, 1)
                pool.wait_ge(consts, 7)
                pool.affine_select(out=before[:], in_=before[:], compare_op=ALU.is_gt, fill=0.0, base=0,
                                   pattern=[[1, P]], channel_multiplier=-1).then_inc(consts, 1)
                pool.tensor_copy(tile_no[:], iota[:]).then_inc(consts, 1)
                pool.wait_ge(consts, 9)
                pool.tensor_scalar(starts[:], tile_no[:, 0:NB], float(P), None, ALU.mult).then_inc(consts, 1)
                pool.tensor_scalar(reverse[:], tile_no[:, 0:NE], -1.0, float(NE), ALU.mult, ALU.add).then_inc(consts, 1)

                pool.wait_ge(ids_blank, 16)
                pool.wait_ge(slots_ready, 1)
                for t in range(NB):
                    pool.indirect_dma_start(ids_dram, bass.IndirectOffsetOnAxis(slot_at[:, t:t + 1].bitcast(U32), 0),
                                            token_id[:, t:t + 1], None).then_inc(ids_scattered, 16)
                pool.wait_ge(ids_loaded, 16)
                last_token = pool.to_reg(TOKENS - 1)

                def held(value):
                    return value if isinstance(value, int) else pool.to_reg(value)

                def gather_z(j, s, i):
                    ready, back, uses = held(j + 1), held(j - NS + 1), held(16 * i)
                    pool.wait_ge(ids_loaded, 16)
                    if inside(j, NS, NT - 1):
                        pool.wait_ge(z_turned, back)
                        pool.wait_ge(z_gathered[s], uses)
                    pool.tensor_copy(z_ids[:, s:s + 1], ids[:, bass.ds(j, 1)]).then_inc(z_ids_ready, 1)
                    pool.wait_ge(ids_loaded, 16)
                    pool.wait_ge(z_ids_ready, ready)
                    index = bass.IndirectOffsetOnAxis(z_ids[:, s:s + 1].bitcast(U32), 0)
                    pool.indirect_dma_start(z[:, s, :], None, z_dram, index, bounds_check=last_token, oob_is_err=False)\
                        .then_inc(z_gathered[s], 16)

                def gather_x3(j, s, i):
                    ready, back, uses = held(j + 1), held(j - NS + 1), held(16 * i)
                    pool.wait_ge(ids_loaded, 16)
                    if inside(j, NS, NT - 1):
                        pool.wait_ge(res_ready, back)
                        pool.wait_ge(x3_gathered[s], uses)
                    pool.tensor_copy(x3_ids[:, s:s + 1], ids[:, bass.ds(j, 1)]).then_inc(x3_ids_ready, 1)
                    pool.wait_ge(ids_loaded, 16)
                    pool.wait_ge(x3_ids_ready, ready)
                    index = bass.IndirectOffsetOnAxis(x3_ids[:, s:s + 1].bitcast(U32), 0)
                    pool.indirect_dma_start(x3[:, s, :], None, x3_dram, index, bounds_check=last_token, oob_is_err=False)\
                        .then_inc(x3_gathered[s], 16)

                def scatter(j, s, i):
                    ready, uses = held(j + 1), held(16 * i)
                    pool.wait_ge(ids_loaded, 16)
                    if inside(j, NS, NT - 1):
                        pool.wait_ge(out_stored[s], uses)
                    pool.tensor_copy(out_ids[:, s:s + 1], ids[:, bass.ds(j, 1)]).then_inc(out_ids_ready, 1)
                    pool.wait_ge(ids_loaded, 16)
                    pool.wait_ge(out_ids_ready, ready)
                    pool.wait_ge(res_ready, ready)
                    index = bass.IndirectOffsetOnAxis(out_ids[:, s:s + 1].bitcast(U32), 0)
                    pool.indirect_dma_start(out, index, res[:, s, :], None, bounds_check=last_token, oob_is_err=False)\
                        .then_inc(out_stored[s], 16)

                def step(j, s, i):
                    if inside(j, 0, NT - NS):
                        gather_z(j + 2, (s + 2) % NS, i if s == 0 else i + 1)
                    if inside(j, 0, NT - 1):
                        gather_x3(j, s, i)
                    if inside(j, 2, NT + 1):
                        scatter(j - 2, (s + 1) % NS, i if s == 2 else i - 1)

                gather_z(0, 0, 0)
                gather_z(1, 1, 0)
                run_tiles(pool, step, NT + 1)
                for s in range(NS):
                    pool.wait_ge(out_stored[s], 16 * (NT // NS))

            @block.tensor
            def _(pe):
                pe.wait_ge(consts, 8)
                pe.wait_ge(onehot_ready, 1)
                flat = onehot[:].rearrange("p t e -> p (t e)")
                pe.matmul(ps_h[:, 0:NB * NE], before[:], flat, start=True, stop=True)
                pe.matmul(ps_h[:, BANK:BANK + NB * NE], ones[:], flat, start=True, stop=True).then_inc(counted, 1)
                pe.wait_ge(relu_b1_ready, 1)
                for e in range(NE):
                    pe.wait_ge(w2_loaded, 16 * NE)
                    if e >= 2:
                        pe.wait_ge(idle_copied, e - 1)
                    for f in range(FB):
                        last = pe.matmul(ps_idle[:, e % 2, 0:D], relu_b1[:, e, f:f + 1].to_broadcast([P, P]), w2[:, e, f, :],
                                         start=(f == 0), stop=(f == FB - 1))
                    last.then_inc(idle_done, 1)
                pe.wait_ge(w1_loaded, 16 * NE)
                pe.wait_ge(tile_expert_ready, 1)

                def turn_z(j, s, i):
                    pe.wait_ge(z_gathered[s], 16 * (i + 1))
                    if inside(j, 1, NT - 1):
                        pe.wait_ge(zT_ready, j)
                    for k in range(ND):
                        last = pe.transpose(ps_zT[:, k * P:(k + 1) * P], z[:, s, k * P:(k + 1) * P], ident[:])
                    last.then_inc(z_turned, 1)

                def first_layer(j, s, e):
                    pe.wait_ge(zT_ready, j + 1)
                    if inside(j, 1, NT - 1):
                        pe.wait_ge(h_ready, 2 * j)
                    for c in range(FE // BANK):
                        for k in range(ND):
                            last = pe.matmul(ps_h[:, c * BANK:(c + 1) * BANK], zT[:, s, k, :],
                                             w1[:, e, k, c * BANK:(c + 1) * BANK], start=(k == 0), stop=(k == ND - 1))
                        last.then_inc(h_done, 1)

                def turn_h(j):
                    for c in range(2):
                        pe.wait_ge(h_ready, 2 * j + c + 1)
                        if inside(j, 1, NT - 1):
                            pe.wait_ge(hT_ready, FB * j - FB // 2 * (1 - c))
                        for f in range(c * FB // 2, (c + 1) * FB // 2):
                            last = pe.transpose(ps_hT[:, f, :], h[:, f * P:(f + 1) * P], ident[:])
                        last.then_inc(h_turned, 1)

                def second_layer(j, s, e):
                    pe.wait_ge(hT_ready, FB * (j + 1))
                    if inside(j, 1, NT - 1):
                        pe.wait_ge(y_read, j)
                    for f in range(FB):
                        last = pe.matmul(ps_y[:, 0:D], hT[:, s, f, :], w2[:, e, f, :], start=(f == 0), stop=(f == FB - 1))
                    last.then_inc(y_done, 1)

                def step(j, s, i):
                    if inside(j, 0, NT - 1):
                        first_layer(j, s, expert_of(pe, j))
                    if inside(j, 0, NT - 2):
                        turn_z(j + 1, (s + 1) % NS, i + (s == NS - 1))
                    if inside(j, 1, NT):
                        second_layer(j - 1, (s + NS - 1) % NS, expert_of(pe, j - 1))
                    if inside(j, 0, NT - 1):
                        turn_h(j)

                turn_z(0, 0, 0)
                run_tiles(pe, step, NT)

            @block.vector
            def _(dve):
                done = [0]

                def then(instruction):
                    done[0] += 1
                    instruction.then_inc(chain, 1)
                    dve.wait_ge(chain, done[0])

                def by_tile(t, n=NE):
                    return t.unsqueeze(2).to_broadcast([P, t.shape[1], n])

                def every_tile(t, n):
                    return t.unsqueeze(1).to_broadcast([P, n, t.shape[1]])

                dve.wait_ge(consts, 11)
                then(dve.tensor_reduce(top[:], logits[:], AX_X, ALU.max))
                then(dve.tensor_tensor(is_top[:], logits[:], by_tile(top[:]), ALU.is_equal))
                then(dve.tensor_tensor(first_top[:], is_top[:], every_tile(reverse[:], NB), ALU.mult))
                then(dve.tensor_reduce(choice[:], first_top[:], AX_X, ALU.max))
                dve.tensor_tensor(onehot[:], every_tile(reverse[:], NB), by_tile(choice[:]), ALU.is_equal)\
                   .then_inc(onehot_ready, 1)
                dve.wait_ge(counted, 1)
                then(dve.tensor_copy(counts[:], ps_h[:, BANK:BANK + NB * NE].rearrange("p (t e) -> p e t", e=NE)))
                src, dst = counts, running
                for reach in (1, 2, 4, 8, 16):
                    dve.tensor_copy(dst[:, :, 0:reach], src[:, :, 0:reach]).then_inc(chain, 1)
                    done[0] += 1
                    then(dve.tensor_tensor(dst[:, :, reach:NB], src[:, :, reach:NB], src[:, :, 0:NB - reach], ALU.add))
                    src, dst = dst, offset if dst is running else running
                totals = running[:, :, NB - 1]
                then(dve.tensor_tensor(fills[:], by_tile(totals, NB), every_tile(starts[:], NE), ALU.is_gt))
                then(dve.tensor_reduce(tiles[:], fills[:], AX_X, ALU.add))
                src, dst = tiles, tile_end
                for reach in (1, 2, 4):
                    dve.tensor_copy(dst[:, 0:reach], src[:, 0:reach]).then_inc(chain, 1)
                    done[0] += 1
                    then(dve.tensor_tensor(dst[:, reach:NE], src[:, reach:NE], src[:, 0:NE - reach], ALU.add))
                    src, dst = dst, base if dst is tile_end else tile_end
                then(dve.tensor_tensor(base[:], tile_end[:], tiles[:], ALU.subtract))
                then(dve.tensor_scalar(base[:], base[:], float(P), None, ALU.mult))
                then(dve.tensor_tensor(offset[:], running[:], counts[:], ALU.subtract))
                then(dve.tensor_tensor(offset[:], offset[:], by_tile(base[:], NB), ALU.add))
                then(dve.tensor_tensor(place[:], ps_h[:, 0:NB * NE].rearrange("p (t e) -> p t e", e=NE),
                                       offset[:].rearrange("p e t -> p t e"), ALU.add))
                then(dve.tensor_tensor(place[:], place[:], onehot[:], ALU.mult))
                then(dve.tensor_reduce(slot_f[:], place[:], AX_X, ALU.add))
                then(dve.tensor_copy(slot[:], slot_f[:]))
                then(dve.tensor_scalar(slot_tile[:], slot[:], P.bit_length() - 1, None, ALU.logical_shift_right))
                then(dve.tensor_scalar(slot_row[:], slot[:], P - 1, None, ALU.bitwise_and))
                then(dve.tensor_scalar(slot_at[:], slot_row[:], NT, None, ALU.mult))
                dve.tensor_tensor(slot_at[:], slot_at[:], slot_tile[:], ALU.add).then_inc(slots_ready, 1)
                then(dve.tensor_tensor(ends_before[:], every_tile(tile_end[:], NT), by_tile(tile_no[:]), ALU.is_le))
                then(dve.tensor_reduce(tile_expert_f[:], ends_before[:], AX_X, ALU.add))
                then(dve.tensor_scalar(tile_expert_f[:], tile_expert_f[:], float(NE - 1), None, ALU.min))
                dve.tensor_copy(tile_expert[:], tile_expert_f[:]).then_inc(tile_expert_ready, 1)

                dve.wait_ge(bias_loaded, 32)
                dve.tensor_scalar(relu_b1[:], b1T[:], 0.0, None, ALU.max).then_inc(relu_b1_ready, 1)
                for e in range(NE):
                    dve.wait_ge(idle_done, e + 1)
                    dve.tensor_copy(idle[:, e, :], ps_idle[:, e % 2, 0:D]).then_inc(idle_copied, 1)
                dve.wait_ge(idle_copied, NE)
                then(dve.tensor_tensor(idle_b2[:], idle[:], b2[:], ALU.add))
                then(dve.tensor_reduce(idle_sum[:], idle_b2[:].rearrange("p e d -> p d e"), AX_X, ALU.add))
                then(dve.tensor_tensor(other[:], every_tile(idle_sum[:], NE), idle[:], ALU.subtract))

                def copy_h(j):
                    for c in range(2):
                        dve.wait_ge(h_done, 2 * j + c + 1)
                        if inside(j, 1, NT - 1):
                            dve.wait_ge(h_turned, 2 * j + c - 1)
                        cols = slice(c * BANK, (c + 1) * BANK)
                        dve.tensor_copy(h[:, cols], ps_h[:, cols]).then_inc(h_ready, 1)

                def finish(j, s, i):
                    dve.wait_ge(y_done, j + 1)
                    e = expert_of(dve, j)
                    dve.tensor_tensor(y[:, s, :], ps_y[:, 0:D], other[:, e, :], ALU.add).then_inc(y_read, 1)
                    dve.wait_ge(y_read, j + 1)
                    dve.wait_ge(x3_gathered[s], 16 * (i + 1))
                    if inside(j, NS, NT - 1):
                        dve.wait_ge(out_stored[s], 16 * i)
                    dve.tensor_tensor(res[:, s, :], y[:, s, :], x3[:, s, :], ALU.add).then_inc(res_ready, 1)

                def step(j, s, i):
                    if inside(j, 0, NT - 1):
                        copy_h(j)
                    if inside(j, 1, NT):
                        finish(j - 1, (s + NS - 1) % NS, i if s else i - 1)

                dve.wait_ge(tile_expert_ready, 1)
                run_tiles(dve, step, NT)

            @block.scalar
            def _(act):
                def copy_z(j, s):
                    act.wait_ge(z_turned, j + 1)
                    if inside(j, NS, NT - 1):
                        act.wait_ge(h_done, 2 * (j - NS + 1))
                    act.activation(zT[:, s], ps_zT[:, 0:D].rearrange("p (k t) -> p k t", t=P), ACT.Copy).then_inc(zT_ready, 1)

                def rectify(j, s):
                    e = expert_of(act, j)
                    if inside(j, NS, NT - 1):
                        act.wait_ge(y_done, j - NS + 1)
                    for f in range(FB):
                        if f % (FB // 2) == 0:
                            act.wait_ge(h_turned, 2 * j + f // (FB // 2) + 1)
                        act.activation(hT[:, s, f, :], ps_hT[:, f, :], ACT.Relu, bias=b1T[:, e, f:f + 1]).then_inc(hT_ready, 1)

                def step(j, s, i):
                    if inside(j, 0, NT - 2):
                        copy_z(j + 1, (s + 1) % NS)
                    rectify(j, s)

                act.wait_ge(bias_loaded, 32)
                act.wait_ge(tile_expert_ready, 1)
                copy_z(0, 0)
                run_tiles(act, step)


def cross_attention_network(nc, eye, x, ctx, ctx_blocks, ctx_t, mask_t, w_up, w_gate, w_down, w, experts_w, out):
    x1, x2, x3, z = (nc.dram_tensor(f"{name}_scratch", [NB, P, D], F32).ap() for name in ("x1", "x2", "x3", "z"))
    ids = nc.dram_tensor("ids_scratch", [P * NT, 1], I32).ap()
    with ExitStack() as persistent:
        def sb(stack, name, shape):
            return stack.enter_context(nc.sbuf_tensor(name, shape, F32))

        ident = sb(persistent, "ident", [P, P])
        mv2 = sb(persistent, "mv2", [P, NB, 2])
        rstd2 = sb(persistent, "rstd2", [P, NB])
        logits = sb(persistent, "logits", [P, NB, NE])
        ident_loaded = persistent.enter_context(nc.semaphore("ident_loaded"))
        with nc.Block() as block:
            @block.sync
            def _(sp):
                sp.dma_start(ident[:], eye).then_inc(ident_loaded, 16)
                sp.wait_ge(ident_loaded, 16)

        with ExitStack() as first:
            yT = sb(first, "yT", [P, ND, NB * P])
            ymax = sb(first, "ymax", [P, NB])
            upT = sb(first, "upT", [P, ND, FF])
            gateT = sb(first, "gateT", [P, ND, FF])
            downT = sb(first, "downT", [P, NF, D])
            used = attention0(nc, ident, [(w_up, upT), (w_gate, gateT), (w_down, downT)], yT, ymax, x, ctx, ctx_blocks, mask_t, x1)
            feed_forward0(nc, yT, ymax, upT, gateT, downT, x1, x2, mv2, rstd2)
        with nc.Block() as block:
            @block.gpsimd
            def _(pool):
                for semaphore in used:
                    pool.sem_clear(semaphore)
        attention1(nc, ident, mv2, rstd2, logits, w, ctx_t, x2, x3, z)
        experts(nc, ident, logits, experts_w, z.rearrange("b p d -> (b p) d"), x3.rearrange("b p d -> (b p) d"), ids, out)


def kernel(**inputs):
    import numpy as np
    from concourse import bacc
    from concourse.bass_utils import run_bass_kernel_spmd

    a = {name: np.asarray(value) for name, value in inputs.items()}
    x, ctx, mask = a["x"], a["ctx_1024"], a["mask_BxSxS2_ik1"]

    def attn(name):
        return a["L1_xattn_" + name]

    def expert(name):
        return a["L1_ffn_" + name]

    def by_rows(weights):
        return weights.reshape(-1, P, weights.shape[-1]).transpose(1, 0, 2)

    arrays = {
        "eye": np.eye(P, dtype=np.float32),
        "x": x,
        "ctx": ctx,
        "ctx_blocks": ctx.reshape(NB // 2, 2, P, 2, NH // 2, HD0).transpose(0, 4, 5, 3, 1, 2),
        "ctx_t": ctx.reshape(NB * P, ND, P).transpose(2, 1, 0),
        "mask_t": mask.transpose(2, 0, 1),
        "w_up": a["L0_ffn_w_up"],
        "w_gate": a["L0_ffn_w_gate"],
        "w_down": a["L0_ffn_w_down"],
        "wq": by_rows(attn("Wq")),
        "wk": by_rows(attn("Wk")),
        "wv": by_rows(attn("Wv")),
        "wo": by_rows(attn("Wo")),
        "wr": by_rows(expert("Wr")),
        "bq": attn("bq").reshape(-1, P).T,
        "bk": attn("bk").reshape(-1, P).T,
        "bv": attn("bv"),
        "bo": attn("bo"),
        "gamma": attn("ln_gamma"),
        "beta": attn("ln_beta"),
        "br": expert("br"),
        "w1": expert("W1").reshape(NE, ND, P, FE).transpose(0, 2, 1, 3),
        "w2": expert("W2").reshape(NE, FE // P, P, D).transpose(0, 2, 1, 3),
        "b1T": expert("b1").reshape(NE, FE // P, P).transpose(2, 0, 1),
        "b2": expert("b2"),
    }
    arrays = {f"{name}_in": np.ascontiguousarray(array) for name, array in arrays.items()}

    nc = bacc.Bacc("TRN2", target_bir_lowering=False, num_devices=1)
    d = {name[:-3]: nc.dram_tensor(name, array.shape, mybir.dt.from_np(array.dtype), kind="ExternalInput").ap()
         for name, array in arrays.items()}
    out = nc.dram_tensor("out", [NB * P, D], F32, kind="ExternalOutput").ap()
    attention_w = {name: d[name] for name in ("wq", "wk", "wv", "wo", "wr", "bq", "bk", "bv", "bo", "gamma", "beta", "br")}
    experts_w = {"w1": [d["w1"][e] for e in range(NE)], "w2": [d["w2"][e] for e in range(NE)], "b1T": d["b1T"], "b2": d["b2"]}
    cross_attention_network(nc, d["eye"], d["x"], d["ctx"], d["ctx_blocks"], d["ctx_t"], d["mask_t"],
                            d["w_up"], d["w_gate"], d["w_down"], attention_w, experts_w, out)
    result = run_bass_kernel_spmd(nc, [arrays], core_ids=[0])
    return result.results[0]["out"].reshape(NB, P, D)
```

```python
from contextlib import ExitStack
from itertools import product
from math import prod

import concourse.bass as bass
from concourse import mybir

ALU = mybir.AluOpType
ACT = mybir.ActivationFunctionType
BF16 = mybir.dt.bfloat16
AX_X = mybir.AxisListType.X
F32 = mybir.dt.float32
F32R = mybir.dt.float32r
F16 = mybir.dt.float16
I32 = mybir.dt.int32
I16 = mybir.dt.int16
U16 = mybir.dt.uint16
U32 = mybir.dt.uint32

P = 128
NB = 32
D = 256
ND = D // P
NH = 16
HD0 = D // NH
HB = 4
BANK = 512
EPS = 1e-5
NEG = -10000.0
PARTS = ((0, 0), (0, 1), (1, 0))
NE = 8
FE = 1024
UN = 4


def inside(b, first, last):
    return not isinstance(b, int) or first <= b <= last


FF = 768
NF = FF // P
BLOCK = 32
W_MAX = 7.0
A_MAX = 32767.0
TINY = 1e-12
MAGIC = 12582912.0


def weight_quantiser(sem, ident, weights, raw, steps, rounded, deq, scale, inv, ps):
    PER = 4
    GROUPS = FF * D // P // P // PER
    loaded = [sem(f"w_loaded{n}") for n in range(len(weights))]
    chain = sem("w_chain")
    deq_ready = sem("w_deq_ready")
    turned = sem("w_turned")
    copied = sem("w_copied")

    def load(sp, n):
        w = weights[n][0]
        dst = raw[:, n].rearrange("p n k -> p (n k)").rearrange("p (o i) -> p o i", i=w.shape[1])
        sp.dma_start(dst, w.rearrange("(o p) i -> p o i", p=P)).then_inc(loaded[n], 16)

    def quantise(dve):
        done = [0]

        def then(instruction):
            done[0] += 1
            instruction.then_inc(chain, 1)
            dve.wait_ge(chain, done[0])

        for n in range(len(weights)):
            s = n % 2

            def wide(t):
                return t[:, s, :].unsqueeze(2).to_broadcast(list(raw[:, n].shape))

            dve.wait_ge(loaded[n], 16)
            then(dve.tensor_reduce(scale[:, s], raw[:, n], AX_X, ALU.max, apply_absolute_value=True))
            then(dve.tensor_scalar(scale[:, s], scale[:, s], 1.0 / W_MAX, TINY, ALU.mult, ALU.max))
            then(dve.reciprocal(inv[:, s], scale[:, s]))
            then(dve.tensor_tensor(steps[:, s], raw[:, n], wide(inv), ALU.mult))
            then(dve.tensor_scalar(rounded[:, s], steps[:, s], W_MAX, -W_MAX - 1.0, ALU.min, ALU.max))
            if n >= 2:
                dve.wait_ge(turned, GROUPS * (n - 1))
            dve.tensor_tensor(deq[:, s], rounded[:, s], wide(scale), ALU.mult).then_inc(deq_ready, 1)

    def turn(pe):
        for n in range(len(weights)):
            pe.wait_ge(deq_ready, n + 1)
            flat = deq[:, n % 2].rearrange("p n k -> p (n k)")
            for g in range(GROUPS):
                m = GROUPS * n + g
                if m >= 4:
                    pe.wait_ge(copied, m - 3)
                for q in range(PER):
                    c = (PER * g + q) * P
                    last = pe.transpose(ps[:, m % 4, q * P:(q + 1) * P], flat[:, c:c + P], ident[:])
                last.then_inc(turned, 1)
        return lambda: pe.wait_ge(copied, GROUPS * len(weights))

    def copy(act):
        for n, (w, wT) in enumerate(weights):
            ni = w.shape[1] // P
            for g in range(GROUPS):
                m = GROUPS * n + g
                act.wait_ge(turned, m + 1)
                for q in range(PER):
                    o, k = divmod(PER * g + q, ni)
                    last = act.activation(wT[:, k, o * P:(o + 1) * P], ps[:, m % 4, q * P:(q + 1) * P], ACT.Copy)
                last.then_inc(copied, 1)

    return load, quantise, turn, copy


def attention0(nc, ident, weights, yT, ymax, x, ctx, ctx_blocks, mask_t, x1_dram):
    HALF = NH // 2
    VW = 2 * HD0
    used = []
    with ExitStack() as ctx_stack:
        def sb(name, shape, dt=F32):
            return ctx_stack.enter_context(nc.sbuf_tensor("a_" + name, shape, dt))

        def psum(name, shape, dt=F32):
            return ctx_stack.enter_context(nc.psum_tensor("a_" + name, shape, dt))

        def sem(name):
            used.append(ctx_stack.enter_context(nc.semaphore("a_" + name)))
            return used[-1]

        x_sb = sb("x", [P, NB, D])
        v_raw = sb("v_raw", [P, NB, D])
        v_ones = sb("v_ones", [P, 2, NH, VW])
        keys = sb("keys", [P, 2, ND, HALF, 2, P])
        mask_int = sb("mask_int", [P, 8, P], I32)
        mask16 = sb("mask16", [P, NB, P], F16)
        neg_eye = sb("neg_eye", [P, HB, P], F16)
        stats0 = sb("stats0", [P, NB, 6])
        mv0 = sb("mv0", [P, NB, 2])
        var0 = sb("var0", [P, NB])
        power = sb("power", [P, NB])
        rstd0 = sb("rstd0", [P, NB])
        q_in = sb("q_in", [P, 2, D])
        qT = sb("qT", [P, 2, ND, P])
        row_max = sb("row_max", [P, 2, HALF])
        prob = sb("prob", [P, 2, 2, HALF, P])
        probT = sb("probT", [P, 4, HB, P])
        outT = sb("outT", [P, NH // HB, P])
        inv_sum = sb("inv_sum", [P, 2, NH])
        attn = sb("attn", [P, 2, NH, HD0])
        stats1 = sb("stats1", [P, 2, 6])
        mv1 = sb("mv1", [P, 2, 2])
        eps = sb("eps", [P, 1])
        var1 = sb("var1", [P, 2, 1])
        rstd1 = sb("rstd1", [P, 2, 1])
        y = sb("y", [P, 2, D])

        ps_score = psum("ps_score", [P, 2, HALF, P])
        ps_probT = psum("ps_probT", [P, 2, HB, P])
        ps_qy = psum("ps_qy", [P, 2, ND, P])
        ps_out = psum("ps_out", [P, BANK])
        out_heads = ps_out[:].rearrange("p (h w) -> p h w", w=VW)

        x_loaded = [sem(f"x_loaded{c}") for c in range(4)]
        v_loaded = [sem(f"v_loaded{c}") for c in range(4)]
        mask_loaded = sem("mask_loaded")
        keys_loaded = [sem(f"keys_loaded{s}") for s in range(2)]
        x1_stored = sem("x1_stored")
        keys_zero = sem("keys_zero")
        consts = sem("consts")
        mask_ready = sem("mask_ready")
        v_ready = sem("v_ready")
        outT_ready = sem("outT_ready")
        out_turned = sem("out_turned")
        stats0_done = sem("stats0_done")
        mv0_done = sem("mv0_done")
        var0_done = sem("var0_done")
        rstd0_done = sem("rstd0_done")
        q_in_ready = sem("q_in_ready")
        qy_done = sem("qy_done")
        qT_ready = sem("qT_ready")
        yT_ready = sem("yT_ready")
        scores_done = sem("scores_done")
        max_done = sem("max_done")
        shifted = sem("shifted")
        exp_done = sem("exp_done")
        probT_done = sem("probT_done")
        probT_ready = sem("probT_ready")
        out_done = sem("out_done")
        inv_done = sem("inv_done")
        out_read = sem("out_read")
        x1_ready = sem("x1_ready")
        stats1_done = sem("stats1_done")
        mv1_done = sem("mv1_done")
        var1_done = sem("var1_done")
        rstd1_done = sem("rstd1_done")
        y_ready = sem("y_ready")
        y_max_done = sem("y_max_done")

        PAIR_DMAS = HALF
        NQ = NH // HB

        COLS = FF * D // P
        MATS = len(weights)
        spare = yT[:].rearrange("p k t -> p (k t)")
        w_scale = sb("w_scale", [P, 2, COLS // BLOCK])
        w_inv = sb("w_inv", [P, 2, COLS // BLOCK])

        def blocks(flat, n):
            return flat[:, 0:n * COLS].rearrange("p (m n k) -> p m n k", m=n, k=BLOCK)

        load_weights, quantise_weights, turn_weights, copy_weights = weight_quantiser(
            sem, ident, weights,
            raw=blocks(spare, MATS), deq=blocks(spare[:, MATS * COLS:], 2),
            steps=blocks(prob[:].rearrange("p a b h k -> p (a b h k)"), 2),
            rounded=blocks(probT[:].rearrange("p q h k -> p (q h k)").bitcast(I16), 2),
            scale=w_scale, inv=w_inv, ps=ps_score[:].rearrange("p a (b h) k -> p (a b) (h k)", h=HB))

        with nc.Block() as block:

            @block.sync
            def _(sp):
                def load_keys(pair, slot):
                    for j in range(HALF):
                        rows = slice(HD0 * j, HD0 * (j + 1))
                        for_j = keys[rows, slot, :, j, :, :]
                        sp.dma_start(for_j, ctx_blocks[pair, j]).then_inc(keys_loaded[slot], 16)

                def load_x(c):
                    part = slice(8 * c, 8 * (c + 1))
                    sp.dma_start(x_sb[:, part, :], x[part].rearrange("b t d -> t b d")).then_inc(x_loaded[c], 16)

                def load_v(c):
                    part = slice(8 * c, 8 * (c + 1))
                    sp.dma_start(v_raw[:, part, :], ctx[part].rearrange("b t d -> t b d")).then_inc(v_loaded[c], 16)

                def load_mask(c):
                    if c >= 1:
                        sp.wait_ge(mask_ready, c)
                    sp.dma_start(mask_int[:], mask_t[:, 8 * c:8 * (c + 1), :]).then_inc(mask_loaded, 16)

                load_weights(sp, 0)
                load_weights(sp, 1)
                load_x(0)
                load_weights(sp, 2)
                load_mask(0)
                sp.wait_ge(keys_zero, 1)
                load_keys(0, 0)
                load_keys(1, 1)
                load_v(0)
                for c in range(1, 4):
                    load_x(c)
                    if c < 3:
                        load_mask(c)

                def step(b, u, pair):
                    if u % 2 == 1 and inside(b, 0, NB - 5):
                        sp.wait_ge(scores_done, 2 * b + 2)
                        load_keys(pair + 2, u // 2)
                    sp.wait_ge(x1_ready, b + 1)
                    sp.dma_start(x1_dram[b], x_sb[:, b, :]).then_inc(x1_stored, 16)

                for b in range(UN):
                    step(b, b, b // 2)
                    if b == 1:
                        load_mask(3)
                        for c in range(1, 4):
                            load_v(c)
                with sp.Fori(1, NB // UN - 1) as i:
                    for u in range(UN):
                        step(UN * i + u, u, 2 * i + u // 2)
                for b in range(NB - UN, NB):
                    step(b, b % UN, b // 2)
                sp.wait_ge(x1_stored, 16 * NB)

            @block.gpsimd
            def _(pool):
                def values(b, s):
                    if inside(b, 2, NB - 1):
                        pool.wait_ge(out_done, NQ * (b - 1))
                    src = v_raw[:, b, :].rearrange("p (h w) -> p h w", w=HD0)
                    pool.tensor_copy(v_ones[:, s, :, 0:HD0], src).then_inc(v_ready, 1)

                pool.memset(keys[:], 0.0).then_inc(keys_zero, 1)
                pool.memset(power[:], -0.5).then_inc(consts, 1)
                pool.memset(eps[:], EPS).then_inc(consts, 1)
                pool.memset(v_ones[:], 1.0).then_inc(consts, 1)
                pool.memset(neg_eye[:], 0.0).then_inc(consts, 1)
                pool.wait_ge(consts, 4)
                pool.affine_select(out=neg_eye[:], in_=neg_eye[:], compare_op=ALU.not_equal, fill=NEG, base=0,
                                   pattern=[[0, HB], [-1, P]], channel_multiplier=1).then_inc(consts, 1)
                def eight_sequences(c):
                    part = slice(8 * c, 8 * (c + 1))
                    pool.wait_ge(mv0_done, 8 * (c + 1))
                    pool.tensor_scalar(var0[:, part], mv0[:, part, 1], EPS, None, ALU.add).then_inc(var0_done, 1)
                    pool.wait_ge(var0_done, c + 1)
                    pool.tensor_tensor(rstd0[:, part], var0[:, part], power[:, part], ALU.pow).then_inc(rstd0_done, 1)
                    pool.wait_ge(mask_loaded, 16 * (c + 1))
                    pool.tensor_copy(mask16[:, part, :], mask_int[:]).then_inc(mask_ready, 1)

                def step(b, s):
                    if inside(b, 0, NB - 3):
                        values(b + 2, s)
                    pool.wait_ge(mv1_done, b + 1)
                    pool.tensor_tensor(var1[:, s], mv1[:, s, 1:2], eps[:], ALU.add).then_inc(var1_done, 1)
                    pool.wait_ge(var1_done, b + 1)
                    pool.tensor_tensor(rstd1[:, s], var1[:, s], power[:, 0:1], ALU.pow).then_inc(rstd1_done, 1)

                eight_sequences(0)
                pool.wait_ge(v_loaded[0], 16)
                for b in range(2):
                    values(b, b)
                for b in range(2 * UN):
                    if b < 3:
                        eight_sequences(b + 1)
                    elif b > UN:
                        pool.wait_ge(v_loaded[b - UN], 16)
                    step(b, b % 2)
                with pool.Fori(2, NB // UN - 1) as i:
                    for u in range(UN):
                        step(UN * i + u, u % 2)
                for b in range(NB - UN, NB):
                    step(b, b % 2)

            @block.tensor
            def _(pe):
                def scores(b, u, half):
                    if half == 0:
                        pe.wait_ge(qT_ready, b + 1)
                        if u % 2 == 0:
                            if not isinstance(b, int):
                                pe.wait_ge(mask_ready, 4)
                            turn = 1 + b // UN if isinstance(b, int) else turns[0] + 1
                            pe.wait_ge(keys_loaded[u // 2], 16 * PAIR_DMAS * turn)
                    if inside(b, 1, NB):
                        pe.wait_ge(shifted, 2 * b + half - 1)
                    for q in range(2):
                        heads = slice(HB * q, HB * (q + 1))
                        out = ps_score[:, half, heads, :]
                        pe.matmul(out, qT[:, u % 2, half, :], keys[:, u // 2, half, heads, u % 2, :],
                                  start=True, stop=False)
                        last = pe.matmul(out, mask16[:, b, :], neg_eye[:], start=False, stop=True)
                    last.then_inc(scores_done, 1)

                def transposes(b, s, q):
                    n = NQ * b + q
                    if q % 2 == 0:
                        pe.wait_ge(exp_done, 2 * b + q // 2 + 1)
                    if inside(b, 1, NB) or q >= 2:
                        pe.wait_ge(probT_ready, n - 1)
                    for h in range(HB):
                        last = pe.transpose(ps_probT[:, q % 2, h, :], prob[:, s, q // 2, HB * (q % 2) + h, :], ident[:])
                    last.then_inc(probT_done, 1)

                def weighted(b, u, q):
                    pe.wait_ge(probT_ready, NQ * b + q + 1)
                    if q == 0:
                        pe.wait_ge(v_ready, b + 1)
                        if inside(b, 1, NB):
                            pe.wait_ge(out_read, b)
                    for h in range(HB):
                        last = pe.matmul(ps_out[h * VW:(h + 1) * VW, q * P:(q + 1) * P], v_ones[:, u % 2, HB * q + h, :],
                                         probT[:, q, h, :], start=True, stop=True)
                    last.then_inc(out_done, 1)

                def turn_out(b):
                    pe.wait_ge(outT_ready, b + 1)
                    for q in range(NQ):
                        last = pe.transpose(ps_out[:, q * P:(q + 1) * P], outT[:, q, :], ident[:])
                    last.then_inc(out_turned, 1)

                def turn_qy(g, s):
                    if inside(g, 5, NB + 4):
                        pe.wait_ge(yT_ready, g - 4)
                    elif g >= 1:
                        pe.wait_ge(qT_ready, g)
                    if inside(g, 0, NB - 1):
                        pe.wait_ge(q_in_ready, g + 1)
                        for k in range(ND):
                            last = pe.transpose(ps_qy[:, 0, k, :], q_in[:, s, k * P:(k + 1) * P], ident[:])
                    if inside(g, 4, NB + 3):
                        pe.wait_ge(y_ready, g - 3)
                        for k in range(ND):
                            last = pe.transpose(ps_qy[:, 1, k, :], y[:, s, k * P:(k + 1) * P], ident[:])
                    last.then_inc(qy_done, 1)

                def step(b, u):
                    for half in range(2):
                        if inside(b, 0, NB - 1):
                            scores(b, u, half)
                        if half == 0 and inside(b, 2, NB + 1):
                            turn_out(b - 2)
                        if inside(b, 1, NB):
                            p, pu = b - 1, (u - 1) % UN
                            if half == 0:
                                transposes(p, pu % 2, 0)
                                transposes(p, pu % 2, 1)
                            else:
                                weighted(p, pu, 0)
                                weighted(p, pu, 1)
                                transposes(p, pu % 2, 2)
                                transposes(p, pu % 2, 3)
                                turn_qy(b + 1, (u + 1) % 2)
                                weighted(p, pu, 2)
                                weighted(p, pu, 3)
                    if isinstance(b, int) and (b < 1 or b > NB):
                        turn_qy(b + 1, (u + 1) % 2)

                weights_copied = turn_weights(pe)
                pe.wait_ge(consts, 5)
                turn_qy(0, 0)
                weights_copied()
                pe.wait_ge(mask_ready, 1)
                turns = [0]
                for b in range(2 * UN):
                    step(b, b % UN)
                with pe.Fori(2, NB // UN - 1) as i:
                    turns[0] = i
                    for u in range(UN):
                        step(UN * i + u, u)
                for b in range(NB - UN, NB + 3):
                    step(b, b % UN)

            @block.vector
            def _(dve):
                def queries(b, s):
                    dve.wait_ge(rstd0_done, b // 8 + 1 if isinstance(b, int) else 4)
                    if inside(b, 2, NB - 1):
                        dve.wait_ge(qy_done, b - 1)
                    dve.tensor_scalar(q_in[:, s, :], x_sb[:, b, :], mv0[:, b, 0:1], rstd0[:, bass.ds(b, 1)],
                                      ALU.subtract, ALU.mult).then_inc(q_in_ready, 1)

                def softmax_shift(b, s, half):
                    n = 2 * b + half + 1
                    dve.wait_ge(scores_done, n)
                    dve.tensor_reduce(row_max[:, half, :], ps_score[:, half], AX_X, ALU.max).then_inc(max_done, 1)
                    dve.wait_ge(max_done, n)
                    if inside(b, 2, NB):
                        dve.wait_ge(probT_done, NQ * (b - 2) + 2 * half + 2)
                    dve.tensor_tensor(prob[:, s, half], ps_score[:, half],
                                      row_max[:, half, :].unsqueeze(2).to_broadcast([P, HALF, P]),
                                      ALU.subtract).then_inc(shifted, 1)

                def divide(b, s):
                    dve.wait_ge(out_turned, b + 1)
                    dve.reciprocal(inv_sum[:, s, :].unsqueeze(2), out_heads[:, :, HD0:HD0 + 1]).then_inc(inv_done, 1)
                    dve.wait_ge(inv_done, b + 1)
                    dve.tensor_tensor(attn[:, s], out_heads[:, :, 0:HD0],
                                      inv_sum[:, s, :].unsqueeze(2).to_broadcast([P, NH, HD0]),
                                      ALU.mult).then_inc(out_read, 1)

                def residual(b, s):
                    dve.wait_ge(out_read, b + 1)
                    dve.tensor_tensor(x_sb[:, b, :], x_sb[:, b, :], attn[:, s].rearrange("p h w -> p (h w)"),
                                      ALU.add).then_inc(x1_ready, 1)
                    dve.wait_ge(stats0_done, 8)
                    dve.wait_ge(x1_ready, b + 1)
                    dve.bn_stats(stats1[:, s, :], x_sb[:, b, :]).then_inc(stats1_done, 1)
                    dve.wait_ge(stats0_done, 8)
                    dve.wait_ge(stats1_done, b + 1)
                    dve.bn_aggr(mv1[:, s, :], stats1[:, s, :]).then_inc(mv1_done, 1)

                def normalise(b, s):
                    dve.wait_ge(rstd1_done, b + 1)
                    if inside(b, 2, NB - 1):
                        dve.wait_ge(qy_done, b + 3)
                    dve.tensor_scalar(y[:, s, :], x_sb[:, b, :], mv1[:, s, 0:1], rstd1[:, s, :],
                                      ALU.subtract, ALU.mult).then_inc(y_ready, 1)
                    dve.wait_ge(y_ready, b + 1)
                    dve.tensor_reduce(ymax[:, bass.ds(b, 1)], y[:, s, :], AX_X, ALU.max, apply_absolute_value=True)\
                       .then_inc(y_max_done, 1)

                def step(b, s):
                    if inside(b, 0, NB - 2):
                        queries(b + 1, 1 - s)
                    if inside(b, 2, NB + 1):
                        divide(b - 2, s)
                    if inside(b, 0, NB - 1):
                        softmax_shift(b, s, 0)
                    if inside(b, 2, NB + 1):
                        residual(b - 2, s)
                    if inside(b, 0, NB - 1):
                        softmax_shift(b, s, 1)
                    if inside(b, 2, NB + 1):
                        normalise(b - 2, s)

                def statistics(c):
                    dve.wait_ge(x_loaded[c], 16)
                    for b in range(8 * c, 8 * (c + 1)):
                        dve.bn_stats(stats0[:, b, :], x_sb[:, b, :]).then_inc(stats0_done, 1)
                    dve.wait_ge(stats0_done, 8 * (c + 1))
                    for b in range(8 * c, 8 * (c + 1)):
                        dve.bn_aggr(mv0[:, b, :], stats0[:, b, :]).then_inc(mv0_done, 1)

                quantise_weights(dve)
                statistics(0)
                queries(0, 0)
                for b in range(UN):
                    step(b, b % 2)
                    if b < 3:
                        statistics(b + 1)
                with dve.Fori(1, NB // UN - 1) as i:
                    for u in range(UN):
                        step(UN * i + u, u % 2)
                for b in range(NB - UN, NB + 2):
                    step(b, b % 2)

            @block.scalar
            def _(act):
                def exponentials(b, s, half):
                    act.wait_ge(shifted, 2 * b + half + 1)
                    act.activation(prob[:, s, half], prob[:, s, half], ACT.Exp).then_inc(exp_done, 1)

                def copy_probT(b, q):
                    act.wait_ge(probT_done, NQ * b + q + 1)
                    if inside(b, 1, NB):
                        act.wait_ge(out_done, NQ * b + q - 3)
                    act.activation(probT[:, q], ps_probT[:, q % 2], ACT.Copy).then_inc(probT_ready, 1)

                def copy_qy(g, s):
                    act.wait_ge(qy_done, g + 1)
                    if inside(g, 0, NB - 1):
                        if inside(g, 2, NB - 1):
                            act.wait_ge(scores_done, 2 * g - 2)
                        last = act.activation(qT[:, s], ps_qy[:, 0], ACT.Copy, scale=float(HD0) ** -0.5)
                        last.then_inc(qT_ready, 1)
                    if inside(g, 4, NB + 3):
                        act.activation(yT[:, :, bass.ds((g - 4) * P, P)], ps_qy[:, 1], ACT.Copy).then_inc(yT_ready, 1)

                def copy_out(b):
                    act.wait_ge(out_done, NQ * (b + 1))
                    if inside(b, 1, NB - 1):
                        act.wait_ge(out_turned, b)
                    act.activation(outT[:], ps_out[:].rearrange("p (q k) -> p q k", k=P), ACT.Copy).then_inc(outT_ready, 1)

                def step(b, u):
                    if inside(b, 1, NB):
                        copy_probT(b - 1, 0)
                        copy_probT(b - 1, 1)
                    if inside(b, 0, NB - 1):
                        exponentials(b, u % 2, 0)
                    if inside(b, 1, NB):
                        copy_probT(b - 1, 2)
                        copy_probT(b - 1, 3)
                    copy_qy(b + 1, (u + 1) % 2)
                    if inside(b, 1, NB):
                        copy_out(b - 1)
                    if inside(b, 0, NB - 1):
                        exponentials(b, u % 2, 1)

                copy_weights(act)
                copy_qy(0, 0)
                for b in range(UN):
                    step(b, b % UN)
                with act.Fori(1, NB // UN - 1) as i:
                    for u in range(UN):
                        step(UN * i + u, u)
                for b in range(NB - UN, NB + 3):
                    step(b, b % UN)
    return used


def feed_forward0(nc, yT, ymax, upT, gateT, downT, x1_dram, x2_dram, mv2, rstd2, b1T_dram, w2_dram, idle_dram, address,
                  wq_raw, wq_dram, finished):
    T = NB * P
    CH = BANK
    NC = T // CH
    COLS = NF * T
    UNIT = 2048
    NU = COLS // UNIT
    used = []
    with ExitStack() as stack:
        def sb(name, shape, dt=F32):
            return stack.enter_context(nc.sbuf_tensor("b_" + name, shape, dt))

        def sem(name):
            used.append(stack.enter_context(nc.semaphore("b_" + name)))
            return used[-1]

        act_sb = sb("act", [P, NF, T])
        up16 = sb("up16", [P, NF, T], I16)
        act_flat = act_sb[:].rearrange("p f t -> p (f t)")
        address["act"] = nc.sbuf_base - NF * T * (4 + 2)
        up_flat = up16[:].rearrange("p f t -> p (f t)")
        address["up16"] = nc.sbuf_base - NF * T * 2
        x_space = sb("x_space", [P, 8 * D])
        address["x_space"] = nc.sbuf_base - 8 * D * 4
        b1T = sb("b1T", [P, NE, FE // P])

        def parts(name, shape, place, words=0):
            return nc.alloc_sbuf_tensor_at("b_" + name, shape, F32R, offset=address[place] + 4 * words)

        up_parts = parts("up_high", [P, ND, FF], "up16"), parts("up_low", [P, ND, FF], "upT")
        inner = parts("inner", [P, 2, 2, NF, CH], "up16")
        spare = yT[:].rearrange("p k t -> p (k t)")
        y16_flat = spare[:, 0:T].bitcast(I16)
        y16 = y16_flat.rearrange("p (k c t) -> p c k t", k=ND, c=NC)
        y_first = parts("y_first", [P, 2, ND, CH], "act", 2 * CH)
        y16_first = act_flat[:, 6 * CH:7 * CH].bitcast(I16).rearrange("p (k t) -> p k t", k=ND)
        y_parts = parts("y_parts", [P, 2, 2, ND, CH], "yT", T)
        quant = spare[:, 0:UNIT].bitcast(I16).rearrange("p (s n) -> p s n", s=2)
        sig = spare[:, UNIT:3 * UNIT].rearrange("p (s n) -> p s n", s=2)
        idle = sig[0:1, 1].rearrange("p (e d) -> p e d", e=NE)
        inner16 = spare[:, 0:NF * CH].bitcast(I16).rearrange("p (s f t) -> p s f t", s=2, f=NF)
        down_parts = parts("down_high", [P, NF, D], "yT", 2 * T - NF * D), parts("down_low", [P, NF, D], "downT")
        gate_parts = parts("gate_high", [P, ND, FF], "x_space"), parts("gate_low", [P, ND, FF], "gateT")
        w2 = x_space[:].rearrange("p (h f d) -> p h f d", h=2, d=D)
        x1_sb, x2_sb = (x_space[:, n * 4 * D:(n + 1) * 4 * D].rearrange("p (s d) -> p s d", s=4) for n in range(2))

        pmax = sb("pmax", [P, NF * NC])
        one = sb("one", [P, 8, 1])
        factors = sb("factors", [P, 5, 2, 1])
        stats2 = sb("stats2", [P, NB, 6])
        var2 = sb("var2", [P, NB])
        power = sb("power", [P, NB])
        ps = stack.enter_context(nc.psum_tensor("b_ps", [P, 8, BANK], F32))

        consts = sem("consts")
        part_max = sem("part_max")
        all_max = sem("all_max")
        scalars = sem("scalars")
        scale_ready = sem("scale_ready")
        w_high = sem("w_high")
        w_ready = sem("w_ready")
        y_rounded = sem("y_rounded")
        y_high = sem("y_high")
        y_ready = sem("y_ready")
        product_done = sem("product_done")
        copied = sem("copied")
        max_done = sem("max_done")
        up_ready = sem("up_ready")
        even_quant = sem("even_quant")
        odd_quant = sem("odd_quant")
        sig_done = sem("sig_done")
        sig_rounded = sem("sig_rounded")
        silu_done = sem("silu_done")
        silu_quant = sem("silu_quant")
        inner_done = sem("inner_done")
        inner_rounded = sem("inner_rounded")
        inner_high = sem("inner_high")
        inner_ready = sem("inner_ready")
        down_done = sem("down_done")
        b1_loaded = sem("b1_loaded")
        relu_b1_ready = sem("relu_b1_ready")
        w2_loaded = [sem(f"w2_loaded{h}") for h in range(2)]
        idle_half = sem("idle_half")
        idle_ready = sem("idle_ready")
        idle_stored = sem("idle_stored")
        wq_loaded = sem("wq_loaded")
        x1_loaded = [sem(f"x1_loaded{s}") for s in range(4)]
        x2_ready = sem("x2_ready")
        x2_stored = [sem(f"x2_stored{s}") for s in range(4)]
        stats_done = sem("stats_done")
        mv_done = sem("mv_done")
        var_done = sem("var_done")
        rstd_done = sem("rstd_done")

        Y, UP, GATE, SILU, INNER = range(5)
        TILES = CH // P
        HF = FE // P // 2

        with nc.Block() as block:

            @block.sync
            def _(sp):
                def step(t, s):
                    if inside(t, 4, NB - 1):
                        sp.wait_ge(x2_ready, t - 3)
                    sp.dma_start(x1_sb[:, s, :], x1_dram[t]).then_inc(x1_loaded[s], 16)
                    if inside(t, 3, NB - 1):
                        store(t - 3, (s + 1) % 4)

                def store(t, s):
                    sp.wait_ge(x2_ready, t + 1)
                    sp.dma_start(x2_dram[t], x2_sb[:, s, :]).then_inc(x2_stored[s], 16)

                sp.dma_start(b1T[:], b1T_dram).then_inc(b1_loaded, 16)
                sp.wait_ge(product_done, 2 * NC * NF)
                for e in range(NE):
                    for h in range(2):
                        if e:
                            sp.wait_ge(idle_half, 2 * e - 1 + h)
                        sp.dma_start(w2[:, h], w2_dram[e][:, h * HF:(h + 1) * HF, :]).then_inc(w2_loaded[h], 16)
                sp.wait_ge(idle_ready, 1)
                sp.dma_start(idle_dram.unsqueeze(0), idle).then_inc(idle_stored, 16)
                sp.wait_ge(idle_stored, 16)
                sp.dma_start(wq_raw[:], wq_dram).then_inc(wq_loaded, 16)
                for t in range(4):
                    step(t, t)
                with sp.Fori(1, NB // 4) as i:
                    for s in range(4):
                        step(4 * i + s, s)
                for t in range(NB - 3, NB):
                    store(t, t % 4)
                sp.wait_ge(wq_loaded, 16)
                for s in range(4):
                    sp.wait_ge(x2_stored[s], 16 * NB // 4)

            @block.gpsimd
            def _(pool):
                pool.memset(power[:], -0.5).then_inc(consts, 1)
                for n in range(5):
                    pool.wait_ge(part_max, n + 1)
                    pool.partition_all_reduce(one[:, 1, :], one[:, 0, :], P, bass.bass_isa.ReduceOp.max)\
                        .then_inc(all_max, 1)
                    if n == 0:
                        for semaphore in finished:
                            pool.sem_clear(semaphore)
                pool.wait_ge(consts, 1)
                for n, (first, end) in enumerate(((0, NB - 2 * TILES), (NB - 2 * TILES, NB - TILES), (NB - TILES, NB))):
                    pool.wait_ge(mv_done, end)
                    part = slice(first, end)
                    pool.tensor_scalar(var2[:, part], mv2[:, part, 1], EPS, None, ALU.add).then_inc(var_done, 1)
                    pool.wait_ge(var_done, n + 1)
                    pool.tensor_tensor(rstd2[:, part], var2[:, part], power[:, part], ALU.pow).then_inc(rstd_done, 1)

            @block.tensor
            def _(pe):
                for m, w_parts in enumerate((up_parts, gate_parts)):
                    def chunk(c, s):
                        pe.wait_ge(y_ready, c + NC * m + 1)
                        for f in range(NF):
                            n = NF * (c + NC * m) + f
                            if inside(n, NF, 2 * NC * NF):
                                pe.wait_ge(copied, n - NF + 1)
                            first = isinstance(c, int) and (m, c) == (0, 0)
                            for j, (k, (a, b)) in enumerate(product(range(ND), PARTS)):
                                y_part = y_first[:, b, k, :] if first else y_parts[:, s, b, k, :]
                                last = pe.matmul(ps[:, f, :], w_parts[a][:, k, f * P:(f + 1) * P], y_part,
                                                 start=(j == 0), stop=(j == ND * len(PARTS) - 1))
                            last.then_inc(product_done, 1)

                    pe.wait_ge(w_ready, m + 1)
                    for c in range(2):
                        chunk(c, c)
                    with pe.Fori(1, NC // 2) as i:
                        for s in range(2):
                            chunk(2 * i + s, s)

                pe.wait_ge(relu_b1_ready, 1)
                pe.wait_ge(copied, 2 * NC * NF)
                for e in range(NE):
                    for h in range(2):
                        pe.wait_ge(w2_loaded[h], 16 * (e + 1))
                        for n in range(HF):
                            f = HF * h + n
                            last = pe.matmul(ps[:, e, 0:D], b1T[:, e, f:f + 1].to_broadcast([P, P]), w2[:, h, n, :],
                                             start=(f == 0), stop=(f == 2 * HF - 1))
                        last.then_inc(idle_half, 1)
                pe.wait_ge(idle_ready, 1)
                pe.wait_ge(w_ready, 3)

                def down(c, s):
                    first = isinstance(c, int) and c == 0
                    if not first:
                        pe.wait_ge(inner_ready, c + TILES)
                    for t in range(TILES):
                        n = TILES * c + t
                        if first:
                            pe.wait_ge(inner_ready, t + 1)
                        if inside(n, TILES, NB):
                            pe.wait_ge(x2_ready, n - TILES + 1)
                        for j, (f, (a, b)) in enumerate(product(range(NF), PARTS)):
                            last = pe.matmul(ps[:, t, 0:D], inner[:, s, a, f, t * P:(t + 1) * P],
                                             down_parts[b][:, f, :], start=(j == 0), stop=(j == NF * len(PARTS) - 1))
                        last.then_inc(down_done, 1)

                for c in range(2):
                    down(c, c)
                with pe.Fori(1, NC // 2) as i:
                    for s in range(2):
                        down(2 * i + s, s)

            @block.scalar
            def _(act):
                def round_weights(wT, parts):
                    act.activation(parts[0][:], wT[:], ACT.Copy).then_inc(w_high, 1)

                def high_y(n, s):
                    c = n % NC if isinstance(n, int) else n
                    act.activation(y_parts[:, s, 0], y16[:, c], ACT.Copy).then_inc(y_high, 1)

                def copy_chunk(c, m):
                    if m == 1:
                        act.wait_ge(up_ready, c + 1)
                    for f in range(NF):
                        act.wait_ge(product_done, NF * (c + NC * m) + f + 1)
                        act.activation(act_sb[:, f, bass.ds(c * CH, CH)], ps[:, f, :], ACT.Copy).then_inc(copied, 1)

                round_weights(upT, up_parts)
                act.wait_ge(y_rounded, 1)
                act.activation(y_first[:, 0], y16_first, ACT.Copy).then_inc(y_high, 1)
                round_weights(gateT, gate_parts)
                act.wait_ge(y_rounded, 2)
                high_y(1, 1)
                for m in range(2):
                    with act.Fori(0, NC // 2 - 1) as i:
                        for s in range(2):
                            copy_chunk(2 * i + s, m)
                            high_y(2 * i + s + 2, s)
                    for c in range(NC - 2, NC):
                        copy_chunk(c, m)
                        if m == 0:
                            high_y(c + 2, c % 2)
                round_weights(downT, down_parts)

                def sigmoid(u, s):
                    act.activation(sig[:, s, :], quant[:, s, :], ACT.Sigmoid, scale=factors[:, GATE, 0, :])\
                       .then_inc(sig_done, 1)
                    act.wait_ge(sig_done, u + 1)
                    act.activation(sig[:, s, :].bitcast(I32), sig[:, s, :], ACT.Copy, scale=65536.0).then_inc(sig_rounded, 1)

                def sigmoids(u, i):
                    act.wait_ge(even_quant, i + 1)
                    if inside(u, 2, NU):
                        act.wait_ge(silu_done, u - 1)
                    sigmoid(u, 0)
                    if inside(u, 2, NU):
                        act.wait_ge(silu_done, u)
                    act.activation(quant[:, 1, :], act_flat[:, bass.ds((u + 1) * UNIT, UNIT)], ACT.Copy,
                                   scale=factors[:, GATE, 1, :]).then_inc(odd_quant, 1)
                    act.wait_ge(odd_quant, i + 1)
                    sigmoid(u + 1, 1)

                act.wait_ge(scale_ready, GATE + 1)
                sigmoids(0, 0)
                with act.Fori(1, NU // 2) as i:
                    sigmoids(2 * i, i)

                act.wait_ge(idle_half, 2 * NE)
                act.wait_ge(silu_done, NU)
                act.activation(idle, ps[0:1, :, 0:D], ACT.Copy).then_inc(idle_ready, 1)

                def quantise_silu(u, s):
                    if inside(u, 2, NU):
                        act.wait_ge(inner_done, u - 1)
                    act.activation(quant[:, s, :], act_flat[:, bass.ds(u * UNIT, UNIT)], ACT.Copy,
                                   scale=factors[:, SILU, 1, :]).then_inc(silu_quant, 1)

                act.wait_ge(scale_ready, SILU + 1)
                for u in range(2):
                    quantise_silu(u, u)
                with act.Fori(1, NU // 2) as i:
                    for s in range(2):
                        quantise_silu(2 * i + s, s)

                def high_inner(c, s):
                    if inside(c, 2, NC):
                        act.wait_ge(inner_ready, c - 2 + TILES)
                        act.activation(inner16[:, s], act_sb[:, :, bass.ds(c * CH, CH)], ACT.Copy,
                                       scale=factors[:, INNER, 1, :]).then_inc(inner_rounded, 1)
                    act.wait_ge(inner_rounded, c + TILES)
                    if inside(c, 2, NC):
                        act.wait_ge(down_done, TILES * (c - 1))
                    act.activation(inner[:, s, 0], inner16[:, s], ACT.Copy).then_inc(inner_high, 1)

                for t in range(TILES):
                    act.wait_ge(inner_rounded, t + 1)
                    tok = slice(t * P, (t + 1) * P)
                    act.activation(inner[:, 0, 0, :, tok], inner16[:, 0, :, tok], ACT.Copy).then_inc(inner_high, 1)
                high_inner(1, 1)
                with act.Fori(1, NC // 2) as i:
                    for s in range(2):
                        high_inner(2 * i + s, s)

            @block.vector
            def _(dve):
                done = [0]

                def then(instruction):
                    done[0] += 1
                    instruction.then_inc(scalars, 1)
                    dve.wait_ge(scalars, done[0])

                def rest_of_weights(m, wT, parts):
                    dve.wait_ge(w_high, m + 1)
                    dve.tensor_tensor(parts[1][:], wT[:], parts[0][:].bitcast(F32), ALU.subtract).then_inc(w_ready, 1)

                def scale_of(n, maxima, unit, meanwhile=()):
                    dve.tensor_reduce(one[:, 0, :], maxima, AX_X, ALU.max).then_inc(part_max, 1)
                    for weights in meanwhile:
                        rest_of_weights(*weights)
                    dve.wait_ge(all_max, n + 1)
                    scale, factor = factors[:, n, 0, :], factors[:, n, 1, :]
                    if unit is None:
                        then(dve.tensor_scalar(scale, one[:, 1, :], 1.0 / A_MAX, TINY, ALU.mult, ALU.max))
                        dve.reciprocal(factor, scale).then_inc(scale_ready, 1)
                    else:
                        then(dve.tensor_scalar(one[:, 2, :], one[:, 1, :], unit, 1.0 / A_MAX, ALU.mult, ALU.mult))
                        then(dve.tensor_scalar(scale, one[:, 2, :], TINY, None, ALU.max))
                        then(dve.reciprocal(one[:, 3, :], scale))
                        dve.tensor_tensor(factor, one[:, 3, :], unit, ALU.mult).then_inc(scale_ready, 1)
                    dve.wait_ge(scale_ready, n + 1)

                def maxima_of_chunk(c, m):
                    for f in range(NF):
                        n = NF * c + f
                        dve.wait_ge(copied, n + NF * NC * m + 1)
                        dve.tensor_reduce(pmax[:, bass.ds(n, 1)], act_sb[:, f, bass.ds(c * CH, CH)], AX_X, ALU.max,
                                          apply_absolute_value=True).then_inc(max_done, 1)

                def low_y(n, s):
                    c = n % NC if isinstance(n, int) else n - NC * by_gate[0]
                    dve.wait_ge(y_high, n + 1)
                    dve.tensor_tensor(y_parts[:, s, 1], y16[:, c], y_parts[:, s, 0].bitcast(F32), ALU.subtract)\
                       .then_inc(y_ready, 1)

                def quantise_up(c):
                    part = bass.ds(c * CH, CH)
                    dve.tensor_scalar(up16[:, :, part], act_sb[:, :, part], factors[:, UP, 1, :], None, ALU.mult)\
                       .then_inc(up_ready, 1)

                by_gate = [0]
                scale_of(Y, ymax[:], None)
                dve.tensor_scalar(y16_first, yT[:, :, 0:CH], factors[:, Y, 1, :], None, ALU.mult).then_inc(y_rounded, 1)
                rest_of_weights(0, upT, up_parts)
                dve.wait_ge(y_high, 1)
                dve.tensor_tensor(y_first[:, 1], y16_first, y_first[:, 0].bitcast(F32), ALU.subtract).then_inc(y_ready, 1)
                dve.wait_ge(y_rounded, 1)
                then(dve.tensor_copy(y16_flat[:, 0:CH], y16_first[:, 0]))
                start = CH
                while start < ND * T:
                    step = dve.tensor_scalar(y16_flat[:, start:2 * start], spare[:, start:2 * start], factors[:, Y, 1, :], None,
                                             ALU.mult)
                    start *= 2
                    if start < ND * T:
                        then(step)
                step.then_inc(y_rounded, 1)
                dve.wait_ge(y_rounded, 2)
                low_y(1, 1)
                rest_of_weights(1, gateT, gate_parts)
                dve.wait_ge(b1_loaded, 16)
                dve.tensor_scalar(b1T[:], b1T[:], 0.0, None, ALU.max).then_inc(relu_b1_ready, 1)
                with dve.Fori(0, NC // 2 - 1) as i:
                    for s in range(2):
                        maxima_of_chunk(2 * i + s, 0)
                        low_y(2 * i + s + 2, s)
                for c in range(NC - 2, NC):
                    maxima_of_chunk(c, 0)
                    low_y(c + 2, c % 2)
                dve.wait_ge(max_done, NF * NC)
                scale_of(UP, pmax[:], factors[:, Y, 0, :])
                by_gate[0] = 1
                quantise_up(0)
                quantise_up(1)
                with dve.Fori(0, NC // 2 - 1) as i:
                    for s in range(2):
                        quantise_up(2 * i + s + 2)
                        maxima_of_chunk(2 * i + s, 1)
                        low_y(NC + 2 * i + s + 2, s)
                for c in range(NC - 2, NC):
                    maxima_of_chunk(c, 1)
                dve.wait_ge(max_done, 2 * NF * NC)
                scale_of(GATE, pmax[:], factors[:, Y, 0, :], [(2, downT, down_parts)])

                def quantise_even(u):
                    dve.tensor_scalar(quant[:, 0, :], act_flat[:, bass.ds(u * UNIT, UNIT)], factors[:, GATE, 1, :], None,
                                      ALU.mult).then_inc(even_quant, 1)

                def silu(u, s):
                    cols = act_flat[:, bass.ds(u * UNIT, UNIT)]
                    dve.wait_ge(sig_rounded, u + 1)
                    dve.scalar_tensor_tensor(cols, sig[:, s, :].bitcast(I32), 65535.0, quant[:, s, :], ALU.min, ALU.mult)\
                       .then_inc(silu_done, 1)
                    dve.wait_ge(silu_done, u + 1)
                    dve.tensor_reduce(pmax[:, bass.ds(u, 1)], cols, AX_X, ALU.max, apply_absolute_value=True)\
                       .then_inc(max_done, 1)

                quantise_even(0)
                with dve.Fori(0, NU // 2 - 1) as i:
                    silu(2 * i, 0)
                    quantise_even(2 * i + 2)
                    silu(2 * i + 1, 1)
                silu(NU - 2, 0)
                silu(NU - 1, 1)
                dve.wait_ge(max_done, 2 * NF * NC + NU)
                then(dve.tensor_scalar(one[:, 4, :], factors[:, GATE, 0, :], 1.0 / 65536.0, None, ALU.mult))
                scale_of(SILU, pmax[:, 0:NU], one[:, 4, :])

                def times_up(u, s):
                    cols = act_flat[:, bass.ds(u * UNIT, UNIT)]
                    dve.wait_ge(silu_quant, u + 1)
                    dve.tensor_tensor(cols, quant[:, s, :], up_flat[:, bass.ds(u * UNIT, UNIT)], ALU.mult)\
                       .then_inc(inner_done, 1)
                    dve.wait_ge(inner_done, u + 1)
                    dve.tensor_reduce(pmax[:, bass.ds(u, 1)], cols, AX_X, ALU.max, apply_absolute_value=True)\
                       .then_inc(max_done, 1)

                with dve.Fori(0, NU // 2) as i:
                    for s in range(2):
                        times_up(2 * i + s, s)
                dve.wait_ge(max_done, 2 * NF * NC + 2 * NU)
                then(dve.tensor_tensor(one[:, 5, :], factors[:, SILU, 0, :], factors[:, UP, 0, :], ALU.mult))
                scale_of(INNER, pmax[:, 0:NU], one[:, 5, :])

                def low_inner(c, s):
                    dve.wait_ge(inner_high, c + TILES)
                    dve.tensor_tensor(inner[:, s, 1], inner16[:, s], inner[:, s, 0].bitcast(F32), ALU.subtract)\
                       .then_inc(inner_ready, 1)

                def residual(t, s):
                    dve.wait_ge(down_done, t + 1)
                    dve.wait_ge(x1_loaded[s], 16 * (t // 4 + 1 if isinstance(t, int) else turn[0] + 1))
                    if inside(t, 4, NB - 1):
                        dve.wait_ge(x2_stored[s], 16 * (t // 4 if isinstance(t, int) else turn[0]))
                    dve.scalar_tensor_tensor(x2_sb[:, s, :], ps[:, s, 0:D], factors[:, INNER, 0, :],
                                             x1_sb[:, s, :], ALU.mult, ALU.add).then_inc(x2_ready, 1)
                    dve.wait_ge(all_max, 1)
                    dve.wait_ge(x2_ready, t + 1)
                    dve.bn_stats(stats2[:, t, :], x2_sb[:, s, :]).then_inc(stats_done, 1)

                def statistics(first, end):
                    dve.wait_ge(stats_done, end)
                    for t in range(first, end):
                        dve.bn_aggr(mv2[:, t, :], stats2[:, t, :]).then_inc(mv_done, 1)

                turn = [0]
                def chunk(c, s):
                    turn[0] = c
                    if inside(c, 0, NC - 2):
                        low_inner(c + 1, 1 - s)
                    for t in range(TILES):
                        residual(TILES * c + t, t)

                for t in range(TILES):
                    tok = slice(t * P, (t + 1) * P)
                    dve.tensor_scalar(inner16[:, 0, :, tok], act_sb[:, :, tok], factors[:, INNER, 1, :], None, ALU.mult)\
                       .then_inc(inner_rounded, 1)
                for t in range(TILES):
                    if t == 2:
                        dve.tensor_scalar(inner16[:, 1], act_sb[:, :, CH:2 * CH], factors[:, INNER, 1, :], None, ALU.mult)\
                           .then_inc(inner_rounded, 1)
                    dve.wait_ge(inner_high, t + 1)
                    tok = slice(t * P, (t + 1) * P)
                    dve.tensor_tensor(inner[:, 0, 1, :, tok], inner16[:, 0, :, tok], inner[:, 0, 0, :, tok].bitcast(F32),
                                      ALU.subtract).then_inc(inner_ready, 1)
                for c in range(2):
                    chunk(c, c)
                with dve.Fori(1, NC // 2 - 1) as i:
                    for s in range(2):
                        chunk(2 * i + s, s)
                statistics(0, NB - 2 * TILES)
                for c in range(NC - 2, NC):
                    chunk(c, c % 2)
                    statistics(TILES * c, TILES * (c + 1))
    return used


KD = 64
INNER_C = NH * KD


def attention1(nc, ident, mv2, rstd2, logits, wq_raw, wq_address, w, ctx_t, x2_dram, x3_dram, z_dram, finished):
    BLKS = INNER_C // P
    PT = 2 * P
    NU = NH // HB
    FIRST, LAST = -4, NB + 3
    with ExitStack() as stack:
        def sb(name, shape, dt=F32):
            return stack.enter_context(nc.sbuf_tensor("c_" + name, shape, dt))

        def psum(name, shape, dt=F32):
            return stack.enter_context(nc.psum_tensor("c_" + name, shape, dt))

        def sem(name):
            return stack.enter_context(nc.semaphore("c_" + name))

        ctx_raw = sb("ctx_raw", [P, 2, ND, PT])
        x2_early = sb("x2_early", [P, 4, D])
        x2_late = sb("x2_late", [P, 4, D])
        assert nc.sbuf_base == wq_address
        w_raw = sb("w_raw", [P, 2, ND * INNER_C])
        prob, probT = (w_raw[:, n].rearrange("p (n h k) -> p n h k", n=NU, h=HB) for n in range(2))
        wq = sb("wq", [P, 2, ND, INNER_C], F32R)
        wk = sb("wk", [P, 2, ND, INNER_C], F32R)
        wv = sb("wv", [P, 2, ND, INNER_C], F32R)
        wo = sb("wo", [P, 2, BLKS, D], F32R)
        wr = sb("wr", [P, ND, NE])
        bq = sb("bq", [P, BLKS])
        bk = sb("bk", [P, BLKS])
        bv = sb("bv", [P, INNER_C])
        bo = sb("bo", [P, D])
        gamma = sb("gamma", [P, D])
        beta = sb("beta", [P, D])
        br = sb("br", [P, NE])
        power = sb("power", [P, 1])
        ctxT = sb("ctxT", [P, 2, 2, ND, PT], F32R)
        xn = sb("xn", [P, 2, D])
        xnT = sb("xnT", [P, 2, 2, ND, PT], F32R)
        qT = sb("qT", [P, 2, BLKS, PT])
        kT = sb("kT", [P, 2, BLKS, PT])
        v = sb("v", [P, 2, 2, NH, KD])
        row_max = sb("row_max", [P, NU, HB])
        shift = sb("shift", [P, NU, HB])
        row_sum = sb("row_sum", [P, NU, HB])
        inv_sum = sb("inv_sum", [P, NU, HB])
        attnT = sb("attnT", [P, 2, 2, BLKS, P], F32R)
        eps = sb("eps", [P, 1])
        xn_bo = sb("xn_bo", [P, 2, D])
        proj = sb("proj", [P, 2, D])
        stats_o = sb("stats_o", [P, 2, 6])
        mv_o = sb("mv_o", [P, 2, 2])
        var_o = sb("var_o", [P, 2, 1])
        rstd_o = sb("rstd_o", [P, 2, 1])
        x3 = sb("x3", [P, 4, D])
        stats_3 = sb("stats_3", [P, 2, 6])
        mv_3 = sb("mv_3", [P, 2, 2])
        var_3 = sb("var_3", [P, 2, 1])
        rstd_3 = sb("rstd_3", [P, 2, 1])
        z = sb("z", [P, 4, D])
        zT = sb("zT", [P, 2, ND, P])

        ps_score = psum("ps_score", [P, 2, HB, P])
        ps_probT = psum("ps_probT", [P, 2, HB, P])
        ps_out = psum("ps_out", [P, HB, P])
        ps_proj = psum("ps_proj", [P, 2, BANK])
        ps_aux = psum("ps_aux", [P, BANK])

        w_loaded = [sem(f"w_loaded{s}") for s in range(2)]
        wr_loaded = sem("wr_loaded")
        w_rounded = sem("w_rounded")
        w_split = sem("w_split")
        ctx_rounded = sem("ctx_rounded")
        ctx_split = sem("ctx_split")
        xnT_rounded = sem("xnT_rounded")
        attnT_rounded = sem("attnT_rounded")
        bias_loaded = sem("bias_loaded")
        ctx_loaded = [sem(f"ctx_loaded{s}") for s in range(2)]
        early_loaded = [sem(f"early_loaded{s}") for s in range(4)]
        late_loaded = [sem(f"late_loaded{s}") for s in range(4)]
        x3_stored = [sem(f"x3_stored{s}") for s in range(4)]
        z_stored = [sem(f"z_stored{s}") for s in range(4)]
        consts = sem("consts")
        xn_ready = sem("xn_ready")
        xnT_done = sem("xnT_done")
        xnT_ready = sem("xnT_ready")
        proj_done = sem("proj_done")
        qk_ready = sem("qk_ready")
        v_ready = sem("v_ready")
        scores_done = sem("scores_done")
        max_done = sem("max_done")
        shift_ready = sem("shift_ready")
        prob_ready = sem("prob_ready")
        exp_done = sem("exp_done")
        probT_done = sem("probT_done")
        probT_ready = sem("probT_ready")
        out_done = sem("out_done")
        inv_done = sem("inv_done")
        attnT_ready = sem("attnT_ready")
        output_done = sem("output_done")
        proj_ready = sem("proj_ready")
        late_centred = sem("late_centred")
        late_norm = sem("late_norm")
        xn_bo_ready = sem("xn_bo_ready")
        x2_beta_ready = sem("x2_beta_ready")
        stats_o_done = sem("stats_o_done")
        mv_o_done = sem("mv_o_done")
        var_o_done = sem("var_o_done")
        rstd_o_done = sem("rstd_o_done")
        normed_done = sem("normed_done")
        scaled_done = sem("scaled_done")
        x3_ready = sem("x3_ready")
        stats_3_done = sem("stats_3_done")
        mv_3_done = sem("mv_3_done")
        var_3_done = sem("var_3_done")
        rstd_3_done = sem("rstd_3_done")
        z_ready = sem("z_ready")
        zT_done = sem("zT_done")
        zT_ready = sem("zT_ready")
        logits_done = sem("logits_done")
        logits_read = sem("logits_read")

        N_BIAS = 7
        projects = (-2, NB - 3)
        split_at = {(-4, 0): 0, (-3, 1): 1, (-2, 0): 2, (-2, 3): 3}

        def uses(t, turn):
            return t // 4 + 1 if isinstance(t, int) else turn

        def run_steps(engine, step, first=FIRST, last=LAST):
            for b in range(first, 8):
                step(b, b % 4, None)
            with engine.Fori(2, NB // 4 - 1) as i:
                for u in range(4):
                    step(4 * i + u, u, i)
            for b in range(NB - 4, last + 1):
                step(b, b % 4, None)

        with nc.Block() as block:

            @block.sync
            def _(sp):
                def early(t, s):
                    if inside(t, 4, NB - 1):
                        sp.wait_ge(xn_ready, t - 3)
                    sp.dma_start(x2_early[:, s, :], x2_dram[t]).then_inc(early_loaded[s], 16)

                def late(t, s):
                    if inside(t, 4, NB - 1):
                        sp.wait_ge(x3_ready, t - 3)
                    sp.dma_start(x2_late[:, s, :], x2_dram[t]).then_inc(late_loaded[s], 16)

                def context(pair, s):
                    if inside(pair, 2, NB // 2 - 1):
                        sp.wait_ge(ctx_split, pair - 1)
                    sp.dma_start(ctx_raw[:, s], ctx_t[:, :, bass.ds(pair * PT, PT)]).then_inc(ctx_loaded[s], 16)

                def step(b, u, i):
                    if inside(b, FIRST, NB - 5):
                        early(b + 4, u)
                    if inside(b, -2, NB - 3):
                        late(b + 2, (u + 2) % 4)
                    if u % 2 == 0 and inside(b, 0, NB - 5):
                        context(b // 2 + 2 if isinstance(b, int) else 2 * i + u // 2 + 2, (u // 2) % 2)
                    if inside(b, 3, NB + 2):
                        sp.wait_ge(x3_ready, b - 2)
                        sp.dma_start(x3_dram[b - 3], x3[:, (u + 1) % 4, :]).then_inc(x3_stored[(u + 1) % 4], 16)
                    if inside(b, 4, NB + 3):
                        sp.wait_ge(z_ready, b - 3)
                        sp.dma_start(z_dram[b - 4], z[:, u, :]).then_inc(z_stored[u], 16)

                def weights(m, name):
                    if m >= 2:
                        sp.wait_ge(w_split, m - 1)
                    sp.dma_start(w_raw[:, m % 2], w[name].rearrange("p k n -> p (k n)")).then_inc(w_loaded[m % 2], 16)

                for b in range(FIRST, 0):
                    step(b, b % 4, None)
                    if b == FIRST + 1:
                        weights(1, "wk")
                for dst, src in ((bq, w["bq"]), (bk, w["bk"])):
                    sp.dma_start(dst[:], src).then_inc(bias_loaded, 16)
                context(0, 0)
                for dst, src in ((bv, w["bv"]), (bo, w["bo"]), (gamma, w["gamma"]), (beta, w["beta"]), (br, w["br"])):
                    sp.dma_start(dst[:], src.partition_broadcast(P)).then_inc(bias_loaded, 16)
                sp.dma_start(wr[:], w["wr"]).then_inc(wr_loaded, 16)
                weights(2, "wv")
                context(1, 1)
                weights(3, "wo")
                run_steps(sp, step, 0)
                for s in range(4):
                    sp.wait_ge(x3_stored[s], 16 * NB // 4)
                    sp.wait_ge(z_stored[s], 16 * NB // 4)

            @block.gpsimd
            def _(pool):
                pool.memset(power[:], -0.5).then_inc(consts, 1)
                pool.memset(eps[:], EPS).then_inc(consts, 1)
                for semaphore in finished:
                    pool.sem_clear(semaphore)
                pool.wait_ge(consts, 2)
                pool.wait_ge(bias_loaded, 16 * N_BIAS)

                def residuals(t, u, i):
                    s = u % 2
                    pool.wait_ge(late_loaded[u], 16 * uses(t, None if i is None else i + 1))
                    if inside(t, 2, NB - 1):
                        pool.wait_ge(proj_ready, t - 1)
                    pool.tensor_tensor(xn_bo[:, s, :], x2_late[:, u, :], mv2[:, t, 0:1].to_broadcast([P, D]),
                                       ALU.subtract).then_inc(late_centred, 1)
                    pool.wait_ge(late_centred, t + 1)
                    pool.wait_ge(consts, 2)
                    pool.tensor_tensor(xn_bo[:, s, :], xn_bo[:, s, :], rstd2[:, bass.ds(t, 1)].to_broadcast([P, D]),
                                       ALU.mult).then_inc(late_norm, 1)
                    pool.wait_ge(late_norm, t + 1)
                    pool.tensor_tensor(xn_bo[:, s, :], xn_bo[:, s, :], bo[:], ALU.add).then_inc(xn_bo_ready, 1)
                    pool.tensor_tensor(x2_late[:, u, :], x2_late[:, u, :], beta[:], ALU.add).then_inc(x2_beta_ready, 1)

                def inverse_deviation(t, s, var, mv, rstd, mv_done, var_done, rstd_done):
                    pool.wait_ge(mv_done, t + 1)
                    pool.tensor_tensor(var[:, s], mv[:, s, 1:2], eps[:], ALU.add).then_inc(var_done, 1)
                    pool.wait_ge(var_done, t + 1)
                    pool.tensor_tensor(rstd[:, s], var[:, s], power[:], ALU.pow).then_inc(rstd_done, 1)

                def step(b, u, i):
                    if inside(b, 0, NB - 1):
                        residuals(b, u, i)
                    if inside(b, 2, NB + 1):
                        inverse_deviation(b - 2, u % 2, var_3, mv_3, rstd_3, mv_3_done, var_3_done, rstd_3_done)
                    if inside(b, 1, NB):
                        inverse_deviation(b - 1, (u + 1) % 2, var_o, mv_o, rstd_o, mv_o_done, var_o_done, rstd_o_done)

                run_steps(pool, step, 0, NB + 1)

            @block.tensor
            def _(pe):
                def scores(b, u, n):
                    g, r = divmod(n, 2)
                    s, tok = u // 2, slice((u % 2) * P, (u % 2 + 1) * P)
                    rows = slice(r * KD, (r + 1) * KD)
                    if n == 0 and u % 2 == 0:
                        pe.wait_ge(qk_ready, BLKS * (b + 2))
                    if inside(b, 1, NB) or n >= 2:
                        pe.wait_ge(exp_done, NU * b + n - 1)
                    for j in range(HB):
                        blk = HB * g + j
                        last = pe.matmul(ps_score[:, n % 2, j, :], qT[rows, s, blk, tok], kT[rows, s, blk, tok],
                                         start=True, stop=True)
                    last.then_inc(scores_done, 1)

                def transposes(b, n):
                    pe.wait_ge(prob_ready, NU * b + n + 1)
                    if inside(b, 1, NB) or n >= 2:
                        pe.wait_ge(probT_ready, NU * b + n - 1)
                    for j in range(HB):
                        last = pe.transpose(ps_probT[:, n % 2, j, :], prob[:, n, j, :], ident[:])
                    last.then_inc(probT_done, 1)

                def weighted(b, u, g):
                    pe.wait_ge(probT_ready, NU * b + 2 * g + 2)
                    if g == 0:
                        pe.wait_ge(v_ready, 2 * (b + 1))
                    if inside(b, 1, NB) or g >= 1:
                        pe.wait_ge(attnT_ready, 2 * b + g)
                    for j, r in product(range(HB), range(2)):
                        last = pe.matmul(ps_out[r * KD:(r + 1) * KD, j, :], v[:, u // 2, u % 2, 2 * (HB * g + j) + r, :],
                                         probT[:, 2 * g + r, j, :], start=True, stop=True)
                    last.then_inc(out_done, 1)

                def project(b, u, j, weights, src):
                    for h in range(2):
                        blk = HB * (u % 2) + 2 * j + h
                        for n, (k, (a, c)) in enumerate(product(range(ND), PARTS)):
                            last = pe.matmul(ps_proj[:, j, h * PT:(h + 1) * PT], weights[:, a, k, blk * P:(blk + 1) * P],
                                             src[:, c, k, :], start=(n == 0), stop=(n == ND * len(PARTS) - 1))
                    last.then_inc(proj_done, 1)

                def queries(b, u, j):
                    if inside(b, *projects):
                        if isinstance(b, int) and b == projects[0]:
                            pe.wait_ge(w_split, 1)
                        if j == 0 and u % 2 == 0:
                            pe.wait_ge(xnT_ready, b + 4)
                        if inside(b, -1, NB - 3):
                            pe.wait_ge(v_ready, 2 * b + 3 + j)
                        project(b, u, j, wq, xnT[:, 1 - u // 2])

                def keys(b, u, j, i):
                    if inside(b, *projects):
                        if j == 0 and u % 2 == 0:
                            pe.wait_ge(ctx_split, b // 2 + 2 if isinstance(b, int) else 2 * i + u // 2 + 2)
                        if isinstance(b, int) and b == projects[0]:
                            pe.wait_ge(w_split, 2)
                        pe.wait_ge(qk_ready, 8 * (b + 2) + 2 * (j + 1))
                        project(b, u, j, wk, ctxT[:, 1 - u // 2])

                def values(b, u, j):
                    if inside(b, *projects):
                        pe.wait_ge(qk_ready, 8 * (b + 2) + 4 + 2 * (j + 1))
                        tok = slice((u % 2) * P, (u % 2 + 1) * P)
                        if isinstance(b, int) and b == projects[0]:
                            pe.wait_ge(w_split, 3)
                        for n, (k, (a, c)) in enumerate(product(range(ND), PARTS)):
                            last = pe.matmul(ps_proj[:, j, :], ctxT[:, 1 - u // 2, a, k, tok],
                                             wv[:, c, k, j * BANK:(j + 1) * BANK],
                                             start=(n == 0), stop=(n == ND * len(PARTS) - 1))
                        last.then_inc(proj_done, 1)

                def bank_after_logits(b):
                    pe.wait_ge(logits_read, b - 3)

                def logits_of(t):
                    if isinstance(t, int) and t == 0:
                        pe.wait_ge(wr_loaded, 16)
                    pe.wait_ge(zT_ready, t + 1)
                    for k in range(ND):
                        last = pe.matmul(ps_aux[:, 0:NE], zT[:, 0, k, :], wr[:, k, :], start=(k == 0), stop=(k == ND - 1))
                    last.then_inc(logits_done, 1)

                def turn_x(b, u):
                    if inside(b, 4, NB - 5):
                        bank_after_logits(b)
                    elif inside(b, 2, 3):
                        pe.wait_ge(proj_ready, b - 1)
                    elif inside(b, FIRST + 1, 1):
                        pe.wait_ge(xnT_ready, b + 4)
                    pe.wait_ge(xn_ready, b + 5)
                    for k in range(ND):
                        last = pe.transpose(ps_aux[:, k * P:(k + 1) * P], xn[:, u % 2, k * P:(k + 1) * P], ident[:])
                    last.then_inc(xnT_done, 1)

                def output(b, u):
                    t, s = b - 1, (u + 1) % 2
                    if inside(b, FIRST, NB - 5):
                        pe.wait_ge(xnT_ready, b + 5)
                    else:
                        bank_after_logits(b)
                    pe.wait_ge(attnT_ready, 2 * t + 2)
                    if isinstance(b, int) and b == 1:
                        pe.wait_ge(w_split, 4)
                    for n, (blk, (a, c)) in enumerate(product(range(BLKS), PARTS)):
                        last = pe.matmul(ps_aux[:, 0:D], attnT[:, s, a, blk, :], wo[:, c, blk, :],
                                         start=(n == 0), stop=(n == BLKS * len(PARTS) - 1))
                    last.then_inc(output_done, 1)

                def turn_z(b, u):
                    pe.wait_ge(proj_ready, min(b - 1, NB) if isinstance(b, int) else b - 1)
                    if not inside(b, FIRST, NB + 1):
                        bank_after_logits(b - 1)
                    pe.wait_ge(z_ready, b - 3)
                    for k in range(ND):
                        last = pe.transpose(ps_aux[:, k * P:(k + 1) * P], z[:, u, k * P:(k + 1) * P], ident[:])
                    last.then_inc(zT_done, 1)

                def step(b, u, i):
                    for n in range(NU):
                        p, pu, pn = (b, u, n - 1) if n else (b - 1, (u - 1) % 4, NU - 1)
                        if inside(b, 0, NB - 1):
                            scores(b, u, n)
                        if n == 1 and inside(b, FIRST, NB - 5):
                            turn_x(b, u)
                        if n == 0:
                            queries(b, u, 0)
                            if inside(b, 4, NB + 3):
                                turn_z(b, u)
                        elif n == 1:
                            keys(b, u, 0, i)
                        elif n == 3:
                            values(b, u, 1)
                        if inside(p, 0, NB - 1):
                            transposes(p, pn)
                        if n == 0:
                            queries(b, u, 1)
                            if inside(b, 4, NB + 3):
                                logits_of(b - 4)
                        elif n == 1:
                            keys(b, u, 1, i)
                        elif n == 2:
                            values(b, u, 0)
                        elif inside(b, 1, NB):
                            output(b, u)
                        if n == 0 and inside(b, 1, NB):
                            weighted(b - 1, (u - 1) % 4, 1)
                        elif n == 2 and inside(b, 0, NB - 1):
                            weighted(b, u, 0)

                run_steps(pe, step)

            @block.vector
            def _(dve):
                def normalise(t, u, i):
                    s = u % 2
                    dve.wait_ge(early_loaded[u], 16 * uses(t, None if i is None else i))
                    if inside(t, 2, NB - 1):
                        dve.wait_ge(xnT_done, t - 1)
                    dve.tensor_scalar(xn[:, s, :], x2_early[:, u, :], mv2[:, t, 0:1], rstd2[:, bass.ds(t, 1)],
                                      ALU.subtract, ALU.mult).then_inc(xn_ready, 1)

                def maxima(b, n):
                    m = NU * b + n + 1
                    dve.wait_ge(scores_done, m)
                    dve.tensor_reduce(row_max[:, n, :], ps_score[:, n % 2], AX_X, ALU.max).then_inc(max_done, 1)
                    dve.wait_ge(max_done, m)
                    dve.tensor_scalar(shift[:, n, :], row_max[:, n, :], -float(KD) ** -0.5, None, ALU.mult)\
                       .then_inc(shift_ready, 1)

                def divide(b, n):
                    m = NU * b + n + 1
                    dve.wait_ge(exp_done, m)
                    dve.reciprocal(inv_sum[:, n, :], row_sum[:, n, :]).then_inc(inv_done, 1)
                    dve.wait_ge(inv_done, m)
                    dve.tensor_tensor(prob[:, n], prob[:, n], inv_sum[:, n, :].unsqueeze(2).to_broadcast([P, HB, P]),
                                      ALU.mult).then_inc(prob_ready, 1)

                def copy_values(b, u, j):
                    dve.wait_ge(proj_done, 6 * (b + 2) + 5 + j)
                    heads = slice(j * NH // 2, (j + 1) * NH // 2)
                    dve.tensor_tensor(v[:, 1 - u // 2, u % 2, heads, :],
                                      ps_proj[:, j, :].rearrange("p (h w) -> p h w", w=KD),
                                      bv[:, j * BANK:(j + 1) * BANK].rearrange("p (h w) -> p h w", w=KD),
                                      ALU.add).then_inc(v_ready, 1)

                def split_x(b, u):
                    dve.wait_ge(xnT_rounded, b + 5)
                    tok = slice((u % 2) * P, (u % 2 + 1) * P)
                    dve.tensor_tensor(xnT[:, u // 2, 1, :, tok], ps_aux[:, 0:D].rearrange("p (k t) -> p k t", t=P),
                                      xnT[:, u // 2, 0, :, tok], ALU.subtract).then_inc(xnT_ready, 1)

                def split_context(b, u):
                    s = (b + 3) // 2 % 2 if isinstance(b, int) else u // 2
                    dve.wait_ge(ctx_rounded, (b + 3) // 2 + 1 if isinstance(b, int) else 2 * turn_of_loop[0] + u // 2 + 3)
                    dve.tensor_tensor(ctxT[:, s, 1], ctx_raw[:, s], ctxT[:, s, 0], ALU.subtract).then_inc(ctx_split, 1)

                def split_attn(t, s, half):
                    dve.wait_ge(attnT_rounded, 2 * t + half + 1)
                    blks = slice(HB * half, HB * (half + 1))
                    dve.tensor_tensor(attnT[:, s, 1, blks, :], ps_out[:],
                                      attnT[:, s, 0, blks, :], ALU.subtract).then_inc(attnT_ready, 1)

                def rest_of_weights(m):
                    dve.wait_ge(w_rounded, m + 1)
                    high, low = ((wq, wk, wv, wo)[m][:, n].rearrange("p k n -> p (k n)") for n in range(2))
                    raw = w_raw[:, m % 2] if m else wq_raw[:].rearrange("p k n -> p (k n)")
                    dve.tensor_tensor(low, raw, high, ALU.subtract).then_inc(w_split, 1)

                turn_of_loop = [None]

                def route(t):
                    dve.wait_ge(logits_done, t + 1)
                    dve.tensor_tensor(logits[:, t, :], ps_aux[:, 0:NE], br[:], ALU.add).then_inc(logits_read, 1)

                def add_residual(t, s):
                    dve.wait_ge(output_done, t + 1)
                    dve.wait_ge(xn_bo_ready, t + 1)
                    dve.tensor_tensor(proj[:, s, :], ps_aux[:, 0:D], xn_bo[:, s, :], ALU.add).then_inc(proj_ready, 1)

                def output_statistics(t, s):
                    dve.wait_ge(proj_ready, t + 1)
                    dve.bn_stats(stats_o[:, s, :], proj[:, s, :]).then_inc(stats_o_done, 1)
                    dve.wait_ge(consts, 2)
                    dve.wait_ge(stats_o_done, t + 1)
                    dve.bn_aggr(mv_o[:, s, :], stats_o[:, s, :]).then_inc(mv_o_done, 1)

                def normalise_output(t, u, i):
                    s = u % 2
                    dve.wait_ge(rstd_o_done, t + 1)
                    dve.tensor_scalar(proj[:, s, :], proj[:, s, :], mv_o[:, s, 0:1], rstd_o[:, s, :],
                                      ALU.subtract, ALU.mult).then_inc(normed_done, 1)
                    dve.wait_ge(normed_done, t + 1)
                    dve.tensor_tensor(proj[:, s, :], proj[:, s, :], gamma[:], ALU.mult).then_inc(scaled_done, 1)
                    dve.wait_ge(scaled_done, t + 1)
                    dve.wait_ge(x2_beta_ready, t + 1)
                    if inside(t, 4, NB - 1):
                        dve.wait_ge(x3_stored[u], 16 * (uses(t, i) - 1))
                    dve.tensor_tensor(x3[:, u, :], proj[:, s, :], x2_late[:, u, :], ALU.add).then_inc(x3_ready, 1)
                    dve.wait_ge(x3_ready, t + 1)
                    dve.bn_stats(stats_3[:, s, :], x3[:, u, :]).then_inc(stats_3_done, 1)
                    dve.wait_ge(consts, 2)
                    dve.wait_ge(stats_3_done, t + 1)
                    dve.bn_aggr(mv_3[:, s, :], stats_3[:, s, :]).then_inc(mv_3_done, 1)

                def normalise_routed(t, u, i):
                    s = u % 2
                    dve.wait_ge(rstd_3_done, t + 1)
                    if inside(t, 4, NB - 1):
                        dve.wait_ge(z_stored[u], 16 * (uses(t, i) - 1))
                    dve.tensor_scalar(z[:, u, :], x3[:, u, :], mv_3[:, s, 0:1], rstd_3[:, s, :],
                                      ALU.subtract, ALU.mult).then_inc(z_ready, 1)

                def step(b, u, i):
                    turn = [None if i is None else (i + 1 if u >= k else i) for k in range(4)]
                    turn_of_loop[0] = i
                    if isinstance(b, int) and b == projects[0]:
                        dve.wait_ge(bias_loaded, 16 * N_BIAS)
                    if inside(b, FIRST, NB - 5):
                        normalise(b + 4, u, None if i is None else i + 2)
                    for n in range(NU):
                        if inside(b, 0, NB - 1):
                            maxima(b, n)
                        if n == 1 and inside(b, FIRST, NB - 5):
                            split_x(b, u)
                        if n == 0:
                            if inside(b, 2, NB + 1):
                                normalise_output(b - 2, (u + 2) % 4, turn[2])
                            if inside(b, 4, NB + 3):
                                route(b - 4)
                        elif n == 2:
                            if inside(b, *projects):
                                copy_values(b, u, 0)
                        elif n == 3:
                            if inside(b, 0, NB - 1):
                                split_attn(b, u % 2, 0)
                            if inside(b, *projects):
                                copy_values(b, u, 1)
                            if u % 2 == 1 and inside(b, -3, NB - 5):
                                split_context(b, u)
                        if inside(b, 0, NB - 1):
                            divide(b, n)
                        if n == 1 and inside(b, 1, NB):
                            split_attn(b - 1, (u + 1) % 2, 1)
                        if n == 1 and inside(b, 3, NB + 2):
                            normalise_routed(b - 3, (u + 1) % 4, turn[3])
                        elif n == 3 and inside(b, 1, NB):
                            add_residual(b - 1, (u + 1) % 2)
                        if isinstance(b, int) and (b, n) in split_at:
                            rest_of_weights(split_at[b, n])
                    if inside(b, 1, NB):
                        output_statistics(b - 1, (u + 1) % 2)

                run_steps(dve, step)

            @block.scalar
            def _(act):
                def exponentials(b, n):
                    m = NU * b + n + 1
                    act.wait_ge(shift_ready, m)
                    if inside(b, 1, NB):
                        act.wait_ge(probT_done, m - NU)
                    for j in range(HB):
                        last = act.activation(prob[:, n, j, :], ps_score[:, n % 2, j, :], ACT.Exp, scale=float(KD) ** -0.5,
                                              bias=shift[:, n, j:j + 1], accum_out=row_sum[:, n, j:j + 1])
                    last.then_inc(exp_done, 1)

                def round_weights(m):
                    if m:
                        act.wait_ge(w_loaded[m % 2], 16 * ((m + 1) // 2))
                    raw = w_raw[:, m % 2] if m else wq_raw[:].rearrange("p k n -> p (k n)")
                    act.activation((wq, wk, wv, wo)[m][:, 0].rearrange("p k n -> p (k n)"), raw, ACT.Copy).then_inc(w_rounded, 1)

                def copy_probT(b, n):
                    m = NU * b + n + 1
                    act.wait_ge(probT_done, m)
                    if inside(b, 1, NB):
                        act.wait_ge(out_done, 2 * b + n // 2 - 1)
                    act.activation(probT[:, n], ps_probT[:, n % 2], ACT.Copy).then_inc(probT_ready, 1)

                def copy_projection(b, u, j, dst, bias, n):
                    if inside(b, *projects):
                        act.wait_ge(proj_done, 6 * (b + 2) + n + j + 1)
                        for h in range(2):
                            blk = HB * (u % 2) + 2 * j + h
                            act.activation(dst[:, 1 - u // 2, blk, :], ps_proj[:, j, h * PT:(h + 1) * PT], ACT.Identity,
                                           bias=bias[:, blk:blk + 1]).then_inc(qk_ready, 1)

                def copy_x(b, u):
                    act.wait_ge(xnT_done, b + 5)
                    tok = slice((u % 2) * P, (u % 2 + 1) * P)
                    if inside(b, 0, NB - 5):
                        act.wait_ge(proj_done, 6 * b)
                    act.activation(xnT[:, u // 2, 0, :, tok], ps_aux[:, 0:D].rearrange("p (k t) -> p k t", t=P),
                                   ACT.Copy).then_inc(xnT_rounded, 1)

                def round_context(b, u, i):
                    if isinstance(b, int):
                        s, uses = (b + 3) // 2 % 2, (b + 3) // 4 + 1
                    else:
                        s, uses = u // 2, i + 2
                    act.wait_ge(ctx_loaded[s], 16 * uses)
                    if inside(b, 1, NB - 5):
                        act.wait_ge(proj_done, 6 * (b + 1))
                    act.activation(ctxT[:, s, 0], ctx_raw[:, s], ACT.Copy).then_inc(ctx_rounded, 1)

                def copy_attn(t, s, half):
                    act.wait_ge(out_done, 2 * t + half + 1)
                    if inside(t, 2, NB - 1):
                        act.wait_ge(output_done, t - 1)
                    act.activation(attnT[:, s, 0, HB * half:HB * (half + 1), :],
                                   ps_out[:], ACT.Copy).then_inc(attnT_rounded, 1)

                def copy_z(t):
                    act.wait_ge(zT_done, t + 1)
                    act.activation(zT[:, 0], ps_aux[:, 0:D].rearrange("p (k t) -> p k t", t=P), ACT.Copy).then_inc(zT_ready, 1)

                def step(b, u, i):
                    if isinstance(b, int) and b == projects[0]:
                        act.wait_ge(bias_loaded, 16 * N_BIAS)
                    for n in range(NU):
                        p, pn = (b, n - 1) if n else (b - 1, NU - 1)
                        if n == 0:
                            copy_projection(b, u, 0, qT, bq, 0)
                            if inside(b, 4, NB + 3):
                                copy_z(b - 4)
                        elif n == 3 and inside(b, 0, NB - 1):
                            copy_attn(b, u % 2, 0)
                        if n % 2 == 0 and inside(p, 0, NB - 1):
                            copy_probT(p, pn)
                        if inside(b, 0, NB - 1):
                            exponentials(b, n)
                        if n == 0:
                            copy_projection(b, u, 1, qT, bq, 0)
                            if inside(b, FIRST, NB - 5):
                                copy_x(b, u)
                        elif n == 1:
                            copy_projection(b, u, 0, kT, bk, 2)
                        if n % 2 == 1 and inside(p, 0, NB - 1):
                            copy_probT(p, pn)
                        if n == 1:
                            if inside(b, 1, NB):
                                copy_attn(b - 1, (u + 1) % 2, 1)
                            copy_projection(b, u, 1, kT, bk, 2)
                        if n == 2 and u % 2 == 1 and inside(b, -3, NB - 5):
                            round_context(b, u, i)
                        if isinstance(b, int) and split_at.get((b, n)):
                            round_weights(split_at[b, n])

                round_weights(0)
                run_steps(act, step)


NT = NB + NE - 1
NS = 3
EARLY = 2
assert NT % NS == 0


def experts(nc, ident, logits, idle_dram, w, z_dram, x3_dram, out):
    FB = FE // P
    TOKENS = NB * P
    with ExitStack() as stack:
        def sb(name, shape, dt=F32):
            return stack.enter_context(nc.sbuf_tensor("d_" + name, shape, dt))

        def psum(name, shape, dt=F32):
            return stack.enter_context(nc.psum_tensor("d_" + name, shape, dt))

        def sem(name):
            return stack.enter_context(nc.semaphore("d_" + name))

        w1 = sb("w1", [P, NE, ND, FE])
        w2 = sb("w2", [P, NE, FB, D])
        w1_tile = sb("w1_tile", [P, 2, ND, FE // 2])
        b1T = sb("b1T", [P, NE, FB])
        idle = sb("idle", [P, NE, D])
        b2 = sb("b2", [P, NE, D])
        w2_parts = nc.alloc_sbuf_tensor_at("d_w2_parts", [P, 2, 2, FB // 2, D], F32R, offset=nc.sbuf_base - 2 * NE * D * 4)
        idle_sum = sb("idle_sum", [P, D])
        other = sb("other", [P, NE, D])
        before = sb("before", [P, P], BF16)
        ones = sb("ones", [P, P], BF16)
        h = sb("h", [P, FB, P])
        pairs = h[:].rearrange("p f t -> p (f t)").rearrange("p (e d) -> p e d", d=D)
        hT = sb("hT", [P, NS, 2, FB, P], F32R)

        early_at = [nc.sbuf_base - NS * 2 * FB * P * 4]

        def early(name, shape, dt=F32):
            tensor = nc.alloc_sbuf_tensor_at("d_" + name, shape, dt, offset=early_at[0])
            early_at[0] += prod(shape[1:]) * 4
            return tensor

        is_top = early("is_top", [P, NB, NE])
        first_top = early("first_top", [P, NB, NE])
        onehot = early("onehot", [P, NB, NE], BF16)
        fills = early("fills", [P, NE, NB])
        place = early("place", [P, NB, NE])
        ends_before = early("ends_before", [P, NT, NE])
        IN = NB // 4
        at_row = early("at_row", [P, NB, P], BF16)
        reverse = sb("reverse", [P, NE])
        starts = sb("starts", [P, NB])
        numbers = sb("numbers", [P, P])
        tile_no = numbers[:, 0:NT]
        numbers16 = sb("numbers16", [P, P], BF16)
        iota = sb("iota", [P, P], I32)
        top = sb("top", [P, NB])
        choice = sb("choice", [P, NB])
        totals = sb("totals", [P, NE])
        tiles = sb("tiles", [P, NE])
        tile_end = sb("tile_end", [P, NE])
        base = sb("base", [P, NE])
        slot_f = sb("slot_f", [P, NB])
        slot = sb("slot", [P, NB], I32)
        slot_tile = sb("slot_tile", [P, NB], I32)
        slot_row = sb("slot_row", [P, NB], I32)
        slot_tile_f = sb("slot_tile_f", [P, NB], BF16)
        slot_row_f = sb("slot_row_f", [P, NB], BF16)
        token_iota = sb("token_iota", [P, 1], I32)
        token_no = sb("token_no", [P, 1])
        slot_token = sb("slot_token", [P, NT])
        tile_expert_f = sb("tile_expert_f", [P, NT])
        tile_expert = sb("tile_expert", [P, NT], I32)
        no_token = sb("no_token", [P, NT])
        ids = sb("ids", [P, NT], I32)
        z_ids = sb("z_ids", [P, NS], I32)
        x3_ids = sb("x3_ids", [P, NS], I32)
        out_ids = sb("out_ids", [P, NS], I32)
        z = sb("z", [P, NS, D])
        x3 = sb("x3", [P, NS, D])
        zT = sb("zT", [P, NS, ND, P])
        res = sb("res", [P, NS, D])
        at_tile = w1_tile[:].rearrange("p c k f -> p (c k f)").bitcast(BF16)[:, 0:NB * 2 * NT]\
            .rearrange("p (t n j) -> p t n j", n=2, j=NT)

        ps_count = psum("ps_count", [P, BANK])
        ps_rank = psum("ps_rank", [P, BANK])
        ps_hT = psum("ps_hT", [P, FB, P])
        ps_y = psum("ps_y", [P, BANK])
        ps_zT = psum("ps_zT", [P, BANK])
        ps_ids = psum("ps_ids", [P, BANK])

        weights_loaded = [sem(f"weights_loaded{e}") for e in range(NE)]
        experts_loaded = sem("experts_loaded")
        bias_loaded = sem("bias_loaded")
        consts = sem("consts")
        chain = sem("chain")
        onehot_ready = sem("onehot_ready")
        counted = sem("counted")
        ranked = sem("ranked")
        at_tile_ready = sem("at_tile_ready")
        at_row_ready = sem("at_row_ready")
        tokens_placed = sem("tokens_placed")
        ids_ready = sem("ids_ready")
        tile_expert_ready = sem("tile_expert_ready")
        z_gathered = [sem(f"z_gathered{s}") for s in range(NS)]
        x3_gathered = [sem(f"x3_gathered{s}") for s in range(NS)]
        z_turned = sem("z_turned")
        z_ids_ready = sem("z_ids_ready")
        x3_ids_ready = sem("x3_ids_ready")
        out_ids_ready = sem("out_ids_ready")
        zT_ready = sem("zT_ready")
        w1_ready = sem("w1_ready")
        h_done = sem("h_done")
        h_ready = sem("h_ready")
        h_high = sem("h_high")
        hT_ready = sem("hT_ready")
        w2_high = sem("w2_high")
        w2_ready = sem("w2_ready")
        w2_used = sem("w2_used")
        summed = sem("summed")
        other_ready = sem("other_ready")
        y_read = sem("y_read")
        res_ready = sem("res_ready")
        out_stored = [sem(f"out_stored{s}") for s in range(NS)]

        def run_tiles(engine, step, last=NT - 1):
            for j in range(2 * NS):
                step(j, j % NS, j // NS)
            with engine.Fori(2, NT // NS - 1) as i:
                for s in range(NS):
                    step(NS * i + s, s, i)
            for j in range(NT - NS, last + 1):
                step(j, j % NS, j // NS)

        def expert_of(engine, j):
            return engine.value_load(tile_expert[0:1, bass.ds(j, 1)], min_val=0, max_val=NE - 1)

        with nc.Block() as block:

            @block.sync
            def _(sp):
                for dst, src in ((b1T, w["b1T"]), (b2, w["b2"].partition_broadcast(P)), (idle, idle_dram.partition_broadcast(P))):
                    sp.dma_start(dst[:], src).then_inc(bias_loaded, 16)
                def load(e):
                    sp.dma_start(w1[:, e], w["w1"][e]).then_inc(weights_loaded[e], 16)
                    sp.dma_start(w2[:, e], w["w2"][e]).then_inc(weights_loaded[e], 16)

                for e in range(EARLY):
                    load(e)
                for e in range(NE):
                    sp.wait_ge(weights_loaded[e], 32)
                    sp.sem_inc(experts_loaded, 1)
                    if EARLY - 1 <= e < NE - 1:
                        sp.wait_ge(z_gathered[1], 16)
                        load(e + 1)

            @block.gpsimd
            def _(pool):
                pool.iota(iota[:], pattern=[[1, P]], base=0, channel_multiplier=0).then_inc(consts, 1)
                pool.wait_ge(consts, 1)
                pool.tensor_copy(numbers[:], iota[:]).then_inc(consts, 1)
                pool.wait_ge(consts, 2)
                pool.tensor_scalar(reverse[:], numbers[:, 0:NE], -1.0, float(NE), ALU.mult, ALU.add).then_inc(consts, 1)
                pool.memset(ones[:], 1.0).then_inc(consts, 1)
                pool.memset(before[:], 1.0).then_inc(consts, 1)
                pool.iota(token_iota[:], pattern=[[1, 1]], base=1, channel_multiplier=1).then_inc(consts, 1)
                pool.wait_ge(consts, 6)
                pool.affine_select(out=before[:], in_=before[:], compare_op=ALU.is_gt, fill=0.0, base=0,
                                   pattern=[[1, P]], channel_multiplier=-1).then_inc(consts, 1)
                pool.tensor_scalar(starts[:], numbers[:, 0:NB], float(P), None, ALU.mult).then_inc(consts, 1)
                pool.tensor_copy(token_no[:], token_iota[:]).then_inc(consts, 1)
                pool.tensor_copy(numbers16[:], iota[:]).then_inc(consts, 1)
                pool.memset(z[:], 0.0).then_inc(consts, 1)
                pool.memset(x3[:], 0.0).then_inc(consts, 1)
                pool.wait_ge(consts, 12)

                pool.wait_ge(bias_loaded, 48)
                pool.tensor_tensor(other[:], idle[:], b2[:], ALU.add).then_inc(summed, 1)
                pool.wait_ge(summed, 1)
                pool.tensor_tensor(pairs[:, 0:4], other[:, 0:4], other[:, 4:8], ALU.add).then_inc(summed, 1)
                pool.wait_ge(summed, 2)
                pool.tensor_tensor(pairs[:, 0:2], pairs[:, 0:2], pairs[:, 2:4], ALU.add).then_inc(summed, 1)
                pool.wait_ge(summed, 3)
                pool.tensor_tensor(idle_sum[:], pairs[:, 0], pairs[:, 1], ALU.add).then_inc(summed, 1)

                last_token = pool.to_reg(TOKENS - 1)

                def held(value):
                    return value if isinstance(value, int) else pool.to_reg(value)

                def gather_z(j, s, i):
                    ready, back, uses = held(j + 1), held(j - NS + 1), held(16 * i)
                    pool.wait_ge(ids_ready, 1)
                    if inside(j, NS, NT - 1):
                        pool.wait_ge(z_turned, back)
                        pool.wait_ge(z_gathered[s], uses)
                    pool.tensor_copy(z_ids[:, s:s + 1], ids[:, bass.ds(j, 1)]).then_inc(z_ids_ready, 1)
                    pool.wait_ge(ids_ready, 1)
                    pool.wait_ge(z_ids_ready, ready)
                    index = bass.IndirectOffsetOnAxis(z_ids[:, s:s + 1].bitcast(U32), 0)
                    pool.indirect_dma_start(z[:, s, :], None, z_dram, index, bounds_check=last_token, oob_is_err=False)\
                        .then_inc(z_gathered[s], 16)

                def gather_x3(j, s, i):
                    ready, back, uses = held(j + 1), held(j - NS + 1), held(16 * i)
                    pool.wait_ge(ids_ready, 1)
                    if inside(j, NS, NT - 1):
                        pool.wait_ge(res_ready, back)
                        pool.wait_ge(x3_gathered[s], uses)
                    pool.tensor_copy(x3_ids[:, s:s + 1], ids[:, bass.ds(j, 1)]).then_inc(x3_ids_ready, 1)
                    pool.wait_ge(ids_ready, 1)
                    pool.wait_ge(x3_ids_ready, ready)
                    index = bass.IndirectOffsetOnAxis(x3_ids[:, s:s + 1].bitcast(U32), 0)
                    pool.indirect_dma_start(x3[:, s, :], None, x3_dram, index, bounds_check=last_token, oob_is_err=False)\
                        .then_inc(x3_gathered[s], 16)

                def scatter(j, s, i):
                    ready, uses = held(j + 1), held(16 * i)
                    pool.wait_ge(ids_ready, 1)
                    if inside(j, NS, NT - 1):
                        pool.wait_ge(out_stored[s], uses)
                    pool.tensor_copy(out_ids[:, s:s + 1], ids[:, bass.ds(j, 1)]).then_inc(out_ids_ready, 1)
                    pool.wait_ge(ids_ready, 1)
                    pool.wait_ge(out_ids_ready, ready)
                    pool.wait_ge(res_ready, ready)
                    index = bass.IndirectOffsetOnAxis(out_ids[:, s:s + 1].bitcast(U32), 0)
                    pool.indirect_dma_start(out, index, res[:, s, :], None, bounds_check=last_token, oob_is_err=False)\
                        .then_inc(out_stored[s], 16)

                def step(j, s, i):
                    if inside(j, 0, NT - NS):
                        gather_z(j + 2, (s + 2) % NS, i if s == 0 else i + 1)
                    if inside(j, 0, NT - 1):
                        gather_x3(j, s, i)
                    if inside(j, 2, NT + 1):
                        scatter(j - 2, (s + 1) % NS, i if s == 2 else i - 1)

                gather_z(0, 0, 0)
                gather_z(1, 1, 0)
                run_tiles(pool, step, NT + 1)
                for s in range(NS):
                    pool.wait_ge(out_stored[s], 16 * (NT // NS))

            @block.tensor
            def _(pe):
                pe.wait_ge(consts, 7)
                pe.wait_ge(onehot_ready, 1)
                flat = onehot[:].rearrange("p t e -> p (t e)")
                pe.matmul(ps_count[:, 0:NB * NE], ones[:], flat, start=True, stop=True).then_inc(counted, 1)
                pe.matmul(ps_rank[:, 0:NB * NE], before[:], flat, start=True, stop=False)
                for t in range(NB - 1):
                    last = pe.matmul(ps_rank[:, (t + 1) * NE:NB * NE], ones[:],
                                     onehot[:, t:t + 1, :].to_broadcast([P, NB - 1 - t, NE]), start=False, stop=(t == NB - 2))
                last.then_inc(ranked, 1)
                pe.wait_ge(at_tile_ready, 1)
                for t in range(NB):
                    if t % IN == 0:
                        pe.wait_ge(at_row_ready, t // IN + 1)
                    last = pe.matmul(ps_ids[:, 0:2 * NT], at_row[:, t, :], at_tile[:, t].rearrange("p n j -> p (n j)"),
                                     start=(t == 0), stop=(t == NB - 1))
                last.then_inc(tokens_placed, 1)

                def turn_z(j, s, i):
                    pe.wait_ge(z_gathered[s], 16 * (i + 1))
                    if inside(j, 1, NT - 1):
                        pe.wait_ge(zT_ready, j)
                    for k in range(ND):
                        last = pe.transpose(ps_zT[:, k * P:(k + 1) * P], z[:, s, k * P:(k + 1) * P], ident[:])
                    last.then_inc(z_turned, 1)

                def first_layer(j, s):
                    pe.wait_ge(zT_ready, j + 1)
                    for f in range(FB):
                        half, n = divmod(f, FB // 2)
                        if n == 0:
                            pe.wait_ge(w1_ready, 2 * j + half + 1)
                            if inside(j, 1, NT - 1):
                                pe.wait_ge(h_ready, FB * j - FB // 2 * (1 - half))
                        for k in range(ND):
                            last = pe.matmul(ps_hT[:, f, :], w1_tile[:, half, k, n * P:(n + 1) * P], zT[:, s, k, :],
                                             start=(k == 0), stop=(k == ND - 1))
                        if n == FB // 2 - 1:
                            last.then_inc(h_done, 1)

                def second_layer(j, s):
                    if inside(j, 1, NT - 1):
                        pe.wait_ge(y_read, j)
                    for half in range(2):
                        pe.wait_ge(hT_ready, 2 * j + half + 1)
                        pe.wait_ge(w2_ready, 2 * j + half + 1)
                        for n, (a, b) in product(range(FB // 2), PARTS):
                            f = FB // 2 * half + n
                            last = pe.matmul(ps_y[:, 0:D], hT[:, s, a, f, :], w2_parts[:, half, b, n, :],
                                             start=(f == 0 and (a, b) == PARTS[0]), stop=(f == FB - 1 and (a, b) == PARTS[-1]))
                        last.then_inc(w2_used, 1)

                def step(j, s, i):
                    if inside(j, 0, NT - 1):
                        first_layer(j, s)
                    if inside(j, 0, NT - 2):
                        turn_z(j + 1, (s + 1) % NS, i + (s == NS - 1))
                    if inside(j, 1, NT):
                        second_layer(j - 1, (s + NS - 1) % NS)

                turn_z(0, 0, 0)
                run_tiles(pe, step, NT)

            @block.vector
            def _(dve):
                done = [0]

                def then(instruction):
                    done[0] += 1
                    instruction.then_inc(chain, 1)
                    dve.wait_ge(chain, done[0])

                def by_tile(t, n=NE):
                    return t.unsqueeze(2).to_broadcast([P, t.shape[1], n])

                def every_tile(t, n):
                    return t.unsqueeze(1).to_broadcast([P, n, t.shape[1]])

                then(dve.tensor_reduce(top[:], logits[:], AX_X, ALU.max))
                then(dve.tensor_tensor(is_top[:], logits[:], by_tile(top[:]), ALU.is_equal))
                dve.wait_ge(consts, 3)
                then(dve.tensor_tensor(first_top[:], is_top[:], every_tile(reverse[:], NB), ALU.mult))
                then(dve.tensor_reduce(choice[:], first_top[:], AX_X, ALU.max))
                dve.tensor_tensor(onehot[:], every_tile(reverse[:], NB), by_tile(choice[:]), ALU.is_equal)\
                   .then_inc(onehot_ready, 1)
                dve.wait_ge(consts, 10)
                dve.wait_ge(counted, 1)
                then(dve.tensor_reduce(totals[:], ps_count[:, 0:NB * NE].rearrange("p (t e) -> p e t", e=NE), AX_X, ALU.add))
                then(dve.tensor_tensor(fills[:], by_tile(totals[:], NB), every_tile(starts[:], NE), ALU.is_gt))
                then(dve.tensor_reduce(tiles[:], fills[:], AX_X, ALU.add))
                src, dst = tiles, tile_end
                for reach in (1, 2, 4):
                    dve.tensor_copy(dst[:, 0:reach], src[:, 0:reach]).then_inc(chain, 1)
                    done[0] += 1
                    then(dve.tensor_tensor(dst[:, reach:NE], src[:, reach:NE], src[:, 0:NE - reach], ALU.add))
                    src, dst = dst, base if dst is tile_end else tile_end
                then(dve.tensor_tensor(base[:], tile_end[:], tiles[:], ALU.subtract))
                then(dve.tensor_scalar(base[:], base[:], float(P), None, ALU.mult))
                dve.wait_ge(ranked, 1)
                then(dve.tensor_tensor(place[:], ps_rank[:, 0:NB * NE].rearrange("p (t e) -> p t e", e=NE),
                                       every_tile(base[:], NB), ALU.add))
                then(dve.tensor_tensor(place[:], place[:], onehot[:], ALU.mult))
                then(dve.tensor_reduce(slot_f[:], place[:], AX_X, ALU.add))
                then(dve.tensor_copy(slot[:], slot_f[:]))
                then(dve.tensor_scalar(slot_tile[:], slot[:], P.bit_length() - 1, None, ALU.logical_shift_right))
                then(dve.tensor_scalar(slot_row[:], slot[:], P - 1, None, ALU.bitwise_and))
                dve.tensor_copy(slot_row_f[:], slot_row[:]).then_inc(chain, 1)
                done[0] += 1
                then(dve.tensor_copy(slot_tile_f[:], slot_tile[:]))
                then(dve.tensor_tensor(at_tile[:, :, 1], every_tile(numbers16[:, 0:NT], NB), by_tile(slot_tile_f[:], NT), ALU.is_equal))
                then(dve.tensor_scalar(at_tile[:, :, 0], at_tile[:, :, 1], token_no[:], None, ALU.mult))
                dve.tensor_tensor(at_tile[:, :, 1], at_tile[:, :, 1], by_tile(numbers16[:, 0:NB], NT), ALU.mult)\
                   .then_inc(at_tile_ready, 1)
                for t in range(0, NB, IN):
                    dve.tensor_tensor(at_row[:, t:t + IN], every_tile(numbers16[:], IN), by_tile(slot_row_f[:, t:t + IN], P),
                                      ALU.is_equal).then_inc(at_row_ready, 1)
                dve.wait_ge(tokens_placed, 1)
                in_tile, tile = ps_ids[:, 0:NT], ps_ids[:, NT:2 * NT]
                dve.tensor_scalar(no_token[:], in_tile, 0.0, float(TOKENS + 1), ALU.is_equal, ALU.mult).then_inc(chain, 1)
                done[0] += 1
                then(dve.tensor_copy(slot_token[:], in_tile))
                then(dve.scalar_tensor_tensor(slot_token[:], tile, float(P), slot_token[:], ALU.mult, ALU.add))
                dve.scalar_tensor_tensor(ids[:], slot_token[:], -1.0, no_token[:], ALU.add, ALU.add).then_inc(ids_ready, 1)
                then(dve.tensor_tensor(ends_before[:], every_tile(tile_end[:], NT), by_tile(tile_no), ALU.is_le))
                then(dve.tensor_reduce(tile_expert_f[:], ends_before[:], AX_X, ALU.add))
                then(dve.tensor_scalar(tile_expert_f[:], tile_expert_f[:], float(NE - 1), None, ALU.min))
                dve.tensor_copy(tile_expert[:], tile_expert_f[:]).then_inc(tile_expert_ready, 1)

                def copy_z(j, s):
                    dve.wait_ge(z_turned, j + 1)
                    if inside(j, NS, NT - 1):
                        dve.wait_ge(h_done, 2 * (j - NS + 1))
                    dve.tensor_copy(zT[:, s], ps_zT[:, 0:D].rearrange("p (k t) -> p k t", t=P)).then_inc(zT_ready, 1)

                def copy_w1(j, c):
                    e = expert_of(dve, j)
                    loaded = dve.to_reg(e + 1)
                    dve.wait_ge(tile_expert_ready, 1)
                    dve.wait_ge(experts_loaded, loaded)
                    if inside(j, 1, NT - 1):
                        dve.wait_ge(h_done, 2 * j + c - 1)
                    dve.tensor_copy(w1_tile[:, c], w1[:, e, :, c * FE // 2:(c + 1) * FE // 2]).then_inc(w1_ready, 1)

                def low_h(j, s, half):
                    dve.wait_ge(h_high, 2 * j + half + 1)
                    f = slice(half * FB // 2, (half + 1) * FB // 2)
                    dve.tensor_tensor(hT[:, s, 1, f], h[:, f], hT[:, s, 0, f].bitcast(F32), ALU.subtract).then_inc(hT_ready, 1)

                def low_w2(j, half, e):
                    dve.wait_ge(w2_high, 2 * j + half + 1)
                    dve.tensor_tensor(w2_parts[:, half, 1], w2[:, e, half * FB // 2:(half + 1) * FB // 2, :],
                                      w2_parts[:, half, 0].bitcast(F32), ALU.subtract).then_inc(w2_ready, 1)

                def finish(j, s, i):
                    e = expert_of(dve, j)
                    dve.wait_ge(w2_used, 2 * (j + 1))
                    if inside(j, NS, NT - 1):
                        dve.wait_ge(out_stored[s], 16 * i)
                    dve.tensor_tensor(res[:, s, :], ps_y[:, 0:D], other[:, e, :], ALU.add).then_inc(y_read, 1)
                    dve.wait_ge(y_read, j + 1)
                    dve.wait_ge(x3_gathered[s], 16 * (i + 1))
                    dve.tensor_tensor(res[:, s, :], res[:, s, :], x3[:, s, :], ALU.add).then_inc(res_ready, 1)

                def step(j, s, i):
                    if inside(j, 0, NT - 2):
                        copy_w1(j + 1, 0)
                    if inside(j, 0, NT - 1):
                        low_h(j, s, 0)
                    if inside(j, 0, NT - 2):
                        copy_w1(j + 1, 1)
                        copy_z(j + 1, (s + 1) % NS)
                    if inside(j, 0, NT - 1):
                        low_h(j, s, 1)
                        e = expert_of(dve, j)
                        low_w2(j, 0, e)
                    if inside(j, 1, NT):
                        finish(j - 1, (s + NS - 1) % NS, i if s else i - 1)
                    if inside(j, 0, NT - 1):
                        low_w2(j, 1, e)

                dve.wait_ge(tile_expert_ready, 1)
                dve.wait_ge(summed, 4)
                dve.tensor_tensor(other[:], idle_sum[:].unsqueeze(1).to_broadcast([P, NE, D]), idle[:], ALU.subtract)\
                   .then_inc(other_ready, 1)
                copy_w1(0, 0)
                copy_w1(0, 1)
                copy_z(0, 0)
                run_tiles(dve, step, NT)

            @block.scalar
            def _(act):
                def rectify(j, s, half, e):
                    for f in range(half * FB // 2, (half + 1) * FB // 2):
                        if f % (FB // 2) == 0:
                            act.wait_ge(h_done, 2 * j + half + 1)
                            if inside(j, 1, NT - 1):
                                act.wait_ge(hT_ready, 2 * j + half - 1)
                        act.activation(h[:, f, :], ps_hT[:, f, :], ACT.Relu, bias=b1T[:, e, f:f + 1]).then_inc(h_ready, 1)
                    act.wait_ge(h_ready, FB * j + FB // 2 * (half + 1))
                    if inside(j, NS, NT - 1):
                        act.wait_ge(w2_used, 2 * (j - NS) + half + 1)
                    f = slice(half * FB // 2, (half + 1) * FB // 2)
                    act.activation(hT[:, s, 0, f], h[:, f], ACT.Copy).then_inc(h_high, 1)

                def round_w2(j, half, e, loaded):
                    act.wait_ge(tile_expert_ready, 1)
                    act.wait_ge(experts_loaded, loaded)
                    if inside(j, 1, NT - 1):
                        act.wait_ge(w2_used, 2 * j + half - 1)
                    act.activation(w2_parts[:, half, 0], w2[:, e, half * FB // 2:(half + 1) * FB // 2, :], ACT.Copy)\
                       .then_inc(w2_high, 1)

                def step(j, s, i):
                    e = expert_of(act, j)
                    loaded = act.to_reg(e + 1)
                    for half in range(2):
                        rectify(j, s, half, e)
                    for half in range(2):
                        round_w2(j, half, e, loaded)

                act.wait_ge(bias_loaded, 48)
                act.wait_ge(tile_expert_ready, 1)
                act.wait_ge(other_ready, 1)
                run_tiles(act, step)


def cross_attention_network(nc, eye, x, ctx, ctx_blocks, ctx_t, mask_t, w_up, w_gate, w_down, w, experts_w, out):
    x1, x2, x3, z = (nc.dram_tensor(f"{name}_scratch", [NB, P, D], F32).ap() for name in ("x1", "x2", "x3", "z"))
    idle = nc.dram_tensor("idle_scratch", [NE, D], F32).ap()
    with ExitStack() as persistent:
        address = {}

        def sb(stack, name, shape):
            tensor = stack.enter_context(nc.sbuf_tensor(name, shape, F32))
            address[name] = nc.sbuf_base - prod(shape[1:]) * 4
            return tensor

        ident = sb(persistent, "ident", [P, P])
        mv2 = sb(persistent, "mv2", [P, NB, 2])
        rstd2 = sb(persistent, "rstd2", [P, NB])
        logits = sb(persistent, "logits", [P, NB, NE])
        ident_loaded = persistent.enter_context(nc.semaphore("ident_loaded"))
        with nc.Block() as block:
            @block.sync
            def _(sp):
                sp.dma_start(ident[:], eye).then_inc(ident_loaded, 16)
                sp.wait_ge(ident_loaded, 16)

        with ExitStack() as first:
            yT = sb(first, "yT", [P, ND, NB * P])
            wq_address = address["yT"] + 12 * D * 4
            wq_raw = nc.alloc_sbuf_tensor_at("wq_raw", [P, ND, NH * KD], F32, offset=wq_address)
            ymax = sb(first, "ymax", [P, NB])
            upT = sb(first, "upT", [P, ND, FF])
            gateT = sb(first, "gateT", [P, ND, FF])
            downT = sb(first, "downT", [P, NF, D])
            used = attention0(nc, ident, [(w_up, upT), (w_gate, gateT), (w_down, downT)], yT, ymax, x, ctx, ctx_blocks, mask_t, x1)
            used = feed_forward0(nc, yT, ymax, upT, gateT, downT, x1, x2, mv2, rstd2, experts_w["b1T"],
                                 experts_w["w2"], idle, address, wq_raw, w["wq"], used)
        attention1(nc, ident, mv2, rstd2, logits, wq_raw, wq_address, w, ctx_t, x2, x3, z, used)
        experts(nc, ident, logits, idle, experts_w, z.rearrange("b p d -> (b p) d"), x3.rearrange("b p d -> (b p) d"), out)


def kernel(**inputs):
    import numpy as np
    from concourse import bacc
    from concourse.bass_utils import run_bass_kernel_spmd

    a = {name: np.asarray(value) for name, value in inputs.items()}
    x, ctx, mask = a["x"], a["ctx_1024"], a["mask_BxSxS2_ik1"]

    def attn(name):
        return a["L1_xattn_" + name]

    def expert(name):
        return a["L1_ffn_" + name]

    def by_rows(weights):
        return weights.reshape(-1, P, weights.shape[-1]).transpose(1, 0, 2)

    arrays = {
        "eye": np.eye(P, dtype=np.float32),
        "x": x,
        "ctx": ctx,
        "ctx_blocks": ctx.reshape(NB // 2, 2, P, 2, NH // 2, HD0).transpose(0, 4, 5, 3, 1, 2),
        "ctx_t": ctx.reshape(NB * P, ND, P).transpose(2, 1, 0),
        "mask_t": mask.transpose(2, 0, 1),
        "w_up": a["L0_ffn_w_up"],
        "w_gate": a["L0_ffn_w_gate"],
        "w_down": a["L0_ffn_w_down"],
        "wq": by_rows(attn("Wq")),
        "wk": by_rows(attn("Wk")),
        "wv": by_rows(attn("Wv")),
        "wo": by_rows(attn("Wo")),
        "wr": by_rows(expert("Wr")),
        "bq": attn("bq").reshape(-1, P).T,
        "bk": attn("bk").reshape(-1, P).T,
        "bv": attn("bv"),
        "bo": attn("bo"),
        "gamma": attn("ln_gamma"),
        "beta": attn("ln_beta"),
        "br": expert("br"),
        "w1": expert("W1").reshape(NE, ND, P, FE).transpose(0, 2, 1, 3),
        "w2": expert("W2").reshape(NE, FE // P, P, D).transpose(0, 2, 1, 3),
        "b1T": expert("b1").reshape(NE, FE // P, P).transpose(2, 0, 1),
        "b2": expert("b2"),
    }
    arrays = {f"{name}_in": np.ascontiguousarray(array) for name, array in arrays.items()}

    nc = bacc.Bacc("TRN2", target_bir_lowering=False, num_devices=1)
    d = {name[:-3]: nc.dram_tensor(name, array.shape, mybir.dt.from_np(array.dtype), kind="ExternalInput").ap()
         for name, array in arrays.items()}
    out = nc.dram_tensor("out", [NB * P, D], F32, kind="ExternalOutput").ap()
    attention_w = {name: d[name] for name in ("wq", "wk", "wv", "wo", "wr", "bq", "bk", "bv", "bo", "gamma", "beta", "br")}
    experts_w = {"w1": [d["w1"][e] for e in range(NE)], "w2": [d["w2"][e] for e in range(NE)], "b1T": d["b1T"], "b2": d["b2"]}
    cross_attention_network(nc, d["eye"], d["x"], d["ctx"], d["ctx_blocks"], d["ctx_t"], d["mask_t"],
                            d["w_up"], d["w_gate"], d["w_down"], attention_w, experts_w, out)
    result = run_bass_kernel_spmd(nc, [arrays], core_ids=[0])
    return result.results[0]["out"].reshape(NB, P, D)
```
